# Optimizing a Trainium2 kernel written in Bass

```python
import numpy as np
import jax
import jax.numpy as jnp

def _softmax(x, axis=-1):
    return jax.nn.softmax(x, axis=axis)

def _gelu(x):
    return jax.nn.gelu(x, approximate=True)

def _silu(x):
    return jax.nn.silu(x)

def _sigmoid(x):
    return jax.nn.sigmoid(x)

def _layernorm(x, axis=-1, eps=1e-05):
    m = jnp.mean(x, axis=axis, keepdims=True)
    v = jnp.var(x, axis=axis, keepdims=True)
    return (x - m) / jnp.sqrt(v + eps)

def _scatter_add(tgt, idx, src, axis=0):
    return tgt.at[idx].add(src)

def _segment_sum(src, seg, n):
    return jax.ops.segment_sum(src, seg, n)
kernel_name = 'mk_gnn_ffn_d1_gnn_r8_2196e6'

def setup_inputs(seed: int=0):
    np.random.seed(seed)
    _w = jnp.asarray

    def _rec_inputs():
        import jax
        import jax.numpy as jnp
        _gk = jax.random.key(seed)
        x = -0.0002117 + 1 * jax.random.normal(jax.random.fold_in(_gk, 1), (6250, 256), jnp.float32)
        src = jax.random.randint(jax.random.fold_in(_gk, 2), (100000,), 0, 6250, jnp.int32)
        dst = jnp.minimum((6250 * jax.random.uniform(jax.random.fold_in(_gk, 3), (100000,)) ** 2.0).astype(jnp.int32), 49999)
        _o = jnp.argsort(dst, stable=True)
        src = src[_o]
        dst = dst[_o]
        edge_weight = jax.random.uniform(jax.random.fold_in(_gk, 12), (100000,), jnp.float32, 0.0, 1)
        return (x, src, dst, edge_weight)
    x, src, dst, edge_weight = _rec_inputs()

    def _L0_gnn_setup():
        import jax, jax.numpy as jnp
        import numpy as np
        N = 12500
        E = 400000
        F_IN = 256
        F_OUT = 256
        key = jax.random.key(seed)
        k1, k2, k3, k4, k5, k6 = jax.random.split(key, 6)
        x = jax.random.normal(k1, (N, F_IN), dtype=jnp.float32)
        edge_val = jax.random.uniform(k2, (E,), dtype=jnp.float32)
        W = jax.random.normal(k3, (F_IN, F_OUT), dtype=jnp.float32) * (1.0 / np.sqrt(F_IN))
        b = jax.random.normal(k4, (F_OUT,), dtype=jnp.float32) * 0.01
        edge_row = jax.random.randint(k5, (E,), 0, N, dtype=jnp.int32)
        edge_col = jax.random.randint(k6, (E,), 0, N, dtype=jnp.int32)
        return {'x': x, 'edge_val': edge_val, 'W': W, 'b': b, 'edge_row': edge_row, 'edge_col': edge_col}
    _L0_gnn_all = _L0_gnn_setup()
    _L0_gnn_in = {k: v for k, v in _L0_gnn_all.items() if k in ('W', 'b')}
    del _L0_gnn_all

    def _L0_ffn_setup():
        import math
        import jax, jax.numpy as jnp
        import numpy as np
        CAPACITY_FACTOR = 1.25
        TOP_K = 2
        LN_EPS = 1e-05

        def _layer_norm(x, gamma, beta):
            mu = jnp.mean(x, axis=-1, keepdims=True)
            var = jnp.var(x, axis=-1, keepdims=True)
            return (x - mu) * jax.lax.rsqrt(var + LN_EPS) * gamma + beta
        key = jax.random.key(seed)
        ks = jax.random.split(key, 4)
        B, S, D, F, E = (8, 512, 256, 512, 8)
        x = jax.random.normal(ks[0], (B, S, D), dtype=jnp.float32)
        Wr = jax.random.normal(ks[1], (D, E), dtype=jnp.float32) / np.sqrt(D)
        br = jnp.zeros((E,), jnp.float32)
        W1 = jax.random.normal(ks[2], (E, D, F), dtype=jnp.float32) / np.sqrt(D)
        b1 = jnp.zeros((E, F), jnp.float32)
        W2 = jax.random.normal(ks[3], (E, F, D), dtype=jnp.float32) / np.sqrt(F)
        b2 = jnp.zeros((E, D), jnp.float32)
        gamma = jnp.ones((D,), jnp.float32)
        beta = jnp.zeros((D,), jnp.float32)
        return {'x': x, 'Wr': Wr, 'br': br, 'W1': W1, 'b1': b1, 'W2': W2, 'b2': b2, 'gamma': gamma, 'beta': beta}
    _L0_ffn_all = _L0_ffn_setup()
    _L0_ffn_in = {k: v for k, v in _L0_ffn_all.items() if k in ('Wr', 'br', 'W1', 'b1', 'W2', 'b2', 'gamma', 'beta')}
    del _L0_ffn_all
    return {'x': x, 'src': src, 'dst': dst, 'edge_weight': edge_weight, 'L0_gnn_W': _L0_gnn_in['W'], 'L0_gnn_b': _L0_gnn_in['b'], 'L0_ffn_Wr': _L0_ffn_in['Wr'], 'L0_ffn_br': _L0_ffn_in['br'], 'L0_ffn_W1': _L0_ffn_in['W1'], 'L0_ffn_b1': _L0_ffn_in['b1'], 'L0_ffn_W2': _L0_ffn_in['W2'], 'L0_ffn_b2': _L0_ffn_in['b2'], 'L0_ffn_gamma': _L0_ffn_in['gamma'], 'L0_ffn_beta': _L0_ffn_in['beta']}

def reference(x, src, dst, edge_weight, L0_gnn_W, L0_gnn_b, L0_ffn_Wr, L0_ffn_br, L0_ffn_W1, L0_ffn_b1, L0_ffn_W2, L0_ffn_b2, L0_ffn_gamma, L0_ffn_beta):
    import jax
    import jax.numpy as jnp

    def _L0_gnn_ref(x, edge_val, W, b, edge_row, edge_col):
        import jax, jax.numpy as jnp
        import numpy as np
        N = 12500
        E = 400000
        F_IN = 256
        F_OUT = 256
        n = x.shape[0]
        support = x @ W + b
        self_idx = jnp.arange(n, dtype=edge_row.dtype)
        rows = jnp.concatenate([edge_row, self_idx])
        cols = jnp.concatenate([edge_col, self_idx])
        vals = jnp.concatenate([edge_val, jnp.ones((n,), dtype=edge_val.dtype)])
        deg = jax.ops.segment_sum(vals, cols, num_segments=n)
        d_inv_sqrt = deg ** (-0.5)
        xs = support * d_inv_sqrt[:, None]
        msgs = xs[cols] * vals[:, None]
        agg = jax.ops.segment_sum(msgs, rows, num_segments=n)
        return agg * d_inv_sqrt[:, None]

    def _L0_ffn_ref(x, Wr, br, W1, b1, W2, b2, gamma, beta):
        import math
        import jax, jax.numpy as jnp
        import numpy as np
        CAPACITY_FACTOR = 1.25
        TOP_K = 2
        LN_EPS = 1e-05

        def _layer_norm(x, gamma, beta):
            mu = jnp.mean(x, axis=-1, keepdims=True)
            var = jnp.var(x, axis=-1, keepdims=True)
            return (x - mu) * jax.lax.rsqrt(var + LN_EPS) * gamma + beta
        B, S, D = x.shape
        E = Wr.shape[1]
        N = B * S
        K = TOP_K
        logits = jnp.mean(x, axis=1) @ Wr + br
        routing_weights = jax.nn.softmax(logits, axis=-1)
        capacity = float(math.ceil(N * CAPACITY_FACTOR / E))
        expected_loads = routing_weights.sum(axis=0) * (N / B)
        scale = jnp.where(expected_loads > capacity, capacity / expected_loads, 1.0)
        routing_weights = jax.nn.softmax(routing_weights * scale, axis=-1)
        rw_tok = jnp.broadcast_to(routing_weights[:, None, :], (B, S, E)).reshape(N, E)
        top_w, top_i = jax.lax.top_k(rw_tok, K)
        top_w = jax.nn.softmax(top_w, axis=-1)
        xf = x.reshape(N, D)
        h = jax.nn.gelu(jnp.einsum('nd,edf->enf', xf, W1) + b1[:, None, :], approximate=False)
        y = jnp.einsum('enf,efd->end', h, W2) + b2[:, None, :]
        w_dense = jnp.zeros((N, E), x.dtype).at[jnp.arange(N)[:, None], top_i].add(top_w)
        out = jnp.einsum('ne,end->nd', w_dense, y).reshape(B, S, D)
        out = _layer_norm(out + x, gamma, beta)
        return out
    x = x + _L0_gnn_ref(_layernorm(x, axis=-1), edge_weight, L0_gnn_W, L0_gnn_b, src, dst)
    x = x + _L0_ffn_ref(_layernorm(x, axis=-1)[None], L0_ffn_Wr, L0_ffn_br, L0_ffn_W1, L0_ffn_b1, L0_ffn_W2, L0_ffn_b2, L0_ffn_gamma, L0_ffn_beta)[0]
    return x

_drawn_inputs = setup_inputs


def setup_inputs(seed=0):
    import zlib

    import numpy as np

    out = dict(_drawn_inputs(seed))
    spreads = {'L0_ffn_br': (0.0, 0.8),
     'L0_ffn_b1': (0.0, 0.381),
     'L0_ffn_b2': (0.0, 0.1),
     'L0_ffn_gamma': (1.0, 0.2),
     'L0_ffn_beta': (0.0, 0.1)}
    factors = {'L0_gnn_b': 5.719, 'L0_ffn_Wr': 8.0}
    for name, (base, spread) in spreads.items():
        noise = np.random.default_rng([zlib.crc32(name.encode()), seed]).standard_normal(out[name].shape)
        drawn = base * np.exp(spread * noise) if base else spread * noise
        out[name] = jnp.asarray(drawn.astype(out[name].dtype))
    for name, factor in factors.items():
        out[name] = (out[name] * factor).astype(out[name].dtype)
    return out
```

```python
import concourse.bass as bass
from concourse import mybir
from contextlib import ExitStack



class Steps:

    def __init__(self, eng, sem):
        self.eng, self.sem, self.base, self.n = eng, sem, 0, 0

    def add(self, ins):
        ins.then_inc(self.sem, 1)
        self.n += 1
        return ins

    def wait(self):
        self.eng.wait_ge(self.sem, self.base + self.n)

    def link(self, ins):
        self.add(ins)
        self.wait()

    def at(self, base):
        self.base, self.n = base, 0


def wait_from(eng, sem, value):
    if isinstance(value, int) and value <= 0:
        return
    eng.wait_ge(sem, value)


def gnn_ffn_kernel(nc, x_d, src_d, dst_d, ew_d, W_d, b_d, Wr_d, br_d, W1_d, b1_d, W2_d, b2_d, gamma_d, beta_d, out_d):
    fp32 = mybir.dt.float32
    bf16 = mybir.dt.bfloat16
    fp32r = mybir.dt.float32r
    i32 = mybir.dt.int32
    ALU = mybir.AluOpType
    ACT = mybir.ActivationFunctionType
    AX = mybir.AxisListType.X

    P = 128
    N, D = x_d.shape
    E = src_d.shape[0]
    NX, _, F = W1_d.shape
    TOP = 2
    EPS = 1e-5
    DC, FC = D // P, F // P
    NT = -(-N // P)
    NFULL = N // P
    TAIL = N - NFULL * P
    G = 8
    Q = -(-E // (G * P))
    QFULL = E // (G * P)
    EREST = E - QFULL * G * P
    EPAD = G * P - EREST
    K = 4
    NB = Q * G // K
    DUMMY = NT * P
    ROWS = DUMMY + P
    PADSRC = DUMMY - 1
    CAP = float(-(-N * 125 // (100 * NX)))
    S4 = 4
    XCH = 7
    CT = NT // XCH

    table_d = nc.dram_tensor("table_d", [N, D], fp32, kind="Internal").ap()
    sums_d = [nc.dram_tensor(f"sums{k}_d", [ROWS, D], fp32, kind="Internal").ap() for k in range(K)]
    starts_d = nc.dram_tensor("starts_d", [Q, G], i32, kind="Internal").ap()

    with ExitStack() as ctx:
        def sb(name, shape, dt=fp32):
            return ctx.enter_context(nc.sbuf_tensor(name, shape, dt))

        def sem(name):
            return ctx.enter_context(nc.semaphore(name))

        x = sb("x", [P, NT, D])
        hT = sb("hT", [P, DC, NT * P])
        edge = sb("edge", [P, 4, G, Q])
        src_hi = sb("src_hi", [P, G * P], bf16)
        src_lo = sb("src_lo", [P, G * P], bf16)
        ident = sb("ident", [P, P])
        identb = sb("identb", [P, P], bf16)
        ones = sb("ones", [P, P])
        iota = sb("iota", [P, P])
        before = sb("before", [P, P])
        dummyc = sb("dummyc", [P, 1])
        W = sb("W", [P, DC, D])
        b_row = sb("b_row", [1, D])
        gamma = sb("gamma", [P, D])
        beta = sb("beta", [P, D])
        b2c = sb("b2c", [P, D])
        Wr = sb("Wr", [P, DC, NX])
        dis = sb("dis", [P, NT])
        stats = sb("stats", [P, 8, 6])
        mv = sb("mv", [P, 8, 2])
        var = sb("var", [P, 8, 1])
        rstd = sb("rstd", [P, 8, 1])
        shiftm = sb("shiftm", [P, 8, 1])
        rowstat = sb("rowstat", [P, NT, 2])
        half_power = sb("half_power", [P, NT])
        same_before = sb("same_before", [P, 2, K])
        shift = sb("shift", [P, 2, K])
        rows_to = sb("rows_to", [P, S4, K], i32)
        rows_of = sb("rows_of", [P, S4, K], i32)
        nat8 = sb("nat8", [P, 4, G])
        starts_i = sb("starts_i", [P, G], i32)
        far = sb("far", [P, 2])
        flag_i = sb("flag_i", [P, 1], i32)
        colsum = sb("colsum", [P, DC, NT + 1])
        mean_col = sb("mean_col", [P, DC])
        rt = sb("rt", [1, 24, NX])
        rs = sb("rs", [1, 16])
        pick_i = sb("pick_i", [1, TOP], i32)
        wtop = sb("wtop", [P, TOP])
        b1s = sb("b1s", [P, TOP, FC])

        with ExitStack() as early:
            arena = early.enter_context(nc.sbuf_tensor("arena", [P, 8192], fp32))
            h = early.enter_context(nc.sbuf_tensor("h", [P, NT, D], fp32))
        W1h = sb("W1h", [P, TOP, DC, F], fp32r)
        W1l = sb("W1l", [P, TOP, DC, F], fp32r)
        W2h = sb("W2h", [P, TOP * FC, D], fp32r)
        W2l = sb("W2l", [P, TOP * FC, D], fp32r)
        hid = sb("hid", [P, 4, K * P])
        hidh = sb("hidh", [P, TOP * FC, K * P], fp32r)
        hidl = sb("hidl", [P, TOP * FC, K * P], fp32r)
        hTh = sb("hTh", [P, DC, K * P], fp32r)
        hTl = sb("hTl", [P, DC, K * P], fp32r)

        def part(t, at, shape, dt=fp32):
            n = 1
            for s in shape:
                n *= s
            if dt == bf16:
                n = (n + 1) // 2
            v = t[:, at:at + n]
            if dt != fp32:
                v = v.bitcast(dt)
            if len(shape) == 2:
                v = v.rearrange("p (a b) -> p a b", b=shape[1])
            if len(shape) == 3:
                v = v.rearrange("p (a b c) -> p a b c", b=shape[1], c=shape[2])
            return v

        scratch = hT[:, :, :].rearrange("p c n -> p (c n)")
        GP = G * P
        src_i = part(arena, 0, [GP], i32)
        dst_i = part(arena, GP, [GP], i32)
        w_n = part(arena, 2 * GP, [GP])
        src_n = part(arena, 3 * GP, [GP])
        dst_n = part(arena, 4 * GP, [GP])
        place_n = part(arena, 5 * GP, [GP])
        tmp_i = part(arena, 6 * GP, [GP], i32)
        tmp_n = part(arena, 7 * GP, [GP])
        dstT = part(scratch, 0, [G, Q])
        dst_hi = part(scratch, GP, [Q, G], bf16)
        dst_lo = part(scratch, GP + GP // 2, [Q, G], bf16)
        w3 = part(scratch, 2 * GP, [3, Q, G], bf16)
        rest = part(scratch, 4 * GP, [G, Q])
        tmpT_i = part(scratch, 5 * GP, [G, Q], i32)
        tmpT2_i = part(scratch, 6 * GP, [G, Q], i32)
        ln = part(scratch, 8 * GP, [D])
        lnT = part(scratch, 8 * GP + D, [DC, P])
        ZCH = 10
        zeros = part(scratch, 9 * GP, [ROWS * D // P // ZCH])
        starts = part(scratch, 9 * GP + ROWS * D // P // ZCH, [Q * G], i32)
        iota8 = part(arena, 0, [P, G], bf16)
        oh_lo = [part(arena, GP // 2 * (1 + n), [P, G], bf16) for n in range(2)]
        oh_hi = [part(arena, 2 * GP + 256 * n, [NT, G], bf16) for n in range(2)]
        oh_w = [part(arena, 3 * GP + 640 * n, [3, NT, G], bf16) for n in range(2)]
        window = part(arena, 0, [S4 * K, D])
        sums = part(arena, S4 * K * D, [S4 * K, D])
        same = part(scratch, 5 * GP, [2, K, P])
        placed = part(scratch, 6 * GP, [2, K, P])
        mixT = part(scratch, 7 * GP, [2, K, P])
        junk = part(scratch, 8 * GP, [2 * K, P])
        SL = 3
        back = part(arena, 0, [SL * K, 2 * D])
        hs = part(arena, SL * K * 2 * D, [4, D])
        flat = edge[:, :, :, :].rearrange("p a g q -> p (a g q)")
        z = part(flat, 0, [K, D])
        zg = part(flat, K * D, [K, D])
        y = part(flat, 2 * K * D, [K, D])
        b2s = part(flat, 2 * K * D, [TOP, D])
        W1raw = hid[:, :, :]
        W2raw = part(flat, 0, [TOP * FC, D])

        srcT, placeT, wT, shiftT = (edge[:, n, :, :] for n in range(4))
        as_tiles = lambda v: v.rearrange("p (g j) -> p g j", j=P)

        bank = [ctx.enter_context(nc.psum_tensor(f"bank{n}", [P, 512], fp32)) for n in range(8)]

        s_pad = sem("s_pad")
        s_src, s_dst, s_ew = sem("s_src"), sem("s_dst"), sem("s_ew")
        s_x, s_W, s_wr, s_gb = sem("s_x"), sem("s_W"), sem("s_wr"), sem("s_gb")
        s_const = sem("s_const")
        s_zero = sem("s_zero")
        s_cleared = sem("s_cleared")
        s_dve = sem("s_dve")
        s_var, s_root = sem("s_var"), sem("s_root")
        s_dis = sem("s_dis")
        s_nat = sem("s_nat")
        s_starts, s_starts_d, s_starts_r = sem("s_starts"), sem("s_starts_d"), sem("s_starts_r")
        s_far, s_farall, s_flag = sem("s_far"), sem("s_farall"), sem("s_flag")
        s_turn = sem("s_turn")
        s_turned = sem("s_turned")
        s_split = sem("s_split")
        s_ln, s_lnt, s_lnT = sem("s_ln"), sem("s_lnt"), sem("s_lnT")
        s_sup, s_supout = sem("s_sup"), sem("s_supout")
        s_nb = sem("s_nb")
        s_hi, s_oh, s_ohp, s_deg = sem("s_hi"), sem("s_oh"), sem("s_ohp"), sem("s_deg")
        s_degall = sem("s_degall")
        s_scaled, s_table = sem("s_scaled"), sem("s_table")
        s_row = sem("s_row")
        s_same = sem("s_same")
        s_placed = sem("s_placed")
        s_dup, s_sh, s_to = sem("s_dup"), sem("s_sh"), sem("s_to")
        s_of = sem("s_of")
        s_mix, s_mixT = sem("s_mix"), sem("s_mixT")
        s_window = [sem(f"s_window{n}") for n in range(S4)]
        s_msg = sem("s_msg")
        s_sums = sem("s_sums")
        s_go = sem("s_go")
        s_tick = sem("s_tick")
        s_scat = [sem(f"s_scat{n}") for n in range(K)]
        s_back = [sem(f"s_back{n}") for n in range(SL)]
        s_pair = sem("s_pair")
        s_used = sem("s_used")
        s_h, s_ht, s_hT = sem("s_h"), sem("s_ht"), sem("s_hT")
        s_mcol, s_logit, s_e, s_pick, s_wt, s_wb, s_lg = (
            sem(n) for n in ("s_mcol", "s_logit", "s_e", "s_pick", "s_wt", "s_wb", "s_lg"))
        s_w1, s_w2, s_b12, s_b2c, s_wtop = sem("s_w1"), sem("s_w2"), sem("s_b12"), sem("s_b2c"), sem("s_wtop")
        s_W1h, s_W1l, s_W2h, s_W2l = sem("s_W1h"), sem("s_W1l"), sem("s_W2h"), sem("s_W2l")
        s_part = sem("s_part")
        s_ff1, s_gelu, s_hidh, s_hidl, s_ff2 = (sem(n) for n in ("s_ff1", "s_gelu", "s_hidh", "s_hidl", "s_ff2"))
        s_res, s_hb = sem("s_res"), sem("s_hb")
        s_z, s_zn, s_zg, s_zx, s_y = sem("s_z"), sem("s_zn"), sem("s_zg"), sem("s_zx"), sem("s_y")
        s_out = sem("s_out")
        s_cons = 9

        block = ctx.enter_context(nc.Block())

        x_v = x_d[0:NFULL * P, :].rearrange("(t p) d -> p t d", p=P)
        table_v = table_d[0:NFULL * P, :].rearrange("(t p) d -> p t d", p=P)

        @block.sync
        def _(sp):
            sp.wait_ge(s_pad, 2)
            for d, v, s in ((src_d, src_i, s_src), (dst_d, dst_i, s_dst), (ew_d, w_n, s_ew)):
                sp.dma_start(v[0:QFULL, :], d[0:QFULL * GP].rearrange("(q c) -> q c", c=GP)).then_inc(s, 16)
                sp.dma_start(v[QFULL:Q, 0:EREST], d[QFULL * GP:E].rearrange("(q c) -> q c", q=1)).then_inc(s, 16)
            sp.dma_start(dst_i[QFULL:Q, EREST:GP], dst_d[E - EPAD:E].rearrange("(q c) -> q c", q=1)).then_inc(s_dst, 16)
            sp.wait_ge(s_zero, 1)
            for k in range(K):
                v = sums_d[k].rearrange("(p r) d -> p (r d)", p=P)
                n = ROWS * D // P // ZCH
                for c in range(ZCH):
                    sp.dma_start(v[:, c * n:(c + 1) * n], zeros).then_inc(s_cleared, 16)
            sp.wait_ge(s_starts, 1)
            sp.dma_start(starts_d, starts_i[0:Q, :]).then_inc(s_starts_d, 16)
            sp.wait_ge(s_starts_d, 16)
            sp.dma_start(starts[0:1, :], starts_d.rearrange("(o q) g -> o (q g)", o=1)).then_inc(s_starts_r, 16)
            for c in range(XCH):
                sp.wait_ge(s_scaled, c + 1)
                last = min((c + 1) * CT, NFULL)
                sp.dma_start(table_v[:, c * CT:last, :], h[:, c * CT:last, :]).then_inc(s_table, 16)
            sp.dma_start(table_d[NFULL * P:N, :], h[0:TAIL, NFULL, :]).then_inc(s_table, 16)
            sp.wait_ge(s_table, 16 * (XCH + 1))
            sp.wait_ge(s_starts_r, 16)
            sp.wait_ge(s_flag, 1)
            sp.wait_ge(s_degall, 1)

            def windows(i):
                for n in range(S4):
                    wait_from(sp, s_msg, S4 * (i - 1) + n + 1)
                    for j in range(K):
                        at = sp.value_load(starts[0:1, bass.ds((i * S4 + n) * K + j, 1)], min_val=0, max_val=N - P)
                        sp.dma_start(window[:, n * K + j, :], table_d[bass.ds(at, P), :]).then_inc(s_window[n], 16)

            gathers = sp.value_load(flag_i[0:1, 0:1], min_val=0, max_val=1)
            with sp.If(gathers < 1):
                windows(0)
                with sp.Fori(1, NB // S4) as i:
                    windows(i)

            for k in range(K):
                sp.wait_ge(s_scat[k], 16 * NB)

            def read_back(p, slot, n=2):
                for k in range(K):
                    v = sums_d[k][bass.ds(p * (2 * P), n * P), :] if not isinstance(p, int) else sums_d[k][p * 2 * P:(p * 2 + n) * P, :]
                    sp.dma_start(back[:, slot * K + k, 0:n * D].rearrange("p (j d) -> p j d", d=D),
                                 v.rearrange("(j p) d -> p j d", p=P)).then_inc(s_back[slot], 16)

            for slot in range(SL):
                read_back(slot, slot)
            with sp.Fori(1, NFULL // 2 // SL) as i:
                for slot in range(SL):
                    sp.wait_ge(s_used, SL * (i - 1) + slot + 1)
                    read_back(SL * i + slot, slot)
            sp.wait_ge(s_used, NFULL // 2 - SL + 1)
            read_back(NFULL // 2, 0, 1)

            sp.wait_ge(s_pick, 1)
            for e in range(TOP):
                pick = sp.value_load(pick_i[0:1, e:e + 1], min_val=0, max_val=NX - 1)
                sp.dma_start(W1raw[:, e * DC:(e + 1) * DC, :], W1_d[bass.ds(pick, 1), :, :].rearrange("o (c p) f -> p (o c) f", p=P)).then_inc(s_w1, 16)
                sp.dma_start(W2raw[:, e * FC:(e + 1) * FC, :], W2_d[bass.ds(pick, 1), :, :].rearrange("o (c p) n -> p (o c) n", p=P)).then_inc(s_w2, 16)
                with nc.allow_non_contiguous_dma(reason="a column of 512 biases"):
                    sp.dma_start(b1s[:, e, :], b1_d[bass.ds(pick, 1), :].rearrange("o (c p) -> p (o c)", p=P)).then_inc(s_b12, 16)
                sp.dma_start(b2s[:, e, :], b2_d[bass.ds(pick, 1), :].broadcast_to([P, D])).then_inc(s_b12, 16)

            with sp.Fori(0, NFULL // K) as i:
                sp.wait_ge(s_y, K * i + K)
                sp.dma_start(out_d[bass.ds(i * (K * P), K * P), :].rearrange("(t p) d -> p t d", p=P), y).then_inc(s_out, 16)
            sp.wait_ge(s_y, NT)
            sp.dma_start(out_d[NFULL * P:N, :], y[0:TAIL, 0, :]).then_inc(s_out, 16)
            sp.wait_ge(s_out, 16 * (NFULL // K + 1))

        @block.gpsimd
        def _(pool):
            nc.gpsimd.memset(src_i, PADSRC).then_inc(s_pad, 1)
            nc.gpsimd.memset(w_n, 0.0).then_inc(s_pad, 1)
            nc.gpsimd.memset(x[:, NFULL, :], 0.0).then_inc(s_const, 1)
            nc.gpsimd.iota(iota[:, :], [[1, P]], base=0, channel_multiplier=0,
                           allow_small_or_imprecise_dtypes=True).then_inc(s_const, 1)
            nc.gpsimd.memset(colsum[:, :, NT:NT + 1], 0.0)
            nc.gpsimd.iota(dummyc[:, :], [[0, 1]], base=DUMMY, channel_multiplier=1,
                           allow_small_or_imprecise_dtypes=True).then_inc(s_const, 1)
            nc.gpsimd.memset(ones[:, :], 1.0).then_inc(s_const, 1)
            nc.gpsimd.memset(half_power[:, :], -0.5).then_inc(s_const, 1)
            nc.gpsimd.memset(ident[:, :], 0.0).then_inc(s_const, 1)
            pool.wait_ge(s_const, 6)
            nc.gpsimd.affine_select(out=ident[:, :], in_=ident[:, :], compare_op=ALU.not_equal, fill=1.0, base=0,
                                    pattern=[[-1, P]], channel_multiplier=1).then_inc(s_const, 1)
            nc.gpsimd.affine_select(out=before[:, :], in_=ones[:, :], compare_op=ALU.is_gt, fill=0.0, base=0,
                                    pattern=[[-1, P]], channel_multiplier=1).then_inc(s_const, 1)
            pool.wait_ge(s_const, 8)
            nc.gpsimd.tensor_copy(identb[:, :], ident[:, :]).then_inc(s_const, 1)
            nc.gpsimd.memset(zeros, 0.0).then_inc(s_zero, 1)
            pool.wait_ge(s_turn, 8)
            pool.wait_ge(s_split, 1)
            nc.gpsimd.iota(iota8, [[1, P], [0, G]], base=0, channel_multiplier=0,
                           allow_small_or_imprecise_dtypes=True).then_inc(s_zero, 1)

            def root(n, m=1):
                nc.gpsimd.tensor_tensor(rstd[:, n:n + m, :], var[:, n:n + m, :],
                                        half_power[:, 0:m].unsqueeze(2), ALU.pow).then_inc(s_root, 1)

            def weigh(c, half):
                pool.wait_ge(s_hi, c + 1)
                wait_from(pool, s_deg, c - 1)
                q = bass.ds(c, 1) if not isinstance(c, int) else slice(c, c + 1)
                nc.gpsimd.tensor_tensor(oh_w[half][:, 2, :, :], oh_hi[half], w3[:, 2, q, :].broadcast_to([P, NT, G]),
                                        ALU.mult).then_inc(s_ohp, 1)

            def pool_rows(i):
                pool.wait_ge(s_var, i + 1)
                wait_from(pool, s_ln, i)
                root(0)
                for half in range(2):
                    weigh(2 * i + half, half)

            pool_rows(0)
            with pool.Fori(1, NT) as i:
                pool_rows(i)
            pool.wait_ge(s_dis, 1)
            nc.gpsimd.tensor_tensor(dis[:, :], dis[:, :], half_power[:, :], ALU.pow).then_inc(s_dis, 1)

            pool.wait_ge(s_cleared, 16 * ZCH * K)
            pool.wait_ge(s_flag, 1)

            def scatter(b, n):
                pool.wait_ge(s_sums, b + 1)
                pool.wait_ge(s_to, b + 1)
                for j in range(K):
                    wait_from(pool, s_scat[j], 16 * b)
                    if not isinstance(b, int):
                        pool.sem_inc(s_go, 1)
                    pool.indirect_dma_start(
                        out=sums_d[j], out_offset=bass.IndirectOffsetOnAxis(ap=rows_to[:, n, j:j + 1], axis=0),
                        in_=sums[:, n * K + j, :], in_offset=None, compute_op=ALU.add).then_inc(s_scat[j], 16)

            def gather(b, n):
                pool.wait_ge(s_of, b + 1)
                wait_from(pool, s_msg, b - S4 + 1)
                if not isinstance(b, int):
                    pool.sem_inc(s_go, 1)
                for j in range(K):
                    pool.indirect_dma_start(
                        out=window[:, n * K + j, :], out_offset=None, in_=table_d,
                        in_offset=bass.IndirectOffsetOnAxis(ap=rows_of[:, n, j:j + 1], axis=0)).then_inc(s_window[n], 16)

            gathers = pool.value_load(flag_i[0:1, 0:1], min_val=0, max_val=1)
            with pool.If(gathers < 1):
                for n in range(S4):
                    scatter(n, n)
                with pool.Fori(1, NB // S4) as i:
                    for n in range(S4):
                        scatter(S4 * i + n, n)
            with pool.Else():
                pool.wait_ge(s_table, 16 * (XCH + 1))
                for n in range(S4):
                    gather(n, n)
                    scatter(n, n)
                with pool.Fori(1, NB // S4) as i:
                    for n in range(S4):
                        gather(S4 * i + n, n)
                        scatter(S4 * i + n, n)

            NP = NFULL // 2

            def pair(slot, turn, n=2):
                pool.wait_ge(s_back[slot], 16 * K * turn)
                a = back[:, slot * K:slot * K + 2, 0:n * D]
                nc.gpsimd.tensor_tensor(a, a, back[:, slot * K + 2:slot * K + 4, 0:n * D], ALU.add).then_inc(s_pair, 1)

            def root_rows(p, s, n=2):
                pool.wait_ge(s_var, NT + p + 1)
                wait_from(pool, s_h, p - 1)
                root(2 * s, n)

            pair(0, 1)
            for slot in range(1, SL):
                pair(slot, 1)
                root_rows(slot - 1, (slot - 1) % 2)
            pair(0, 2)
            root_rows(SL - 1, (SL - 1) % 2)
            for slot in range(1, SL):
                pair(slot, 2)
                root_rows(SL + slot - 1, (SL + slot - 1) % 2)
            with pool.Fori(1, NP // SL // 2) as i:
                for m in range(2 * SL):
                    pair(m % SL, 2 * i + m // SL + 1)
                    root_rows(2 * SL * i + m - 1, (m - 1) % 2)
            pair(0, NP // SL + 1, 1)
            root_rows(NP - 1, (NP - 1) % 2)
            root_rows(NP, NP % 2, 1)

            pool.wait_ge(s_b2c, 1)
            pool.wait_ge(s_gb, 32)

            def residual(t, j):
                pool.wait_ge(s_res, t + 1)
                nc.gpsimd.tensor_tensor(z[:, j, :], z[:, j, :], b2c[:, :], ALU.add).then_inc(s_hb, 1)

            def scaled(t, j, i):
                tt = slice(t, t + 1) if isinstance(t, int) else bass.ds(t, 1)
                pool.wait_ge(s_var, NT + NP + 1 + t + 1)
                root(4 + j)
                pool.wait_ge(s_zn, t + 1)
                nc.gpsimd.tensor_tensor(zg[:, j, :], z[:, j, :], gamma[:, :], ALU.mult).then_inc(s_zg, 1)
                pool.wait_ge(s_zg, t + 1)
                pool.sem_inc(s_go, 1)
                nc.gpsimd.tensor_tensor(zg[:, j:j + 1, :], zg[:, j:j + 1, :], x[:, tt, :], ALU.add).then_inc(s_zx, 1)
                pool.wait_ge(s_zx, t + 1)
                wait_from(pool, s_out, 16 * i)
                nc.gpsimd.tensor_tensor(y[:, j, :], zg[:, j, :], beta[:, :], ALU.add).then_inc(s_y, 1)

            def four(i):
                for j in range(K):
                    residual(K * i + j, j)
                for j in range(K):
                    scaled(K * i + j, j, i)

            four(0)
            with pool.Fori(1, NFULL // K) as i:
                four(i)
            residual(NFULL, 0)
            scaled(NFULL, 0, NFULL // K)

        @block.scalar
        def _(act):
            for c in range(XCH):
                last = min((c + 1) * CT, NFULL)
                act.dma_start(x[:, c * CT:last, :], x_v[:, c * CT:last, :]).then_inc(s_x, 16)
            act.wait_ge(s_const, 1)
            act.dma_start(x[0:TAIL, NFULL, :], x_d[NFULL * P:N, :]).then_inc(s_x, 16)
            act.dma_start(W[:, :, :], W_d.rearrange("(c p) n -> p c n", p=P)).then_inc(s_W, 16)
            act.dma_start(b_row[0:1, :], b_d.rearrange("(o n) -> o n", o=1)).then_inc(s_W, 16)
            act.dma_start(Wr[:, :, :], Wr_d.rearrange("(c p) n -> p c n", p=P)).then_inc(s_wr, 16)
            act.dma_start(rt[0:1, 0, :], br_d.rearrange("(o n) -> o n", o=1)).then_inc(s_wr, 16)
            act.dma_start(gamma[:, :], gamma_d.rearrange("(o n) -> o n", o=1).broadcast_to([P, D])).then_inc(s_gb, 16)
            act.dma_start(beta[:, :], beta_d.rearrange("(o n) -> o n", o=1).broadcast_to([P, D])).then_inc(s_gb, 16)

            for n, to in enumerate((dstT, wT, srcT, placeT)):
                for half in range(2):
                    act.wait_ge(s_turn, 2 * n + half + 1)
                    nc.scalar.copy(to[:, half * K:(half + 1) * K, :],
                                   bank[2 * (n % 2) + half][:, 0:K * Q].rearrange("p (g q) -> p g q", q=Q)).then_inc(s_turned, 1)

            def act_rows(i):
                ii = slice(i, i + 1) if isinstance(i, int) else bass.ds(i, 1)
                act.wait_ge(s_nb, i + 1)
                wait_from(act, s_lnt, i)
                nc.scalar.activation(ln.unsqueeze(1), x[:, ii, :], ACT.Identity, bias=shiftm[:, 0, :], scale=rstd[:, 0, :]).then_inc(s_ln, 1)
                act.wait_ge(s_lnt, i + 1)
                nc.scalar.copy(lnT, bank[1][:, 0:D].rearrange("p (c n) -> p c n", n=P)).then_inc(s_lnT, 1)
                act.wait_ge(s_sup, i + 1)
                nc.scalar.copy(h[:, ii, :], bank[2][:, None, 0:D]).then_inc(s_supout, 1)

            act_rows(0)
            with act.Fori(1, NT) as i:
                act_rows(i)

            def mix_out(i, n):
                b, q, half, m = S4 * i + n, 2 * i + n // 2, n % 2, n % 2
                ks = slice(half * K, (half + 1) * K)
                qq = slice(q, q + 1) if isinstance(q, int) else bass.ds(q, 1)
                wait_from(act, s_window[n], 16 * K * i)
                nc.scalar.copy(rows_of[:, n, :].unsqueeze(2), dstT[:, ks, qq]).then_inc(s_of, 1)
                act.wait_ge(s_mix, b + 1)
                wait_from(act, s_msg, b - 1)
                nc.scalar.copy(mixT[:, m, :, :], bank[2 + m][:, :].rearrange("p (k n) -> p k n", n=P)).then_inc(s_mixT, 1)

            def sums_out(b, n):
                act.wait_ge(s_msg, b + 1)
                for k in range(K):
                    wait_from(act, s_scat[k], 16 * (b - S4 + 1))
                for c in range(2):
                    last = nc.scalar.copy(sums[:, n * K + 2 * c:n * K + 2 * c + 2, :],
                                          bank[4 + 2 * (n % 2) + c][:, :].rearrange("p (k n) -> p k n", n=D))
                last.then_inc(s_sums, 1)

            def act_blocks(i):
                for n in range(S4):
                    mix_out(i, n)
                    if not isinstance(i, int) or S4 * i + n >= 1:
                        sums_out(S4 * i + n - 1, (n - 1) % S4)

            act.wait_ge(s_degall, 1)
            act.wait_ge(s_table, 16 * (XCH + 1))
            act.wait_ge(s_cleared, 16 * ZCH * K)
            act_blocks(0)
            act_blocks(1)
            with act.Fori(2, NB // S4) as i:
                act_blocks(i)
            sums_out(NB - 1, S4 - 1)

            for k in range(K):
                act.wait_ge(s_scat[k], 16 * NB)

            def row_norm(p, s, n=2):
                for m in range(n):
                    t = 2 * p + m
                    tt = slice(t, t + 1) if isinstance(t, int) else bass.ds(t, 1)
                    if m == 0:
                        act.wait_ge(s_nb, NT + p + 1)
                        wait_from(act, s_ht, 2 * p - 2)
                    last = nc.scalar.activation(hs[:, 2 * s + m:2 * s + m + 1, :], x[:, tt, :], ACT.Identity,
                                                bias=shiftm[:, 2 * s + m, :], scale=rstd[:, 2 * s + m, :])
                last.then_inc(s_h, 1)

            def row_out(t, s, n=P):
                at = t * P
                act.wait_ge(s_ht, t + 1)
                for c in range(DC):
                    last = nc.scalar.activation(hT[:, c, at:at + n] if isinstance(t, int) else hT[:, c, bass.ds(at, n)],
                                                bank[s][:, c * P:c * P + n], ACT.Copy,
                                                accum_out=colsum[:, c, t:t + 1] if isinstance(t, int) else colsum[:, c, bass.ds(t, 1)])
                if n < P:
                    for c in range(DC):
                        last = nc.scalar.copy(hT[:, c, at + n:at + P], bank[s][:, c * P + n:(c + 1) * P])
                last.then_inc(s_hT, 1)

            def row_pairs(p, s):
                row_norm(p, s)
                if not isinstance(p, int) or p >= 1:
                    for m in range(2):
                        row_out(2 * (p - 1) + m, 2 * (1 - s) + m)

            NP = NFULL // 2
            for p in range(2):
                row_pairs(p, p % 2)
            with act.Fori(1, NP // 2) as i:
                for s in range(2):
                    row_pairs(2 * i + s, s)
            row_norm(NP, 0, 1)
            for m in range(2):
                row_out(NFULL - 2 + m, 2 + m)
            row_out(NFULL, 0, TAIL)

            for n in range(3):
                act.wait_ge(s_lg, n + 1)
                w = NX if n < 2 else TOP
                nc.scalar.activation(rt[0:1, 20 + n, 0:w], rt[0:1, 16 + n, 0:w], ACT.Exp).then_inc(s_e, 1)

            for e in range(TOP):
                if e == 0:
                    act.wait_ge(s_w1, 32)
                for c in range(DC):
                    nc.scalar.copy(W1h[:, e, c, :], W1raw[:, e * DC + c, :]).then_inc(s_W1h, 1)
            act.wait_ge(s_w2, 32)
            act.wait_ge(s_wtop, 1)
            for e in range(TOP):
                nc.scalar.activation(W2h[:, e * FC:(e + 1) * FC, :], W2raw[:, e * FC:(e + 1) * FC, :], ACT.Copy,
                                     scale=wtop[:, e:e + 1]).then_inc(s_W2h, 1)

            act.wait_ge(s_b12, 64)
            act.wait_ge(s_W1l, TOP)

            def gelu(i, n):
                for k in range(TOP * FC):
                    c = TOP * FC * i + k
                    act.wait_ge(s_ff1, c + 1)
                    wait_from(act, s_hidl, c - 3)
                    nc.scalar.activation(hid[:, k % 4, 0:n], bank[k % 4][:, 0:n], ACT.Gelu,
                                         bias=b1s[:, k // FC, k % FC:k % FC + 1]).then_inc(s_gelu, 1)
                    act.wait_ge(s_gelu, c + 1)
                    if k == 0:
                        wait_from(act, s_ff2, K * i)
                    nc.scalar.copy(hidh[:, k, 0:n], hid[:, k % 4, 0:n]).then_inc(s_hidh, 1)

            gelu(0, K * P)
            with act.Fori(1, NFULL // K) as i:
                gelu(i, K * P)
            gelu(NFULL // K, P)

        @block.vector
        def _(dve):
            me = Steps(dve, s_dve)

            dve.wait_ge(s_dst, 48)
            nc.vector.tensor_copy(dst_n[0:Q, :], dst_i[0:Q, :]).then_inc(s_nat, 1)
            dve.wait_ge(s_src, 32)
            nc.vector.tensor_copy(src_n[0:Q, :], src_i[0:Q, :]).then_inc(s_nat, 1)
            dve.wait_ge(s_nat, 2)
            least, most, start, toofar = (nat8[0:Q, n, :] for n in range(4))
            nc.vector.tensor_reduce(least, as_tiles(dst_n[0:Q, :]), AX, ALU.min)
            me.link(nc.vector.tensor_reduce(most, as_tiles(dst_n[0:Q, :]), AX, ALU.max))
            me.link(nc.vector.tensor_scalar(start, least, float(N - P), None, ALU.min))
            nc.vector.tensor_copy(starts_i[0:Q, :], start).then_inc(s_starts, 1)
            me.link(nc.vector.tensor_tensor(toofar, most, start, ALU.subtract))
            me.link(nc.vector.tensor_scalar(toofar, toofar, P - 0.5, None, ALU.is_gt))
            nc.vector.tensor_reduce(far[0:Q, 0:1], toofar, AX, ALU.add).then_inc(s_far, 1)
            me.link(nc.vector.tensor_tensor(as_tiles(place_n[0:Q, :]), as_tiles(dst_n[0:Q, :]),
                                            start.unsqueeze(2).broadcast_to([Q, G, P]), ALU.subtract))
            dve.wait_ge(s_farall, 1)
            me.link(nc.vector.tensor_scalar(far[:, 1:2], bank[7][:, 0:1], 0.5, None, ALU.is_gt))
            nc.vector.tensor_copy(flag_i[:, :], far[:, 1:2]).then_inc(s_flag, 1)
            dve.wait_ge(s_const, s_cons)
            me.link(nc.vector.tensor_tensor(as_tiles(tmp_n[0:Q, :]), iota[0:Q, None, :].broadcast_to([Q, G, P]),
                                            as_tiles(place_n[0:Q, :]), ALU.subtract))
            nc.vector.scalar_tensor_tensor(out=place_n[0:Q, :], in0=tmp_n[0:Q, :], scalar=far[0:Q, 1:2],
                                           in1=place_n[0:Q, :], op0=ALU.mult, op1=ALU.add).then_inc(s_nat, 1)
            me.link(nc.vector.tensor_scalar(tmp_i[0:Q, :], src_i[0:Q, :], 7, 7, ALU.arith_shift_right, ALU.arith_shift_left))
            me.link(nc.vector.tensor_copy(src_hi[0:Q, :], tmp_i[0:Q, :]))
            me.link(nc.vector.tensor_scalar(tmp_i[0:Q, :], src_i[0:Q, :], 127, None, ALU.bitwise_and))
            nc.vector.tensor_copy(src_lo[0:Q, :], tmp_i[0:Q, :]).then_inc(s_split, 1)
            by_g = lambda v: v.rearrange("p q g -> p g q")
            dve.wait_ge(s_turned, 2)
            me.link(nc.vector.tensor_copy(tmpT_i, dstT))
            me.link(nc.vector.tensor_scalar(tmpT2_i, tmpT_i, 7, None, ALU.arith_shift_right))
            me.link(nc.vector.tensor_copy(by_g(dst_hi), tmpT2_i))
            me.link(nc.vector.tensor_scalar(tmpT2_i, tmpT_i, 127, None, ALU.bitwise_and))
            me.link(nc.vector.tensor_copy(by_g(dst_lo), tmpT2_i))
            dve.wait_ge(s_turned, 4)
            me.link(nc.vector.tensor_copy(by_g(w3[:, 0, :, :]), wT))
            me.link(nc.vector.tensor_tensor(rest, wT, by_g(w3[:, 0, :, :]), ALU.subtract))
            me.link(nc.vector.tensor_copy(by_g(w3[:, 1, :, :]), rest))
            me.link(nc.vector.tensor_tensor(by_g(w3[:, 2, :, :]), rest, by_g(w3[:, 1, :, :]), ALU.subtract))
            dve.wait_ge(s_turned, 6)
            me.link(nc.vector.tensor_scalar(shiftT, srcT, -1.0, dummyc[:, 0:1], ALU.mult, ALU.add))
            dve.wait_ge(s_x, 16 * (XCH + 1))

            def statistics(of, n):
                dve.sem_inc(s_tick, 1)
                me.link(nc.vector.bn_stats(stats[:, n, :], of))
                dve.sem_inc(s_tick, 1)
                me.link(nc.vector.bn_aggr(mv[:, n, :], stats[:, n, :]))
                nc.vector.tensor_scalar(var[:, n, :], mv[:, n, 1:2], EPS, None, ALU.add).then_inc(s_var, 1)

            def normalize(to, of, n):
                return nc.vector.tensor_scalar(to, of, mv[:, n, 0:1], rstd[:, n, :], ALU.subtract, ALU.mult)

            def minus_mean(n, m=1):
                nc.vector.scalar_tensor_tensor(out=shiftm[:, n:n + m, :], in0=mv[:, n:n + m, 0:1], scalar=-1.0,
                                               in1=rstd[:, n:n + m, :], op0=ALU.mult, op1=ALU.mult).then_inc(s_nb, 1)

            def degrees(c, half):
                q = slice(c, c + 1) if isinstance(c, int) else bass.ds(c, 1)
                wait_from(dve, s_deg, c - 1)
                wait_from(dve, s_ohp, c - 1)
                nc.vector.tensor_tensor(oh_hi[half], iota8[:, 0:NT, :], dst_hi[:, q, :].broadcast_to([P, NT, G]),
                                        ALU.is_equal).then_inc(s_hi, 1)
                nc.vector.tensor_tensor(oh_lo[half], iota8, dst_lo[:, q, :].broadcast_to([P, P, G]), ALU.is_equal)
                dve.wait_ge(s_hi, c + 1)
                for n in range(2):
                    last = nc.vector.tensor_tensor(oh_w[half][:, n, :, :], oh_hi[half],
                                                   w3[:, n, q, :].broadcast_to([P, NT, G]), ALU.mult)
                last.then_inc(s_oh, 1)

            def layernorm_x(i):
                row = x[:, 0, :] if isinstance(i, int) else x[:, bass.ds(i, 1), :].rearrange("p o d -> p (o d)")
                statistics(row, 0)
                degrees(2 * i, 0)
                dve.wait_ge(s_root, i + 1)
                wait_from(dve, s_ln, i)
                minus_mean(0)
                degrees(2 * i + 1, 1)

            dve.wait_ge(s_zero, 2)
            done = me.base + me.n
            me.at(done)
            layernorm_x(0)
            per = me.n
            with dve.Fori(1, NT) as i:
                me.at(done + i * per)
                layernorm_x(i)
                assert me.n == per
            me.at(done + NT * per)

            dve.wait_ge(s_degall, 1)
            me.link(nc.vector.tensor_scalar(dis[:, :], bank[0][:, 0:NT], 1.0, None, ALU.add))
            me.link(nc.vector.tensor_tensor(dis[:, :], dis[:, :], bank[0][:, NT:2 * NT], ALU.add))
            nc.vector.tensor_tensor(dis[:, :], dis[:, :], bank[0][:, 2 * NT:3 * NT], ALU.add).then_inc(s_dis, 1)
            dve.wait_ge(s_dis, 2)
            dve.wait_ge(s_supout, NT)
            for c in range(XCH):
                v = h[:, c * CT:(c + 1) * CT, :]
                nc.vector.tensor_tensor(v, v, dis[:, c * CT:(c + 1) * CT].unsqueeze(2).broadcast_to([P, CT, D]),
                                        ALU.mult).then_inc(s_scaled, 1)

            def messages(i, n):
                b, q, half, m = S4 * i + n, 2 * i + n // 2, n % 2, n % 2
                qq = slice(q, q + 1) if isinstance(q, int) else bass.ds(q, 1)
                ks = slice(half * K, (half + 1) * K)
                wait_from(dve, s_mix, b - 1)
                dve.wait_ge(s_row, b + 1)
                nc.vector.tensor_tensor(same[:, m, :, :], bank[m][:, :].rearrange("p (k n) -> p k n", n=P),
                                        srcT[:, ks, qq].broadcast_to([P, K, P]), ALU.is_equal).then_inc(s_same, 1)
                for j in range(K):
                    last = nc.vector.tensor_scalar(placed[:, m, j, :], iota[:, :], placeT[:, half * K + j, qq],
                                                   wT[:, half * K + j, qq], ALU.is_equal, ALU.mult)
                last.then_inc(s_placed, 1)
                dve.wait_ge(s_same, b + 1)
                for j in range(K):
                    last = nc.vector.tensor_tensor_reduce(out=junk[:, m * K + j, :], in0=same[:, m, j, :], in1=before[:, :],
                                                          scale=1.0, scalar=0.0, op0=ALU.mult, op1=ALU.add,
                                                          accum_out=same_before[:, m, j:j + 1])
                last.then_inc(s_dup, 1)
                dve.wait_ge(s_dup, b + 1)
                nc.vector.scalar_tensor_tensor(out=shift[:, m, :].unsqueeze(2), in0=same_before[:, m, :].unsqueeze(2),
                                               scalar=0.5, in1=shiftT[:, ks, qq], op0=ALU.is_gt, op1=ALU.mult).then_inc(s_sh, 1)
                dve.wait_ge(s_sh, b + 1)
                for k in range(K):
                    wait_from(dve, s_scat[k], 16 * (b - S4 + 1))
                nc.vector.tensor_tensor(rows_to[:, n, :].unsqueeze(2), shift[:, m, :].unsqueeze(2),
                                        srcT[:, ks, qq], ALU.add).then_inc(s_to, 1)

            dve.wait_ge(s_turned, 8)
            dve.wait_ge(s_cleared, 16 * ZCH * K)
            for n in range(S4):
                messages(0, n)
            with dve.Fori(1, NB // S4) as i:
                for n in range(S4):
                    messages(i, n)

            done = me.base + me.n
            NP = NFULL // 2

            def new_rows(p, slot, s, n=2):
                tt = bass.ds(2 * p, n) if not isinstance(p, int) else slice(2 * p, 2 * p + n)
                a, c = (back[:, slot * K + k, 0:n * D] for k in range(2))
                dve.wait_ge(s_pair, p + 1)
                me.link(nc.vector.tensor_tensor(a, a, c, ALU.add))
                a2 = a.rearrange("p (j d) -> p j d", d=D)
                me.link(nc.vector.tensor_tensor(a2, a2, h[:, tt, :], ALU.add))
                one = []
                for m in range(n):
                    t = 2 * p + m
                    t1 = bass.ds(t, 1) if not isinstance(t, int) else slice(t, t + 1)
                    xt = x[:, t1, :].rearrange("p o d -> p (o d)")
                    one.append(xt)
                    last = nc.vector.scalar_tensor_tensor(out=xt, in0=a2[:, m, :], scalar=dis[:, t1], in1=xt, op0=ALU.mult, op1=ALU.add)
                last.then_inc(s_used, 1)
                dve.wait_ge(s_used, p + 1)
                dve.sem_inc(s_tick, 1)
                for m, xt in enumerate(one):
                    last = nc.vector.bn_stats(stats[:, 2 * s + m, :], xt)
                me.link(last)
                dve.sem_inc(s_tick, 1)
                for m in range(n):
                    last = nc.vector.bn_aggr(mv[:, 2 * s + m, :], stats[:, 2 * s + m, :])
                me.link(last)
                nc.vector.tensor_scalar(var[:, 2 * s:2 * s + n, :], mv[:, 2 * s:2 * s + n, 1:2], EPS, None, ALU.add).then_inc(s_var, 1)

            def new_stats(p, s, n=2):
                tt = bass.ds(2 * p, n) if not isinstance(p, int) else slice(2 * p, 2 * p + n)
                dve.wait_ge(s_root, NT + p + 1)
                wait_from(dve, s_h, p - 1)
                minus_mean(2 * s, n)
                nc.vector.tensor_copy(rowstat[:, tt, 0:1], rstd[:, 2 * s:2 * s + n, :])
                dve.wait_ge(s_nb, NT + p + 1)
                me.add(nc.vector.tensor_copy(rowstat[:, tt, 1:2], shiftm[:, 2 * s:2 * s + n, :]))

            dve.wait_ge(s_to, NB)
            dve.wait_ge(s_mix, NB)
            me.at(done)
            new_rows(0, 0, 0)
            first = me.n
            new_stats_n = 1
            for p in range(1, 2 * SL):
                new_rows(p, p % SL, p % 2)
                new_stats(p - 1, (p - 1) % 2)
            one = first + new_stats_n
            with dve.Fori(1, NP // SL // 2) as i:
                for m in range(2 * SL):
                    p = 2 * SL * i + m
                    me.at(done + p * one - new_stats_n)
                    new_rows(p, m % SL, m % 2)
                    new_stats(p - 1, (m - 1) % 2)
                    assert me.n == one
            me.at(done + NP * one - new_stats_n)
            new_rows(NP, 0, NP % 2, 1)
            new_stats(NP - 1, (NP - 1) % 2)
            new_stats(NP, NP % 2, 1)

            R = lambda n: rt[0:1, n, :]
            S = lambda n: rs[0:1, n:n + 1]
            dve.wait_ge(s_hT, NT)
            me.link(nc.vector.tensor_reduce(mean_col[:, :], colsum[:, :, 0:NT], AX, ALU.add))
            nc.vector.tensor_scalar(mean_col[:, :], mean_col[:, :], 1.0 / N, None, ALU.mult).then_inc(s_mcol, 1)
            dve.wait_ge(s_logit, 1)
            dve.wait_ge(s_wr, 32)
            me.link(nc.vector.tensor_tensor(R(1), bank[5][0:1, 0:NX], R(0), ALU.add))

            def softmax(of, n, w, to):
                me.link(nc.vector.tensor_reduce(S(0), of, AX, ALU.max))
                nc.vector.tensor_scalar(rt[0:1, 16 + n, 0:w], of, S(0), None, ALU.subtract).then_inc(s_lg, 1)
                dve.wait_ge(s_e, n + 1)
                me.link(nc.vector.tensor_reduce(S(1), rt[0:1, 20 + n, 0:w], AX, ALU.add))
                me.link(nc.vector.reciprocal(S(2), S(1)))
                me.link(nc.vector.tensor_scalar(to, rt[0:1, 20 + n, 0:w], S(2), None, ALU.mult))

            softmax(R(1), 0, NX, R(2))
            me.link(nc.vector.tensor_scalar(R(3), R(2), float(N), None, ALU.mult))
            me.link(nc.vector.reciprocal(R(4), R(3)))
            me.link(nc.vector.tensor_scalar(R(4), R(4), CAP, None, ALU.mult))
            me.link(nc.vector.tensor_scalar(R(5), R(3), CAP, None, ALU.is_gt))
            me.link(nc.vector.tensor_scalar(R(6), R(3), CAP, None, ALU.is_le))
            me.link(nc.vector.tensor_tensor(R(4), R(4), R(5), ALU.mult))
            me.link(nc.vector.tensor_tensor(R(4), R(4), R(6), ALU.add))
            me.link(nc.vector.tensor_tensor(R(7), R(2), R(4), ALU.mult))
            softmax(R(7), 1, NX, R(8))
            for e in range(TOP):
                me.link(nc.vector.tensor_reduce(rs[0:1, 4 + e:5 + e], R(8), AX, ALU.max))
                me.link(nc.vector.tensor_scalar(R(9), R(8), S(4 + e), float(NX), ALU.is_lt, ALU.mult))
                me.link(nc.vector.tensor_tensor(R(9), R(9), iota[0:1, 0:NX], ALU.add))
                me.link(nc.vector.tensor_reduce(rs[0:1, 6 + e:7 + e], R(9), AX, ALU.min))
                me.link(nc.vector.tensor_scalar(R(10), iota[0:1, 0:NX], S(6 + e), -2.0, ALU.is_equal, ALU.mult))
                me.link(nc.vector.tensor_tensor(R(8), R(8), R(10), ALU.add))
            nc.vector.tensor_copy(pick_i[0:1, :], rs[0:1, 6:6 + TOP]).then_inc(s_pick, 1)
            softmax(rs[0:1, 4:4 + TOP], 2, TOP, rs[0:1, 8:8 + TOP])
            dve.wait_ge(s_dve, me.base + me.n)
            nc.vector.tensor_copy(rs[0:1, 10:10 + TOP], rs[0:1, 8:8 + TOP]).then_inc(s_wt, 1)

            dve.wait_ge(s_W1h, TOP * DC)
            for e in range(TOP):
                nc.vector.tensor_tensor(W1l[:, e, :, :], W1raw[:, e * DC:(e + 1) * DC, :], W1h[:, e, :, :].bitcast(fp32),
                                        ALU.subtract).then_inc(s_W1l, 1)
            dve.wait_ge(s_wb, 1)
            nc.vector.tensor_copy(wtop[:, :], bank[4][:, 0:TOP]).then_inc(s_wtop, 1)

            def split_rows(i, n):
                cols = slice(i * K * P, i * K * P + n) if isinstance(i, int) else bass.ds(i * (K * P), n)
                wait_from(dve, s_ff1, TOP * FC * i)
                nc.vector.tensor_copy(hTh[:, :, 0:n], hT[:, :, cols]).then_inc(s_part, 1)
                dve.wait_ge(s_part, 2 * i + 1)
                nc.vector.tensor_tensor(hTl[:, :, 0:n], hT[:, :, cols], hTh[:, :, 0:n].bitcast(fp32), ALU.subtract).then_inc(s_part, 1)

            split_rows(0, K * P)
            dve.wait_ge(s_wtop, 1)
            dve.wait_ge(s_b12, 64)
            me.link(nc.vector.tensor_scalar(b2c[:, :], b2s[:, 0, :], wtop[:, 0:1], None, ALU.mult))
            nc.vector.scalar_tensor_tensor(out=b2c[:, :], in0=b2s[:, 1, :], scalar=wtop[:, 1:2], in1=b2c[:, :],
                                           op0=ALU.mult, op1=ALU.add).then_inc(s_b2c, 1)
            dve.wait_ge(s_W2h, TOP)
            for e in range(TOP):
                v = slice(e * FC, (e + 1) * FC)
                nc.vector.scalar_tensor_tensor(out=W2l[:, v, :], in0=W2raw[:, v, :], scalar=wtop[:, e:e + 1],
                                               in1=W2h[:, v, :].bitcast(fp32), op0=ALU.mult, op1=ALU.subtract).then_inc(s_W2l, 1)
            dve.wait_ge(s_W2l, TOP)

            def residual(t, j):
                t1 = bass.ds(t, 1) if not isinstance(t, int) else slice(t, t + 1)
                wait_from(dve, s_zg, t - K + 1)
                nc.vector.tensor_scalar(z[:, j:j + 1, :], x[:, t1, :], rowstat[:, t1, 0:1].rearrange("p o d -> p (o d)"),
                                        rowstat[:, t1, 1:2].rearrange("p o d -> p (o d)"), ALU.mult, ALU.add).then_inc(s_res, 1)

            def low_part(i, n):
                for k in range(TOP * FC):
                    dve.wait_ge(s_hidh, TOP * FC * i + k + 1)
                    if k == 0:
                        wait_from(dve, s_ff2, K * i)
                    nc.vector.tensor_tensor(hidl[:, k, 0:n], hid[:, k % 4, 0:n], hidh[:, k, 0:n].bitcast(fp32),
                                            ALU.subtract).then_inc(s_hidl, 1)

            def last_rows(t, j):
                dve.wait_ge(s_ff2, t + 1)
                dve.wait_ge(s_hb, t + 1)
                nc.vector.tensor_tensor(z[:, j, :], bank[4 + j][:, 0:D], z[:, j, :], ALU.add).then_inc(s_z, 1)
                dve.wait_ge(s_z, t + 1)
                statistics(z[:, j, :], 4 + j)

            def last_normal(t, j):
                dve.wait_ge(s_root, NT + NP + 1 + t + 1)
                normalize(z[:, j, :], z[:, j, :], 4 + j).then_inc(s_zn, 1)

            done = me.base + me.n
            GR = NFULL // K

            def group(i, n, tiles, after):
                for j in range(tiles):
                    residual(K * i + j, j)
                low_part(i, n)
                if after:
                    split_rows(i + 1, after)
                for j in range(tiles):
                    me.at(done + (K * i + j) * 2)
                    last_rows(K * i + j, j)
                    assert me.n == 2
                    if j:
                        last_normal(K * i + j - 1, j - 1)
                last_normal(K * i + tiles - 1, tiles - 1)

            group(0, K * P, K, K * P)
            with dve.Fori(1, GR - 1) as i:
                group(i, K * P, K, K * P)
            group(GR - 1, K * P, K, P)
            group(GR, P, 1, 0)

        @block.tensor
        def _(pe):
            mm = nc.tensor.matmul
            pe.wait_ge(s_const, s_cons)
            for n, of in enumerate((dst_n, w_n, src_n, place_n)):
                if n == 0:
                    pe.wait_ge(s_nat, 1)
                if n == 1:
                    pe.wait_ge(s_ew, 32)
                if n == 2:
                    pe.wait_ge(s_nat, 2)
                if n == 3:
                    pe.wait_ge(s_far, 1)
                    mm(bank[7][:, 0:1], ones[0:Q, :], far[0:Q, 0:1], start=True, stop=True).then_inc(s_farall, 1)
                    pe.wait_ge(s_nat, 3)
                for half in range(2):
                    to = bank[2 * (n % 2) + half]
                    if n >= 2:
                        pe.wait_ge(s_turned, 2 * (n - 2) + half + 1)
                    for j in range(K):
                        last = nc.tensor.transpose(to[:, j * Q:(j + 1) * Q], of[0:Q, (half * K + j) * P:(half * K + j + 1) * P],
                                                   ident[0:Q, 0:Q])
                    last.then_inc(s_turn, 1)

            pe.wait_ge(s_turned, 8)
            pe.wait_ge(s_zero, 1)
            pe.wait_ge(s_W, 32)
            mm(bank[0][:, 0:3 * NT], zeros[:, 0:P], zeros[:, 0:3 * NT], start=True, stop=False, skip_group_check=True)

            def one_hots(c, half):
                pe.wait_ge(s_oh, c + 1)
                pe.wait_ge(s_ohp, c + 1)
                for g in range(G):
                    last = mm(bank[0][:, 0:3 * NT], oh_lo[half][:, :, g], oh_w[half][:, :, :, g], start=False,
                              stop=False, skip_group_check=True)
                last.then_inc(s_deg, 1)

            with pe.Fori(0, NT) as i:
                pe.wait_ge(s_ln, i + 1)
                for c in range(DC):
                    last = nc.tensor.transpose(bank[1][:, c * P:(c + 1) * P], ln[:, c * P:(c + 1) * P], ident[:, :])
                last.then_inc(s_lnt, 1)
                one_hots(2 * i, 0)
                pe.wait_ge(s_lnT, i + 1)
                mm(bank[2][:, 0:D], ones[0:1, :], b_row[0:1, :], start=True, stop=False)
                for c in range(DC):
                    last = mm(bank[2][:, 0:D], lnT[:, c, :], W[:, c, :], start=False, stop=(c == DC - 1))
                last.then_inc(s_sup, 1)
                one_hots(2 * i + 1, 1)
            mm(bank[0][:, 0:3 * NT], zeros[:, 0:P], zeros[:, 0:3 * NT], start=False, stop=True,
               skip_group_check=True).then_inc(s_degall, 1)

            def src_rows(i, half):
                to = bank[half][:, :]
                pick = identb[0:Q, bass.ds(i, 1)] if not isinstance(i, int) else identb[0:Q, i:i + 1]
                pick = pick.broadcast_to([Q, P])
                mm(to, pick, src_hi[0:Q, half * K * P:(half + 1) * K * P], start=True, stop=False)
                mm(to, pick, src_lo[0:Q, half * K * P:(half + 1) * K * P], start=False, stop=True).then_inc(s_row, 1)

            def mix(b, half):
                pe.wait_ge(s_same, b + 1)
                pe.wait_ge(s_placed, b + 1)
                wait_from(pe, s_mixT, b - 1)
                for j in range(K):
                    last = mm(bank[2 + half][:, j * P:(j + 1) * P], placed[:, half, j, :], same[:, half, j, :],
                              start=True, stop=True)
                last.then_inc(s_mix, 1)

            def msgs(b, n, turn):
                pe.wait_ge(s_mixT, b + 1)
                pe.wait_ge(s_window[n], 16 * K * turn)
                wait_from(pe, s_sums, b - 1)
                for j in range(K):
                    c = j % 2
                    last = mm(bank[4 + 2 * (n % 2) + j // 2][:, c * D:(c + 1) * D], mixT[:, n % 2, j, :],
                              window[:, n * K + j, :], start=True, stop=True)
                last.then_inc(s_msg, 1)

            pe.wait_ge(s_split, 1)
            pe.wait_ge(s_scaled, 1)
            pe.wait_ge(s_supout, NT)
            def pe_blocks(i):
                for n in range(S4):
                    b, q = S4 * i + n, 2 * i + n // 2
                    wait_from(pe, s_same, b - 1)
                    src_rows(q, n % 2)
                    if not isinstance(i, int) or b >= 1:
                        mix(b - 1, (n - 1) % 2)
                    if not isinstance(i, int) or b >= 2:
                        msgs(b - 2, (n - 2) % S4, i + n // 2)

            pe_blocks(0)
            with pe.Fori(1, NB // S4) as i:
                pe_blocks(i)
            mix(NB - 1, 1)
            msgs(NB - 2, S4 - 2, NB // S4)
            msgs(NB - 1, S4 - 1, NB // S4)

            pe.wait_ge(s_sums, NB)
            NP = NFULL // 2

            def turn_rows(p, s, n=2):
                pe.wait_ge(s_h, p + 1)
                for m in range(n):
                    t = 2 * p + m
                    wait_from(pe, s_hT, t - 3)
                    for c in range(DC):
                        last = nc.tensor.transpose(bank[2 * s + m][:, c * P:(c + 1) * P], hs[:, 2 * s + m, c * P:(c + 1) * P], ident[:, :])
                    last.then_inc(s_ht, 1)

            for p in range(2):
                turn_rows(p, p)
            with pe.Fori(1, NP // 2) as i:
                for s in range(2):
                    turn_rows(2 * i + s, s)
            turn_rows(NP, 0, 1)

            pe.wait_ge(s_mcol, 1)
            pe.wait_ge(s_wr, 32)
            for c in range(DC):
                last = mm(bank[5][0:1, 0:NX], mean_col[:, c:c + 1], Wr[:, c, :], start=(c == 0), stop=(c == DC - 1))
            last.then_inc(s_logit, 1)
            pe.wait_ge(s_wt, 1)
            mm(bank[4][:, 0:TOP], ones[0:1, :], rs[0:1, 10:10 + TOP], start=True, stop=True).then_inc(s_wb, 1)

            def ffn(i, n, tiles):
                pe.wait_ge(s_part, 2 * i + 2)
                for k in range(TOP * FC):
                    e, f = k // FC, k % FC
                    wait_from(pe, s_gelu, TOP * FC * i + k - 3)
                    step = 0
                    for c in range(DC):
                        for w, v in ((W1h, hTh), (W1h, hTl), (W1l, hTh)):
                            last = mm(bank[k % 4][:, 0:n], w[:, e, c, f * P:(f + 1) * P], v[:, c, 0:n],
                                      start=(step == 0), stop=(step == 3 * DC - 1))
                            step += 1
                    last.then_inc(s_ff1, 1)
                for k in range(TOP * FC):
                    pe.wait_ge(s_hidl, TOP * FC * i + k + 1)
                    for j in range(tiles):
                        if k == 0:
                            wait_from(pe, s_z, K * (i - 1) + j + 1)
                        js = slice(j * P, (j + 1) * P)
                        for step, (v, w) in enumerate(((hidh, W2h), (hidh, W2l), (hidl, W2h))):
                            last = mm(bank[4 + j][:, 0:D], v[:, k, js], w[:, k, :], start=(k == 0 and step == 0),
                                      stop=(k == TOP * FC - 1 and step == 2))
                        if k == TOP * FC - 1:
                            last.then_inc(s_ff2, 1)

            pe.wait_ge(s_W1l, TOP)
            pe.wait_ge(s_W2l, TOP)
            ffn(0, K * P, K)
            with pe.Fori(1, NFULL // K) as i:
                ffn(i, K * P, K)
            ffn(NFULL // K, P, 1)


_INS = ['x', 'src', 'dst', 'edge_weight', 'L0_gnn_W', 'L0_gnn_b', 'L0_ffn_Wr', 'L0_ffn_br', 'L0_ffn_W1', 'L0_ffn_b1',
        'L0_ffn_W2', 'L0_ffn_b2', 'L0_ffn_gamma', 'L0_ffn_beta']
_OUTS = [((6250, 256), 'float32')]


def kernel(**inputs):
    import numpy as _np
    import concourse.bacc as _bacc
    from concourse import mybir as _mybir
    from concourse.bass_utils import run_bass_kernel_spmd as _run

    nc = _bacc.Bacc("TRN2", target_bir_lowering=False, num_devices=1)
    arrays, args = {}, []
    for name in _INS:
        a = _np.ascontiguousarray(inputs[name])
        arrays[f"in_{name}_dram"] = a
        args.append(nc.dram_tensor(f"in_{name}_dram", a.shape, _mybir.dt.from_np(a.dtype), kind="ExternalInput").ap())
    for i, (shape, dtype) in enumerate(_OUTS):
        dt = _mybir.dt.from_np(_np.dtype(dtype))
        args.append(nc.dram_tensor(f"out_{i}_dram", shape, dt, kind="ExternalOutput").ap())
    gnn_ffn_kernel(nc, *args)
    r = _run(nc, [arrays], core_ids=[0])
    return r.results[0]["out_0_dram"]
```

```python
import concourse.bass as bass
from concourse import mybir
from contextlib import ExitStack



class Steps:

    def __init__(self, eng, sem):
        self.eng, self.sem, self.base, self.n = eng, sem, 0, 0

    def add(self, ins):
        ins.then_inc(self.sem, 1)
        self.n += 1
        return ins

    def wait(self, n=None):
        self.eng.wait_ge(self.sem, self.base + (self.n if n is None else n))

    def link(self, ins):
        self.add(ins)
        self.wait()

    def at(self, base):
        self.base, self.n = base, 0


def wait_from(eng, sem, value):
    if isinstance(value, int) and value <= 0:
        return
    eng.wait_ge(sem, value)


def gnn_ffn_kernel(nc, x_d, src_d, dst_d, ew_d, W_d, b_d, Wr_d, br_d, W1_d, b1_d, W2_d, b2_d, gamma_d, beta_d, out_d):
    fp32 = mybir.dt.float32
    bf16 = mybir.dt.bfloat16
    fp32r = mybir.dt.float32r
    i32 = mybir.dt.int32
    ALU = mybir.AluOpType
    ACT = mybir.ActivationFunctionType
    AX = mybir.AxisListType.X

    P = 128
    N, D = x_d.shape
    E = src_d.shape[0]
    NX, _, F = W1_d.shape
    TOP = 2
    EPS = 1e-5
    DC, FC = D // P, F // P
    NT = -(-N // P)
    NFULL = N // P
    TAIL = N - NFULL * P
    G = 8
    Q = -(-E // (G * P))
    QFULL = E // (G * P)
    EREST = E - QFULL * G * P
    EPAD = G * P - EREST
    K = 4
    NB = Q * G // K
    DUMMY = NT * P
    ROWS = DUMMY + P
    PADSRC = DUMMY - 1
    CAP = float(-(-N * 125 // (100 * NX)))
    S4 = 4
    XCH = 7
    CT = NT // XCH

    table_d = nc.dram_tensor("table_d", [N, D], fp32, kind="Internal").ap()
    sums_d = [nc.dram_tensor(f"sums{k}_d", [ROWS, D], fp32, kind="Internal").ap() for k in range(K)]
    starts_d = nc.dram_tensor("starts_d", [Q, G], i32, kind="Internal").ap()

    with ExitStack() as ctx:
        def sb(name, shape, dt=fp32):
            return ctx.enter_context(nc.sbuf_tensor(name, shape, dt))

        def sem(name):
            return ctx.enter_context(nc.semaphore(name))

        x = sb("x", [P, NT, D])
        hT = sb("hT", [P, DC, NT * P])
        edge = sb("edge", [P, 4, G, Q])
        src_hi = sb("src_hi", [P, G * P], bf16)
        src_lo = sb("src_lo", [P, G * P], bf16)
        ident = sb("ident", [P, P])
        identb = sb("identb", [P, P], bf16)
        ones = sb("ones", [P, P])
        iota = sb("iota", [P, P])
        before = sb("before", [P, P])
        dummyc = sb("dummyc", [P, 1])
        W = sb("W", [P, DC, D])
        b_row = sb("b_row", [1, D])
        gamma = sb("gamma", [P, D])
        beta = sb("beta", [P, D])
        b2c = sb("b2c", [P, D])
        Wr = sb("Wr", [P, DC, NX])
        dis = sb("dis", [P, NT])
        stats = sb("stats", [P, 8, 6])
        mv = sb("mv", [P, 8, 2])
        var = sb("var", [P, 8, 1])
        rstd = sb("rstd", [P, 8, 1])
        shiftm = sb("shiftm", [P, 8, 1])
        rowstat = sb("rowstat", [P, NT, 2])
        half_power = sb("half_power", [P, NT])
        same_before = sb("same_before", [P, 2, K])
        shift = sb("shift", [P, 2, K])
        rows_to = sb("rows_to", [P, S4, K], i32)
        rows_of = sb("rows_of", [P, S4, K], i32)
        nat8 = sb("nat8", [P, 4, G])
        starts_i = sb("starts_i", [P, G], i32)
        far = sb("far", [P, 2])
        flag_i = sb("flag_i", [P, 1], i32)
        colsum = sb("colsum", [P, DC, NT + 1])
        mean_col = sb("mean_col", [P, DC])
        rt = sb("rt", [1, 24, NX])
        rs = sb("rs", [1, 16])
        pick_i = sb("pick_i", [1, TOP], i32)
        wtop = sb("wtop", [P, TOP])
        b1s = sb("b1s", [P, TOP, FC])

        with ExitStack() as early:
            arena = early.enter_context(nc.sbuf_tensor("arena", [P, 8192], fp32))
            h = early.enter_context(nc.sbuf_tensor("h", [P, NT, D], fp32))
        W1h = sb("W1h", [P, TOP, DC, F], fp32r)
        W1l = sb("W1l", [P, TOP, DC, F], fp32r)
        W2h = sb("W2h", [P, TOP * FC, D], fp32r)
        W2l = sb("W2l", [P, TOP * FC, D], fp32r)
        hid = sb("hid", [P, 4, K * P])
        hidh = sb("hidh", [P, TOP * FC, K * P], fp32r)
        hidl = sb("hidl", [P, TOP * FC, K * P], fp32r)
        hTh = sb("hTh", [P, DC, K * P], fp32r)
        hTl = sb("hTl", [P, DC, K * P], fp32r)

        def part(t, at, shape, dt=fp32):
            n = 1
            for s in shape:
                n *= s
            if dt == bf16:
                n = (n + 1) // 2
            v = t[:, at:at + n]
            if dt != fp32:
                v = v.bitcast(dt)
            if len(shape) == 2:
                v = v.rearrange("p (a b) -> p a b", b=shape[1])
            if len(shape) == 3:
                v = v.rearrange("p (a b c) -> p a b c", b=shape[1], c=shape[2])
            return v

        scratch = hT[:, :, :].rearrange("p c n -> p (c n)")
        GP = G * P
        src_i = part(arena, 0, [GP], i32)
        dst_i = part(arena, GP, [GP], i32)
        w_n = part(arena, 2 * GP, [GP])
        src_n = part(arena, 3 * GP, [GP])
        dst_n = part(arena, 4 * GP, [GP])
        place_n = part(arena, 5 * GP, [GP])
        tmp_i = part(arena, 6 * GP, [GP], i32)
        tmp_n = part(arena, 7 * GP, [GP])
        dstT = part(scratch, 0, [G, Q])
        G2 = 2 * G
        assert Q == 2 * NT
        dst_hi = part(scratch, GP, [NT, G2], bf16)
        dst_lo = part(scratch, GP + GP // 2, [NT, G2], bf16)
        w3 = part(scratch, 2 * GP, [3, NT, G2], bf16)
        rest = part(scratch, 4 * GP, [G, Q])
        tmpT_i = part(scratch, 5 * GP, [G, Q], i32)
        tmpT2_i = part(scratch, 6 * GP, [G, Q], i32)
        ln = part(scratch, 8 * GP, [D])
        lnT = part(scratch, 8 * GP + D, [DC, P])
        ZCH = 10
        zeros = part(scratch, 9 * GP, [ROWS * D // P // ZCH])
        starts = part(scratch, 9 * GP + ROWS * D // P // ZCH, [Q * G], i32)
        iota16 = part(arena, 0, [P, G2], bf16)
        oh_lo = [part(arena, GP * (1 + n), [P, G2], bf16) for n in range(2)]
        oh_hi = [part(arena, 3 * GP + 512 * n, [NT, G2], bf16) for n in range(2)]
        oh_w = [part(arena, 4 * GP + 1280 * n, [3, NT, G2], bf16) for n in range(2)]
        window = part(arena, 0, [S4 * K, D])
        sums = part(arena, S4 * K * D, [S4 * K, D])
        same = part(scratch, 5 * GP, [2, K, P])
        placed = part(scratch, 6 * GP, [2, K, P])
        mixT = part(scratch, 7 * GP, [2, K, P])
        junk = part(scratch, 8 * GP, [2 * K, P])
        SL = 4
        back = part(arena, 0, [SL * K, 2 * D])
        flat = edge[:, :, :, :].rearrange("p a g q -> p (a g q)")
        hs = part(flat, 0, [4, D])
        z = part(flat, 0, [K, D])
        zg = part(flat, K * D, [K, D])
        y = part(flat, 2 * K * D, [K, D])
        b2s = part(flat, 2 * K * D, [TOP, D])
        W1raw = hid[:, :, :]
        W2raw = part(flat, 0, [TOP * FC, D])

        srcT, placeT, wT, shiftT = (edge[:, n, :, :] for n in range(4))
        as_tiles = lambda v: v.rearrange("p (g j) -> p g j", j=P)

        bank = [ctx.enter_context(nc.psum_tensor(f"bank{n}", [P, 512], fp32)) for n in range(8)]

        s_pad = sem("s_pad")
        s_src, s_dst, s_ew = sem("s_src"), sem("s_dst"), sem("s_ew")
        s_x, s_W, s_wr, s_gb = sem("s_x"), sem("s_W"), sem("s_wr"), sem("s_gb")
        s_const = sem("s_const")
        s_zero = sem("s_zero")
        s_cleared = sem("s_cleared")
        s_dve = sem("s_dve")
        s_var, s_root = sem("s_var"), sem("s_root")
        s_dis = sem("s_dis")
        s_nat = sem("s_nat")
        s_starts, s_starts_d, s_starts_r = sem("s_starts"), sem("s_starts_d"), sem("s_starts_r")
        s_far, s_farall, s_flag = sem("s_far"), sem("s_farall"), sem("s_flag")
        s_turn = sem("s_turn")
        s_turned = sem("s_turned")
        s_split = sem("s_split")
        s_ln, s_lnt, s_lnT = sem("s_ln"), sem("s_lnt"), sem("s_lnT")
        s_sup, s_supout = sem("s_sup"), sem("s_supout")
        s_nb = sem("s_nb")
        s_hi, s_oh, s_ohp, s_deg = sem("s_hi"), sem("s_oh"), sem("s_ohp"), sem("s_deg")
        s_degall = sem("s_degall")
        s_scaled, s_table = sem("s_scaled"), sem("s_table")
        s_row = sem("s_row")
        s_same = sem("s_same")
        s_placed = sem("s_placed")
        s_dup, s_sh, s_to = sem("s_dup"), sem("s_sh"), sem("s_to")
        s_of = sem("s_of")
        s_mix, s_mixT = sem("s_mix"), sem("s_mixT")
        s_window = [sem(f"s_window{n}") for n in range(S4)]
        s_msg = sem("s_msg")
        s_sums = sem("s_sums")
        s_go = sem("s_go")
        s_tick = sem("s_tick")
        s_scat = [sem(f"s_scat{n}") for n in range(K)]
        s_back = [sem(f"s_back{n}") for n in range(SL)]
        s_pair = sem("s_pair")
        s_used = sem("s_used")
        s_h, s_ht, s_hT = sem("s_h"), sem("s_ht"), sem("s_hT")
        s_mcol, s_logit, s_e, s_pick, s_wt, s_wb, s_lg = (
            sem(n) for n in ("s_mcol", "s_logit", "s_e", "s_pick", "s_wt", "s_wb", "s_lg"))
        s_w1, s_w2, s_b12, s_b2c, s_wtop = sem("s_w1"), sem("s_w2"), sem("s_b12"), sem("s_b2c"), sem("s_wtop")
        s_W1h, s_W1l, s_W2h, s_W2l = sem("s_W1h"), sem("s_W1l"), sem("s_W2h"), sem("s_W2l")
        s_part = sem("s_part")
        s_ff1, s_gelu, s_hidh, s_hidl, s_ff2 = (sem(n) for n in ("s_ff1", "s_gelu", "s_hidh", "s_hidl", "s_ff2"))
        s_res, s_hb = sem("s_res"), sem("s_hb")
        s_z, s_zn, s_zg, s_zx, s_y = sem("s_z"), sem("s_zn"), sem("s_zg"), sem("s_zx"), sem("s_y")
        s_out = sem("s_out")
        s_cons = 9

        block = ctx.enter_context(nc.Block())

        x_v = x_d[0:NFULL * P, :].rearrange("(t p) d -> p t d", p=P)
        table_v = table_d[0:NFULL * P, :].rearrange("(t p) d -> p t d", p=P)

        @block.sync
        def _(sp):
            sp.wait_ge(s_pad, 2)
            for d, v, s in ((src_d, src_i, s_src), (dst_d, dst_i, s_dst), (ew_d, w_n, s_ew)):
                sp.dma_start(v[0:QFULL, :], d[0:QFULL * GP].rearrange("(q c) -> q c", c=GP)).then_inc(s, 16)
                sp.dma_start(v[QFULL:Q, 0:EREST], d[QFULL * GP:E].rearrange("(q c) -> q c", q=1)).then_inc(s, 16)
            sp.dma_start(dst_i[QFULL:Q, EREST:GP], dst_d[E - EPAD:E].rearrange("(q c) -> q c", q=1)).then_inc(s_dst, 16)
            sp.wait_ge(s_zero, 1)
            for k in range(K):
                v = sums_d[k].rearrange("(p r) d -> p (r d)", p=P)
                n = ROWS * D // P // ZCH
                for c in range(ZCH):
                    sp.dma_start(v[:, c * n:(c + 1) * n], zeros).then_inc(s_cleared, 16)
            sp.wait_ge(s_starts, 1)
            sp.dma_start(starts_d, starts_i[0:Q, :]).then_inc(s_starts_d, 16)
            sp.wait_ge(s_starts_d, 16)
            sp.dma_start(starts[0:1, :], starts_d.rearrange("(o q) g -> o (q g)", o=1)).then_inc(s_starts_r, 16)
            for c in range(XCH):
                sp.wait_ge(s_scaled, c + 1)
                last = min((c + 1) * CT, NFULL)
                sp.dma_start(table_v[:, c * CT:last, :], h[:, c * CT:last, :]).then_inc(s_table, 16)
            sp.dma_start(table_d[NFULL * P:N, :], h[0:TAIL, NFULL, :]).then_inc(s_table, 16)
            sp.wait_ge(s_table, 16 * (XCH + 1))
            sp.wait_ge(s_starts_r, 16)
            sp.wait_ge(s_flag, 1)
            sp.wait_ge(s_degall, 1)

            def windows(i):
                for n in range(S4):
                    wait_from(sp, s_msg, S4 * (i - 1) + n + 1)
                    _, at4 = nc.values_load_multi_w_load_instructions(starts[0:1, bass.ds((i * S4 + n) * K, K)],
                                                                      engines=(mybir.EngineType.SP,), min_val=0, max_val=N - P)
                    for j, at in enumerate(at4):
                        sp.dma_start(window[:, n * K + j, :], table_d[bass.ds(at, P), :]).then_inc(s_window[n], 16)

            gathers = sp.value_load(flag_i[0:1, 0:1], min_val=0, max_val=1)
            with sp.If(gathers < 1):
                windows(0)
                with sp.Fori(1, NB // S4) as i:
                    windows(i)

            for k in range(K):
                sp.wait_ge(s_scat[k], 16 * NB)

            def read_back(p, slot, n=2):
                for k in range(K):
                    v = sums_d[k][bass.ds(p * (2 * P), n * P), :] if not isinstance(p, int) else sums_d[k][p * 2 * P:(p * 2 + n) * P, :]
                    sp.dma_start(back[:, slot * K + k, 0:n * D].rearrange("p (j d) -> p j d", d=D),
                                 v.rearrange("(j p) d -> p j d", p=P)).then_inc(s_back[slot], 16)

            for slot in range(SL):
                read_back(slot, slot)
            with sp.Fori(1, NFULL // 2 // SL) as i:
                for slot in range(SL):
                    sp.wait_ge(s_used, SL * (i - 1) + slot + 1)
                    read_back(SL * i + slot, slot)
            sp.wait_ge(s_used, NFULL // 2 - SL + 1)
            read_back(NFULL // 2, 0, 1)

            sp.wait_ge(s_pick, 1)
            for e in range(TOP):
                pick = sp.value_load(pick_i[0:1, e:e + 1], min_val=0, max_val=NX - 1)
                sp.dma_start(W1raw[:, e * DC:(e + 1) * DC, :], W1_d[bass.ds(pick, 1), :, :].rearrange("o (c p) f -> p (o c) f", p=P)).then_inc(s_w1, 16)
                sp.dma_start(W2raw[:, e * FC:(e + 1) * FC, :], W2_d[bass.ds(pick, 1), :, :].rearrange("o (c p) n -> p (o c) n", p=P)).then_inc(s_w2, 16)
                with nc.allow_non_contiguous_dma(reason="a column of 512 biases"):
                    sp.dma_start(b1s[:, e, :], b1_d[bass.ds(pick, 1), :].rearrange("o (c p) -> p (o c)", p=P)).then_inc(s_b12, 16)
                sp.dma_start(b2s[:, e, :], b2_d[bass.ds(pick, 1), :].broadcast_to([P, D])).then_inc(s_b12, 16)

            with sp.Fori(0, NFULL // K) as i:
                sp.wait_ge(s_y, K * i + K)
                sp.dma_start(out_d[bass.ds(i * (K * P), K * P), :].rearrange("(t p) d -> p t d", p=P), y).then_inc(s_out, 16)
            sp.wait_ge(s_y, NT)
            sp.dma_start(out_d[NFULL * P:N, :], y[0:TAIL, 0, :]).then_inc(s_out, 16)
            sp.wait_ge(s_out, 16 * (NFULL // K + 1))

        @block.gpsimd
        def _(pool):
            nc.gpsimd.memset(src_i, PADSRC).then_inc(s_pad, 1)
            nc.gpsimd.memset(w_n, 0.0).then_inc(s_pad, 1)
            nc.gpsimd.memset(x[:, NFULL, :], 0.0).then_inc(s_const, 1)
            nc.gpsimd.iota(iota[:, :], [[1, P]], base=0, channel_multiplier=0,
                           allow_small_or_imprecise_dtypes=True).then_inc(s_const, 1)
            nc.gpsimd.memset(colsum[:, :, NT:NT + 1], 0.0)
            nc.gpsimd.iota(dummyc[:, :], [[0, 1]], base=DUMMY, channel_multiplier=1,
                           allow_small_or_imprecise_dtypes=True).then_inc(s_const, 1)
            nc.gpsimd.memset(ones[:, :], 1.0).then_inc(s_const, 1)
            nc.gpsimd.memset(half_power[:, :], -0.5).then_inc(s_const, 1)
            nc.gpsimd.memset(ident[:, :], 0.0).then_inc(s_const, 1)
            pool.wait_ge(s_const, 6)
            nc.gpsimd.affine_select(out=ident[:, :], in_=ident[:, :], compare_op=ALU.not_equal, fill=1.0, base=0,
                                    pattern=[[-1, P]], channel_multiplier=1).then_inc(s_const, 1)
            nc.gpsimd.affine_select(out=before[:, :], in_=ones[:, :], compare_op=ALU.is_gt, fill=0.0, base=0,
                                    pattern=[[-1, P]], channel_multiplier=1).then_inc(s_const, 1)
            pool.wait_ge(s_const, 8)
            nc.gpsimd.tensor_copy(identb[:, :], ident[:, :]).then_inc(s_const, 1)
            nc.gpsimd.memset(zeros, 0.0).then_inc(s_zero, 1)
            pool.wait_ge(s_turn, 8)
            pool.wait_ge(s_split, 1)
            nc.gpsimd.iota(iota16, [[1, P], [0, G2]], base=0, channel_multiplier=0,
                           allow_small_or_imprecise_dtypes=True).then_inc(s_zero, 1)

            def root(n, m=1):
                nc.gpsimd.tensor_tensor(rstd[:, n:n + m, :], var[:, n:n + m, :],
                                        half_power[:, 0:m].unsqueeze(2), ALU.pow).then_inc(s_root, 1)

            def pool_rows(t, m):
                pool.wait_ge(s_var, t + 1)
                wait_from(pool, s_ln, t - 1)
                root(m)
                pool.wait_ge(s_hi, t + 1)
                wait_from(pool, s_deg, t - 1)
                tt = bass.ds(t, 1) if not isinstance(t, int) else slice(t, t + 1)
                nc.gpsimd.tensor_tensor(oh_w[m][:, 2, :, :], oh_hi[m], w3[:, 2, tt, :].broadcast_to([P, NT, G2]),
                                        ALU.mult).then_inc(s_ohp, 1)

            for t in range(3):
                pool_rows(t, t % 2)
            with pool.Fori(1, NT // 2) as i:
                for m in range(2):
                    pool_rows(2 * i + 1 + m, 1 - m)
            pool.wait_ge(s_dis, 1)
            nc.gpsimd.tensor_tensor(dis[:, :], dis[:, :], half_power[:, :], ALU.pow).then_inc(s_dis, 1)

            pool.wait_ge(s_cleared, 16 * ZCH * K)
            pool.wait_ge(s_flag, 1)

            def scatter(b, n):
                pool.wait_ge(s_sums, b + 1)
                pool.wait_ge(s_to, b + 1)
                for j in range(K):
                    wait_from(pool, s_scat[j], 16 * b)
                    if not isinstance(b, int):
                        pool.sem_inc(s_go, 1)
                    pool.indirect_dma_start(
                        out=sums_d[j], out_offset=bass.IndirectOffsetOnAxis(ap=rows_to[:, n, j:j + 1], axis=0),
                        in_=sums[:, n * K + j, :], in_offset=None, compute_op=ALU.add).then_inc(s_scat[j], 16)

            def gather(b, n):
                pool.wait_ge(s_of, b + 1)
                wait_from(pool, s_msg, b - S4 + 1)
                if not isinstance(b, int):
                    pool.sem_inc(s_go, 1)
                for j in range(K):
                    pool.indirect_dma_start(
                        out=window[:, n * K + j, :], out_offset=None, in_=table_d,
                        in_offset=bass.IndirectOffsetOnAxis(ap=rows_of[:, n, j:j + 1], axis=0)).then_inc(s_window[n], 16)

            gathers = pool.value_load(flag_i[0:1, 0:1], min_val=0, max_val=1)
            with pool.If(gathers < 1):
                for n in range(S4):
                    scatter(n, n)
                with pool.Fori(1, NB // S4) as i:
                    for n in range(S4):
                        scatter(S4 * i + n, n)
            with pool.Else():
                pool.wait_ge(s_table, 16 * (XCH + 1))
                for n in range(S4):
                    gather(n, n)
                    scatter(n, n)
                with pool.Fori(1, NB // S4) as i:
                    for n in range(S4):
                        gather(S4 * i + n, n)
                        scatter(S4 * i + n, n)

            NP = NFULL // 2

            def pair(slot, turn, n=2):
                pool.wait_ge(s_back[slot], 16 * K * turn)
                a = back[:, slot * K:slot * K + 2, 0:n * D]
                nc.gpsimd.tensor_tensor(a, a, back[:, slot * K + 2:slot * K + 4, 0:n * D], ALU.add).then_inc(s_pair, 1)

            def root_rows(p, s, n=2):
                pool.wait_ge(s_var, NT + p + 1)
                wait_from(pool, s_h, p - 1)
                root(2 * s, n)

            assert NP % SL == 0
            for p in range(2):
                pair(p, 1)
            for p in range(SL):
                pair((p + 2) % SL, (p + 2) // SL + 1)
                root_rows(p, p % 2)
            with pool.Fori(1, NP // SL - 1) as i:
                for m in range(SL):
                    pair((m + 2) % SL, i + (m + 2) // SL + 1)
                    root_rows(SL * i + m, m % 2)
            for p in range(NP - SL, NP - 1):
                pair((p + 2) % SL, (p + 2) // SL + 1, 1 if p + 2 == NP else 2)
                root_rows(p, p % 2)
            root_rows(NP - 1, (NP - 1) % 2)
            root_rows(NP, NP % 2, 1)

            pool.wait_ge(s_b2c, 1)
            pool.wait_ge(s_gb, 32)

            def residual(t, j):
                pool.wait_ge(s_res, t + 1)
                nc.gpsimd.tensor_tensor(z[:, j, :], z[:, j, :], b2c[:, :], ALU.add).then_inc(s_hb, 1)

            def scaled(t, j, i):
                tt = slice(t, t + 1) if isinstance(t, int) else bass.ds(t, 1)
                pool.wait_ge(s_zn, t + 1)
                nc.gpsimd.tensor_tensor(zg[:, j, :], z[:, j, :], gamma[:, :], ALU.mult).then_inc(s_zg, 1)
                pool.wait_ge(s_zg, t + 1)
                pool.sem_inc(s_go, 1)
                nc.gpsimd.tensor_tensor(zg[:, j:j + 1, :], zg[:, j:j + 1, :], x[:, tt, :], ALU.add).then_inc(s_zx, 1)
                pool.wait_ge(s_zx, t + 1)
                wait_from(pool, s_out, 16 * i)
                nc.gpsimd.tensor_tensor(y[:, j, :], zg[:, j, :], beta[:, :], ALU.add).then_inc(s_y, 1)

            def pool_group(i, tiles):
                for j in range(tiles):
                    residual(K * i + j, j)
                pool.wait_ge(s_var, NT + NP + 1 + i + 1)
                root(4, tiles)
                for j in range(tiles):
                    scaled(K * i + j, j, i)

            pool_group(0, K)
            with pool.Fori(1, NFULL // K) as i:
                pool_group(i, K)
            pool_group(NFULL // K, 1)

        @block.scalar
        def _(act):
            for c in range(XCH):
                last = min((c + 1) * CT, NFULL)
                act.dma_start(x[:, c * CT:last, :], x_v[:, c * CT:last, :]).then_inc(s_x, 16)
            act.wait_ge(s_const, 1)
            act.dma_start(x[0:TAIL, NFULL, :], x_d[NFULL * P:N, :]).then_inc(s_x, 16)
            act.dma_start(W[:, :, :], W_d.rearrange("(c p) n -> p c n", p=P)).then_inc(s_W, 16)
            act.dma_start(b_row[0:1, :], b_d.rearrange("(o n) -> o n", o=1)).then_inc(s_W, 16)
            act.dma_start(Wr[:, :, :], Wr_d.rearrange("(c p) n -> p c n", p=P)).then_inc(s_wr, 16)
            act.dma_start(rt[0:1, 0, :], br_d.rearrange("(o n) -> o n", o=1)).then_inc(s_wr, 16)
            act.dma_start(gamma[:, :], gamma_d.rearrange("(o n) -> o n", o=1).broadcast_to([P, D])).then_inc(s_gb, 16)
            act.dma_start(beta[:, :], beta_d.rearrange("(o n) -> o n", o=1).broadcast_to([P, D])).then_inc(s_gb, 16)

            for n, to in enumerate((dstT, wT, srcT, placeT)):
                for half in range(2):
                    act.wait_ge(s_turn, 2 * n + half + 1)
                    nc.scalar.copy(to[:, half * K:(half + 1) * K, :],
                                   bank[2 * (n % 2) + half][:, 0:K * Q].rearrange("p (g q) -> p g q", q=Q)).then_inc(s_turned, 1)

            def act_rows(t, m):
                tt = slice(t, t + 1) if isinstance(t, int) else bass.ds(t, 1)
                act.wait_ge(s_nb, t + 1)
                wait_from(act, s_lnt, t)
                nc.scalar.activation(ln.unsqueeze(1), x[:, tt, :], ACT.Identity, bias=shiftm[:, m, :], scale=rstd[:, m, :]).then_inc(s_ln, 1)
                act.wait_ge(s_lnt, t + 1)
                nc.scalar.copy(lnT, bank[1][:, 0:D].rearrange("p (c n) -> p c n", n=P)).then_inc(s_lnT, 1)
                act.wait_ge(s_sup, t + 1)
                nc.scalar.copy(h[:, tt, :], bank[2][:, None, 0:D]).then_inc(s_supout, 1)

            for t in range(3):
                act_rows(t, t % 2)
            with act.Fori(1, NT // 2) as i:
                for m in range(2):
                    act_rows(2 * i + 1 + m, 1 - m)

            def mix_out(i, n):
                b, q, half, m = S4 * i + n, 2 * i + n // 2, n % 2, n % 2
                ks = slice(half * K, (half + 1) * K)
                qq = slice(q, q + 1) if isinstance(q, int) else bass.ds(q, 1)
                wait_from(act, s_window[n], 16 * K * i)
                nc.scalar.copy(rows_of[:, n, :].unsqueeze(2), dstT[:, ks, qq]).then_inc(s_of, 1)
                act.wait_ge(s_mix, b + 1)
                wait_from(act, s_msg, b - 1)
                nc.scalar.copy(mixT[:, m, :, :], bank[2 + m][:, :].rearrange("p (k n) -> p k n", n=P)).then_inc(s_mixT, 1)

            def sums_out(b, n):
                act.wait_ge(s_msg, b + 1)
                for k in range(K):
                    wait_from(act, s_scat[k], 16 * (b - S4 + 1))
                for c in range(2):
                    last = nc.scalar.copy(sums[:, n * K + 2 * c:n * K + 2 * c + 2, :],
                                          bank[4 + 2 * (n % 2) + c][:, :].rearrange("p (k n) -> p k n", n=D))
                last.then_inc(s_sums, 1)

            def act_blocks(i):
                for n in range(S4):
                    mix_out(i, n)
                    if not isinstance(i, int) or S4 * i + n >= 1:
                        sums_out(S4 * i + n - 1, (n - 1) % S4)

            act.wait_ge(s_degall, 1)
            act.wait_ge(s_table, 16 * (XCH + 1))
            act.wait_ge(s_cleared, 16 * ZCH * K)
            act_blocks(0)
            act_blocks(1)
            with act.Fori(2, NB // S4) as i:
                act_blocks(i)
            sums_out(NB - 1, S4 - 1)

            for k in range(K):
                act.wait_ge(s_scat[k], 16 * NB)

            def row_norm(p, s, n=2):
                for m in range(n):
                    t = 2 * p + m
                    tt = slice(t, t + 1) if isinstance(t, int) else bass.ds(t, 1)
                    if m == 0:
                        act.wait_ge(s_nb, NT + p + 1)
                        wait_from(act, s_ht, 2 * p - 2)
                    last = nc.scalar.activation(hs[:, 2 * s + m:2 * s + m + 1, :], x[:, tt, :], ACT.Identity,
                                                bias=shiftm[:, 2 * s + m, :], scale=rstd[:, 2 * s + m, :])
                last.then_inc(s_h, 1)

            def row_out(t, s, n=P):
                at = t * P
                act.wait_ge(s_ht, t + 1)
                for c in range(DC):
                    last = nc.scalar.activation(hT[:, c, at:at + n] if isinstance(t, int) else hT[:, c, bass.ds(at, n)],
                                                bank[s][:, c * P:c * P + n], ACT.Copy,
                                                accum_out=colsum[:, c, t:t + 1] if isinstance(t, int) else colsum[:, c, bass.ds(t, 1)])
                if n < P:
                    for c in range(DC):
                        last = nc.scalar.copy(hT[:, c, at + n:at + P], bank[s][:, c * P + n:(c + 1) * P])
                last.then_inc(s_hT, 1)

            def row_pairs(p, s):
                row_norm(p, s)
                if not isinstance(p, int) or p >= 1:
                    for m in range(2):
                        row_out(2 * (p - 1) + m, 2 * (1 - s) + m)

            NP = NFULL // 2
            for p in range(2):
                row_pairs(p, p % 2)
            with act.Fori(1, NP // 2) as i:
                for s in range(2):
                    row_pairs(2 * i + s, s)
            row_norm(NP, 0, 1)
            for m in range(2):
                row_out(NFULL - 2 + m, 2 + m)
            row_out(NFULL, 0, TAIL)

            for n in range(3):
                act.wait_ge(s_lg, n + 1)
                w = NX if n < 2 else TOP
                nc.scalar.activation(rt[0:1, 20 + n, 0:w], rt[0:1, 16 + n, 0:w], ACT.Exp).then_inc(s_e, 1)

            for e in range(TOP):
                if e == 0:
                    act.wait_ge(s_w1, 32)
                for c in range(DC):
                    nc.scalar.copy(W1h[:, e, c, :], W1raw[:, e * DC + c, :]).then_inc(s_W1h, 1)
            act.wait_ge(s_w2, 32)
            act.wait_ge(s_wtop, 1)
            for e in range(TOP):
                nc.scalar.activation(W2h[:, e * FC:(e + 1) * FC, :], W2raw[:, e * FC:(e + 1) * FC, :], ACT.Copy,
                                     scale=wtop[:, e:e + 1]).then_inc(s_W2h, 1)

            act.wait_ge(s_b12, 64)
            act.wait_ge(s_W1l, TOP)

            def gelu(i, n):
                for k in range(TOP * FC):
                    c = TOP * FC * i + k
                    act.wait_ge(s_ff1, c + 1)
                    wait_from(act, s_hidl, c - 3)
                    nc.scalar.activation(hid[:, k % 4, 0:n], bank[k % 4][:, 0:n], ACT.Gelu,
                                         bias=b1s[:, k // FC, k % FC:k % FC + 1]).then_inc(s_gelu, 1)
                    act.wait_ge(s_gelu, c + 1)
                    if k == 0:
                        wait_from(act, s_ff2, K * i)
                    nc.scalar.copy(hidh[:, k, 0:n], hid[:, k % 4, 0:n]).then_inc(s_hidh, 1)

            gelu(0, K * P)
            with act.Fori(1, NFULL // K) as i:
                gelu(i, K * P)
            gelu(NFULL // K, P)

        @block.vector
        def _(dve):
            me = Steps(dve, s_dve)

            dve.wait_ge(s_dst, 48)
            nc.vector.tensor_copy(dst_n[0:Q, :], dst_i[0:Q, :]).then_inc(s_nat, 1)
            dve.wait_ge(s_src, 32)
            nc.vector.tensor_copy(src_n[0:Q, :], src_i[0:Q, :]).then_inc(s_nat, 1)
            dve.wait_ge(s_nat, 2)
            least, most, start, toofar = (nat8[0:Q, n, :] for n in range(4))
            nc.vector.tensor_reduce(least, as_tiles(dst_n[0:Q, :]), AX, ALU.min)
            me.link(nc.vector.tensor_reduce(most, as_tiles(dst_n[0:Q, :]), AX, ALU.max))
            me.link(nc.vector.tensor_scalar(start, least, float(N - P), None, ALU.min))
            nc.vector.tensor_copy(starts_i[0:Q, :], start).then_inc(s_starts, 1)
            me.link(nc.vector.tensor_tensor(toofar, most, start, ALU.subtract))
            me.link(nc.vector.tensor_scalar(toofar, toofar, P - 0.5, None, ALU.is_gt))
            nc.vector.tensor_reduce(far[0:Q, 0:1], toofar, AX, ALU.add).then_inc(s_far, 1)
            me.link(nc.vector.tensor_tensor(as_tiles(place_n[0:Q, :]), as_tiles(dst_n[0:Q, :]),
                                            start.unsqueeze(2).broadcast_to([Q, G, P]), ALU.subtract))
            dve.wait_ge(s_farall, 1)
            me.link(nc.vector.tensor_scalar(far[:, 1:2], bank[7][:, 0:1], 0.5, None, ALU.is_gt))
            nc.vector.tensor_copy(flag_i[:, :], far[:, 1:2]).then_inc(s_flag, 1)
            dve.wait_ge(s_const, s_cons)
            me.link(nc.vector.tensor_tensor(as_tiles(tmp_n[0:Q, :]), iota[0:Q, None, :].broadcast_to([Q, G, P]),
                                            as_tiles(place_n[0:Q, :]), ALU.subtract))
            nc.vector.scalar_tensor_tensor(out=place_n[0:Q, :], in0=tmp_n[0:Q, :], scalar=far[0:Q, 1:2],
                                           in1=place_n[0:Q, :], op0=ALU.mult, op1=ALU.add).then_inc(s_nat, 1)
            me.link(nc.vector.tensor_scalar(tmp_i[0:Q, :], src_i[0:Q, :], 7, 7, ALU.arith_shift_right, ALU.arith_shift_left))
            me.link(nc.vector.tensor_copy(src_hi[0:Q, :], tmp_i[0:Q, :]))
            me.link(nc.vector.tensor_scalar(tmp_i[0:Q, :], src_i[0:Q, :], 127, None, ALU.bitwise_and))
            nc.vector.tensor_copy(src_lo[0:Q, :], tmp_i[0:Q, :]).then_inc(s_split, 1)
            by_g = lambda v: v.rearrange("p t (u g) -> p g (t u)", g=G)
            dve.wait_ge(s_turned, 2)
            me.link(nc.vector.tensor_copy(tmpT_i, dstT))
            me.link(nc.vector.tensor_scalar(tmpT2_i, tmpT_i, 7, None, ALU.arith_shift_right))
            me.link(nc.vector.tensor_copy(by_g(dst_hi), tmpT2_i))
            me.link(nc.vector.tensor_scalar(tmpT2_i, tmpT_i, 127, None, ALU.bitwise_and))
            me.link(nc.vector.tensor_copy(by_g(dst_lo), tmpT2_i))
            dve.wait_ge(s_turned, 4)
            me.link(nc.vector.tensor_copy(by_g(w3[:, 0, :, :]), wT))
            me.link(nc.vector.tensor_tensor(rest, wT, by_g(w3[:, 0, :, :]), ALU.subtract))
            me.link(nc.vector.tensor_copy(by_g(w3[:, 1, :, :]), rest))
            me.link(nc.vector.tensor_tensor(by_g(w3[:, 2, :, :]), rest, by_g(w3[:, 1, :, :]), ALU.subtract))
            dve.wait_ge(s_turned, 6)
            me.link(nc.vector.tensor_scalar(shiftT, srcT, -1.0, dummyc[:, 0:1], ALU.mult, ALU.add))
            dve.wait_ge(s_x, 16 * (XCH + 1))

            def statistics(of, n):
                dve.sem_inc(s_tick, 1)
                me.link(nc.vector.bn_stats(stats[:, n, :], of))
                dve.sem_inc(s_tick, 1)
                me.link(nc.vector.bn_aggr(mv[:, n, :], stats[:, n, :]))
                nc.vector.tensor_scalar(var[:, n, :], mv[:, n, 1:2], EPS, None, ALU.add).then_inc(s_var, 1)

            def normalize(to, of, n):
                return nc.vector.tensor_scalar(to, of, mv[:, n, 0:1], rstd[:, n, :], ALU.subtract, ALU.mult)

            def minus_mean(n, m=1):
                nc.vector.scalar_tensor_tensor(out=shiftm[:, n:n + m, :], in0=mv[:, n:n + m, 0:1], scalar=-1.0,
                                               in1=rstd[:, n:n + m, :], op0=ALU.mult, op1=ALU.mult).then_inc(s_nb, 1)

            def step(t, m, ahead=True):
                if ahead:
                    dve.sem_inc(s_tick, 1)
                    me.add(nc.vector.bn_stats(stats[:, 1 - m, :], row(t + 1)))
                tt = slice(t, t + 1) if isinstance(t, int) else bass.ds(t, 1)
                wait_from(dve, s_deg, t - 1)
                wait_from(dve, s_ohp, t - 1)
                nc.vector.tensor_tensor(oh_hi[m], iota16[:, 0:NT, :], dst_hi[:, tt, :].broadcast_to([P, NT, G2]),
                                        ALU.is_equal).then_inc(s_hi, 1)
                if ahead:
                    me.wait()
                    dve.sem_inc(s_tick, 1)
                    me.add(nc.vector.bn_aggr(mv[:, 1 - m, :], stats[:, 1 - m, :]))
                nc.vector.tensor_tensor(oh_lo[m], iota16, dst_lo[:, tt, :].broadcast_to([P, P, G2]), ALU.is_equal)
                if ahead:
                    me.wait()
                    nc.vector.tensor_scalar(var[:, 1 - m, :], mv[:, 1 - m, 1:2], EPS, None, ALU.add).then_inc(s_var, 1)
                dve.wait_ge(s_hi, t + 1)
                for n in range(2):
                    last = nc.vector.tensor_tensor(oh_w[m][:, n, :, :], oh_hi[m], w3[:, n, tt, :].broadcast_to([P, NT, G2]),
                                                   ALU.mult)
                last.then_inc(s_oh, 1)
                if ahead:
                    dve.wait_ge(s_root, t + 2)
                    wait_from(dve, s_ln, t)
                    minus_mean(1 - m)

            row = lambda t: x[:, t, :] if isinstance(t, int) else x[:, bass.ds(t, 1), :].rearrange("p o d -> p (o d)")
            dve.wait_ge(s_zero, 2)
            done = me.base + me.n
            me.at(done)
            statistics(row(0), 0)
            per = me.n
            dve.wait_ge(s_root, 1)
            minus_mean(0)
            for t in range(3):
                step(t, t % 2)
            assert me.n == 4 * per
            with dve.Fori(1, NT // 2 - 1) as i:
                for m in range(2):
                    me.at(done + (2 * i + 2 + m) * per)
                    step(2 * i + 1 + m, 1 - m)
                    assert me.n == per
            me.at(done + (NT - 1) * per)
            step(NT - 2, 1)
            step(NT - 1, 0, ahead=False)
            me.at(done + NT * per)

            dve.wait_ge(s_degall, 1)
            me.link(nc.vector.tensor_scalar(dis[:, :], bank[0][:, 0:NT], 1.0, None, ALU.add))
            me.link(nc.vector.tensor_tensor(dis[:, :], dis[:, :], bank[0][:, NT:2 * NT], ALU.add))
            nc.vector.tensor_tensor(dis[:, :], dis[:, :], bank[0][:, 2 * NT:3 * NT], ALU.add).then_inc(s_dis, 1)
            dve.wait_ge(s_dis, 2)
            dve.wait_ge(s_supout, NT)
            for c in range(XCH):
                v = h[:, c * CT:(c + 1) * CT, :]
                nc.vector.tensor_tensor(v, v, dis[:, c * CT:(c + 1) * CT].unsqueeze(2).broadcast_to([P, CT, D]),
                                        ALU.mult).then_inc(s_scaled, 1)

            def messages(i, n):
                b, q, half, m = S4 * i + n, 2 * i + n // 2, n % 2, n % 2
                qq = slice(q, q + 1) if isinstance(q, int) else bass.ds(q, 1)
                ks = slice(half * K, (half + 1) * K)
                wait_from(dve, s_mix, b - 1)
                dve.wait_ge(s_row, b + 1)
                nc.vector.tensor_tensor(same[:, m, :, :], bank[m][:, :].rearrange("p (k n) -> p k n", n=P),
                                        srcT[:, ks, qq].broadcast_to([P, K, P]), ALU.is_equal).then_inc(s_same, 1)
                for j in range(K):
                    last = nc.vector.tensor_scalar(placed[:, m, j, :], iota[:, :], placeT[:, half * K + j, qq],
                                                   wT[:, half * K + j, qq], ALU.is_equal, ALU.mult)
                last.then_inc(s_placed, 1)
                dve.wait_ge(s_same, b + 1)
                for j in range(K):
                    last = nc.vector.tensor_tensor_reduce(out=junk[:, m * K + j, :], in0=same[:, m, j, :], in1=before[:, :],
                                                          scale=1.0, scalar=0.0, op0=ALU.mult, op1=ALU.add,
                                                          accum_out=same_before[:, m, j:j + 1])
                last.then_inc(s_dup, 1)
                dve.wait_ge(s_dup, b + 1)
                nc.vector.scalar_tensor_tensor(out=shift[:, m, :].unsqueeze(2), in0=same_before[:, m, :].unsqueeze(2),
                                               scalar=0.5, in1=shiftT[:, ks, qq], op0=ALU.is_gt, op1=ALU.mult).then_inc(s_sh, 1)
                dve.wait_ge(s_sh, b + 1)
                for k in range(K):
                    wait_from(dve, s_scat[k], 16 * (b - S4 + 1))
                nc.vector.tensor_tensor(rows_to[:, n, :].unsqueeze(2), shift[:, m, :].unsqueeze(2),
                                        srcT[:, ks, qq], ALU.add).then_inc(s_to, 1)

            dve.wait_ge(s_turned, 8)
            dve.wait_ge(s_cleared, 16 * ZCH * K)
            for n in range(S4):
                messages(0, n)
            with dve.Fori(1, NB // S4) as i:
                for n in range(S4):
                    messages(i, n)

            done = me.base + me.n
            NP = NFULL // 2

            def squares(p, s, n=2):
                dve.wait_ge(s_used, p + 1)
                dve.sem_inc(s_tick, 1)
                for m in range(n):
                    t = 2 * p + m
                    xt = x[:, bass.ds(t, 1) if not isinstance(t, int) else slice(t, t + 1), :].rearrange("p o d -> p (o d)")
                    last = nc.vector.bn_stats(stats[:, 2 * s + m, :], xt)
                me.add(last)

            def moments(s, n=2):
                dve.sem_inc(s_tick, 1)
                for m in range(n):
                    last = nc.vector.bn_aggr(mv[:, 2 * s + m, :], stats[:, 2 * s + m, :])
                me.add(last)

            def variances(s, n=2):
                nc.vector.tensor_scalar(var[:, 2 * s:2 * s + n, :], mv[:, 2 * s:2 * s + n, 1:2], EPS, None, ALU.add).then_inc(s_var, 1)

            def new_stats(p, s, n=2):
                tt = bass.ds(2 * p, n) if not isinstance(p, int) else slice(2 * p, 2 * p + n)
                dve.wait_ge(s_root, NT + p + 1)
                wait_from(dve, s_h, p - 1)
                minus_mean(2 * s, n)
                nc.vector.tensor_copy(rowstat[:, tt, 0:1], rstd[:, 2 * s:2 * s + n, :])
                dve.wait_ge(s_nb, NT + p + 1)
                me.add(nc.vector.tensor_copy(rowstat[:, tt, 1:2], shiftm[:, 2 * s:2 * s + n, :]))

            def new_rows(p, slot, n=2, before_it=True, two_before=True):
                tt = bass.ds(2 * p, n) if not isinstance(p, int) else slice(2 * p, 2 * p + n)
                s = slot % 2
                a, c = (back[:, slot * K + k, 0:n * D] for k in range(2))
                dve.wait_ge(s_pair, p + 1)
                me.add(nc.vector.tensor_tensor(a, a, c, ALU.add))
                one = me.n
                if before_it:
                    squares(p - 1, 1 - s)
                me.wait(one)
                a2 = a.rearrange("p (j d) -> p j d", d=D)
                me.add(nc.vector.tensor_tensor(a2, a2, h[:, tt, :], ALU.add))
                two = me.n
                if before_it:
                    me.wait(one + 1)
                    moments(1 - s)
                me.wait(two)
                for m in range(n):
                    t = 2 * p + m
                    t1 = bass.ds(t, 1) if not isinstance(t, int) else slice(t, t + 1)
                    xt = x[:, t1, :].rearrange("p o d -> p (o d)")
                    last = nc.vector.scalar_tensor_tensor(out=xt, in0=a2[:, m, :], scalar=dis[:, t1], in1=xt, op0=ALU.mult, op1=ALU.add)
                last.then_inc(s_used, 1)
                if before_it:
                    me.wait()
                    variances(1 - s)
                if two_before:
                    new_stats(p - 2, s)

            dve.wait_ge(s_to, NB)
            dve.wait_ge(s_mix, NB)
            me.at(done)
            new_rows(0, 0, before_it=False, two_before=False)
            new_rows(1, 1, two_before=False)
            done += me.n
            one = 5
            for p in range(2, SL):
                me.at(done + (p - 2) * one)
                new_rows(p, p % SL)
            assert me.n == one
            with dve.Fori(1, NP // SL) as i:
                for m in range(SL):
                    p = SL * i + m
                    me.at(done + (p - 2) * one)
                    new_rows(p, m)
                    assert me.n == one
            me.at(done + (NP - 2) * one)
            new_rows(NP, 0, n=1)
            new_stats(NP - 1, 1)
            squares(NP, 0, 1)
            me.wait()
            moments(0, 1)
            me.wait()
            variances(0, 1)
            new_stats(NP, 0, 1)

            R = lambda n: rt[0:1, n, :]
            S = lambda n: rs[0:1, n:n + 1]
            dve.wait_ge(s_hT, NT)
            me.link(nc.vector.tensor_reduce(mean_col[:, :], colsum[:, :, 0:NT], AX, ALU.add))
            nc.vector.tensor_scalar(mean_col[:, :], mean_col[:, :], 1.0 / N, None, ALU.mult).then_inc(s_mcol, 1)
            dve.wait_ge(s_logit, 1)
            dve.wait_ge(s_wr, 32)
            me.link(nc.vector.tensor_tensor(R(1), bank[5][0:1, 0:NX], R(0), ALU.add))

            def softmax(of, n, w, to):
                me.link(nc.vector.tensor_reduce(S(0), of, AX, ALU.max))
                nc.vector.tensor_scalar(rt[0:1, 16 + n, 0:w], of, S(0), None, ALU.subtract).then_inc(s_lg, 1)
                dve.wait_ge(s_e, n + 1)
                me.link(nc.vector.tensor_reduce(S(1), rt[0:1, 20 + n, 0:w], AX, ALU.add))
                me.link(nc.vector.reciprocal(S(2), S(1)))
                me.link(nc.vector.tensor_scalar(to, rt[0:1, 20 + n, 0:w], S(2), None, ALU.mult))

            softmax(R(1), 0, NX, R(2))
            me.link(nc.vector.tensor_scalar(R(3), R(2), float(N), None, ALU.mult))
            me.link(nc.vector.reciprocal(R(4), R(3)))
            me.link(nc.vector.tensor_scalar(R(4), R(4), CAP, None, ALU.mult))
            me.link(nc.vector.tensor_scalar(R(5), R(3), CAP, None, ALU.is_gt))
            me.link(nc.vector.tensor_scalar(R(6), R(3), CAP, None, ALU.is_le))
            me.link(nc.vector.tensor_tensor(R(4), R(4), R(5), ALU.mult))
            me.link(nc.vector.tensor_tensor(R(4), R(4), R(6), ALU.add))
            me.link(nc.vector.tensor_tensor(R(7), R(2), R(4), ALU.mult))
            softmax(R(7), 1, NX, R(8))
            for e in range(TOP):
                me.link(nc.vector.tensor_reduce(rs[0:1, 4 + e:5 + e], R(8), AX, ALU.max))
                me.link(nc.vector.tensor_scalar(R(9), R(8), S(4 + e), float(NX), ALU.is_lt, ALU.mult))
                me.link(nc.vector.tensor_tensor(R(9), R(9), iota[0:1, 0:NX], ALU.add))
                me.link(nc.vector.tensor_reduce(rs[0:1, 6 + e:7 + e], R(9), AX, ALU.min))
                me.link(nc.vector.tensor_scalar(R(10), iota[0:1, 0:NX], S(6 + e), -2.0, ALU.is_equal, ALU.mult))
                me.link(nc.vector.tensor_tensor(R(8), R(8), R(10), ALU.add))
            nc.vector.tensor_copy(pick_i[0:1, :], rs[0:1, 6:6 + TOP]).then_inc(s_pick, 1)
            softmax(rs[0:1, 4:4 + TOP], 2, TOP, rs[0:1, 8:8 + TOP])
            dve.wait_ge(s_dve, me.base + me.n)
            nc.vector.tensor_copy(rs[0:1, 10:10 + TOP], rs[0:1, 8:8 + TOP]).then_inc(s_wt, 1)

            dve.wait_ge(s_W1h, TOP * DC)
            for e in range(TOP):
                nc.vector.tensor_tensor(W1l[:, e, :, :], W1raw[:, e * DC:(e + 1) * DC, :], W1h[:, e, :, :].bitcast(fp32),
                                        ALU.subtract).then_inc(s_W1l, 1)
            dve.wait_ge(s_wb, 1)
            nc.vector.tensor_copy(wtop[:, :], bank[4][:, 0:TOP]).then_inc(s_wtop, 1)

            def split_rows(i, n):
                cols = slice(i * K * P, i * K * P + n) if isinstance(i, int) else bass.ds(i * (K * P), n)
                wait_from(dve, s_ff1, TOP * FC * i)
                nc.vector.tensor_copy(hTh[:, :, 0:n], hT[:, :, cols]).then_inc(s_part, 1)
                dve.wait_ge(s_part, 2 * i + 1)
                nc.vector.tensor_tensor(hTl[:, :, 0:n], hT[:, :, cols], hTh[:, :, 0:n].bitcast(fp32), ALU.subtract).then_inc(s_part, 1)

            split_rows(0, K * P)
            dve.wait_ge(s_wtop, 1)
            dve.wait_ge(s_b12, 64)
            me.link(nc.vector.tensor_scalar(b2c[:, :], b2s[:, 0, :], wtop[:, 0:1], None, ALU.mult))
            nc.vector.scalar_tensor_tensor(out=b2c[:, :], in0=b2s[:, 1, :], scalar=wtop[:, 1:2], in1=b2c[:, :],
                                           op0=ALU.mult, op1=ALU.add).then_inc(s_b2c, 1)
            dve.wait_ge(s_W2h, TOP)
            for e in range(TOP):
                v = slice(e * FC, (e + 1) * FC)
                nc.vector.scalar_tensor_tensor(out=W2l[:, v, :], in0=W2raw[:, v, :], scalar=wtop[:, e:e + 1],
                                               in1=W2h[:, v, :].bitcast(fp32), op0=ALU.mult, op1=ALU.subtract).then_inc(s_W2l, 1)
            dve.wait_ge(s_W2l, TOP)

            def residual(t, j):
                t1 = bass.ds(t, 1) if not isinstance(t, int) else slice(t, t + 1)
                wait_from(dve, s_zg, t - K + 1)
                nc.vector.tensor_scalar(z[:, j:j + 1, :], x[:, t1, :], rowstat[:, t1, 0:1].rearrange("p o d -> p (o d)"),
                                        rowstat[:, t1, 1:2].rearrange("p o d -> p (o d)"), ALU.mult, ALU.add).then_inc(s_res, 1)

            def low_part(i, k, n):
                dve.wait_ge(s_hidh, TOP * FC * i + k + 1)
                if k == 0:
                    wait_from(dve, s_ff2, K * i)
                nc.vector.tensor_tensor(hidl[:, k, 0:n], hid[:, k % 4, 0:n], hidh[:, k, 0:n].bitcast(fp32),
                                        ALU.subtract).then_inc(s_hidl, 1)

            def last_sum(t, j):
                dve.wait_ge(s_ff2, t + 1)
                dve.wait_ge(s_hb, t + 1)
                nc.vector.tensor_tensor(z[:, j, :], bank[4 + j][:, 0:D], z[:, j, :], ALU.add).then_inc(s_z, 1)

            def last_squares(t, j):
                dve.wait_ge(s_z, t + 1)
                dve.sem_inc(s_tick, 1)
                me.add(nc.vector.bn_stats(stats[:, 4 + j, :], z[:, j, :]))

            def last_variances(tiles):
                me.wait()
                dve.sem_inc(s_tick, 1)
                for j in range(tiles):
                    me.add(nc.vector.bn_aggr(mv[:, 4 + j, :], stats[:, 4 + j, :]))
                me.wait()
                nc.vector.tensor_scalar(var[:, 4:4 + tiles, :], mv[:, 4:4 + tiles, 1:2], EPS, None, ALU.add).then_inc(s_var, 1)

            def last_normal(i, j):
                dve.wait_ge(s_root, NT + NP + 1 + i + 1)
                normalize(z[:, j, :], z[:, j, :], 4 + j).then_inc(s_zn, 1)

            done = me.base + me.n
            GR = NFULL // K

            def group(i, n, tiles, after):
                me.at(done + (i - 1) * (2 * K))
                t = K * (i - 1)
                for j in range(2):
                    last_sum(t + j, j)
                for j in range(2):
                    last_squares(t + j, j)
                last_sum(t + 2, 2)
                low_part(i, 0, n)
                last_sum(t + 3, 3)
                for j in range(2, K):
                    last_squares(t + j, j)
                low_part(i, 1, n)
                last_variances(K)
                assert me.n == 2 * K
                low_part(i, 2, n)
                for j in range(K):
                    last_normal(i - 1, j)
                    low_part(i, 3 + j, n)
                low_part(i, TOP * FC - 1, n)
                if after:
                    split_rows(i + 1, after)
                for j in range(tiles):
                    residual(K * i + j, j)

            for k in range(TOP * FC):
                low_part(0, k, K * P)
            split_rows(1, K * P)
            for j in range(K):
                residual(j, j)
            with dve.Fori(1, GR - 1) as i:
                group(i, K * P, K, K * P)
            group(GR - 1, K * P, K, P)
            group(GR, P, 1, 0)
            me.at(done + GR * 2 * K)
            last_sum(NFULL, 0)
            last_squares(NFULL, 0)
            last_variances(1)
            last_normal(GR, 0)

        @block.tensor
        def _(pe):
            mm = nc.tensor.matmul
            pe.wait_ge(s_const, s_cons)
            for n, of in enumerate((dst_n, w_n, src_n, place_n)):
                if n == 0:
                    pe.wait_ge(s_nat, 1)
                if n == 1:
                    pe.wait_ge(s_ew, 32)
                if n == 2:
                    pe.wait_ge(s_nat, 2)
                if n == 3:
                    pe.wait_ge(s_far, 1)
                    mm(bank[7][:, 0:1], ones[0:Q, :], far[0:Q, 0:1], start=True, stop=True).then_inc(s_farall, 1)
                    pe.wait_ge(s_nat, 3)
                for half in range(2):
                    to = bank[2 * (n % 2) + half]
                    if n >= 2:
                        pe.wait_ge(s_turned, 2 * (n - 2) + half + 1)
                    for j in range(K):
                        last = nc.tensor.transpose(to[:, j * Q:(j + 1) * Q], of[0:Q, (half * K + j) * P:(half * K + j + 1) * P],
                                                   ident[0:Q, 0:Q])
                    last.then_inc(s_turn, 1)

            pe.wait_ge(s_turned, 8)
            pe.wait_ge(s_zero, 1)
            pe.wait_ge(s_W, 32)
            mm(bank[0][:, 0:3 * NT], zeros[:, 0:P], zeros[:, 0:3 * NT], start=True, stop=False, skip_group_check=True)

            def pe_rows(t, m):
                pe.wait_ge(s_ln, t + 1)
                for c in range(DC):
                    last = nc.tensor.transpose(bank[1][:, c * P:(c + 1) * P], ln[:, c * P:(c + 1) * P], ident[:, :])
                last.then_inc(s_lnt, 1)
                pe.wait_ge(s_lnT, t + 1)
                mm(bank[2][:, 0:D], ones[0:1, :], b_row[0:1, :], start=True, stop=False)
                for c in range(DC):
                    last = mm(bank[2][:, 0:D], lnT[:, c, :], W[:, c, :], start=False, stop=(c == DC - 1))
                last.then_inc(s_sup, 1)
                pe.wait_ge(s_oh, t + 1)
                pe.wait_ge(s_ohp, t + 1)
                for g in range(G2):
                    last = mm(bank[0][:, 0:3 * NT], oh_lo[m][:, :, g], oh_w[m][:, :, :, g], start=False,
                              stop=False, skip_group_check=True)
                last.then_inc(s_deg, 1)

            for t in range(3):
                pe_rows(t, t % 2)
            with pe.Fori(1, NT // 2) as i:
                for m in range(2):
                    pe_rows(2 * i + 1 + m, 1 - m)
            mm(bank[0][:, 0:3 * NT], zeros[:, 0:P], zeros[:, 0:3 * NT], start=False, stop=True,
               skip_group_check=True).then_inc(s_degall, 1)

            def src_rows(i, half):
                to = bank[half][:, :]
                pick = identb[0:Q, bass.ds(i, 1)] if not isinstance(i, int) else identb[0:Q, i:i + 1]
                pick = pick.broadcast_to([Q, P])
                mm(to, pick, src_hi[0:Q, half * K * P:(half + 1) * K * P], start=True, stop=False)
                mm(to, pick, src_lo[0:Q, half * K * P:(half + 1) * K * P], start=False, stop=True).then_inc(s_row, 1)

            def mix(b, half):
                pe.wait_ge(s_same, b + 1)
                pe.wait_ge(s_placed, b + 1)
                wait_from(pe, s_mixT, b - 1)
                for j in range(K):
                    last = mm(bank[2 + half][:, j * P:(j + 1) * P], placed[:, half, j, :], same[:, half, j, :],
                              start=True, stop=True)
                last.then_inc(s_mix, 1)

            def msgs(b, n, turn):
                pe.wait_ge(s_mixT, b + 1)
                pe.wait_ge(s_window[n], 16 * K * turn)
                wait_from(pe, s_sums, b - 1)
                for j in range(K):
                    c = j % 2
                    last = mm(bank[4 + 2 * (n % 2) + j // 2][:, c * D:(c + 1) * D], mixT[:, n % 2, j, :],
                              window[:, n * K + j, :], start=True, stop=True)
                last.then_inc(s_msg, 1)

            pe.wait_ge(s_split, 1)
            pe.wait_ge(s_scaled, 1)
            pe.wait_ge(s_supout, NT)
            def pe_blocks(i):
                for n in range(S4):
                    b, q = S4 * i + n, 2 * i + n // 2
                    wait_from(pe, s_same, b - 1)
                    src_rows(q, n % 2)
                    if not isinstance(i, int) or b >= 1:
                        mix(b - 1, (n - 1) % 2)
                    if not isinstance(i, int) or b >= 2:
                        msgs(b - 2, (n - 2) % S4, i + n // 2)

            pe_blocks(0)
            with pe.Fori(1, NB // S4) as i:
                pe_blocks(i)
            mix(NB - 1, 1)
            msgs(NB - 2, S4 - 2, NB // S4)
            msgs(NB - 1, S4 - 1, NB // S4)

            pe.wait_ge(s_sums, NB)
            NP = NFULL // 2

            def turn_rows(p, s, n=2):
                pe.wait_ge(s_h, p + 1)
                for m in range(n):
                    t = 2 * p + m
                    wait_from(pe, s_hT, t - 3)
                    for c in range(DC):
                        last = nc.tensor.transpose(bank[2 * s + m][:, c * P:(c + 1) * P], hs[:, 2 * s + m, c * P:(c + 1) * P], ident[:, :])
                    last.then_inc(s_ht, 1)

            for p in range(2):
                turn_rows(p, p)
            with pe.Fori(1, NP // 2) as i:
                for s in range(2):
                    turn_rows(2 * i + s, s)
            turn_rows(NP, 0, 1)

            pe.wait_ge(s_mcol, 1)
            pe.wait_ge(s_wr, 32)
            for c in range(DC):
                last = mm(bank[5][0:1, 0:NX], mean_col[:, c:c + 1], Wr[:, c, :], start=(c == 0), stop=(c == DC - 1))
            last.then_inc(s_logit, 1)
            pe.wait_ge(s_wt, 1)
            mm(bank[4][:, 0:TOP], ones[0:1, :], rs[0:1, 10:10 + TOP], start=True, stop=True).then_inc(s_wb, 1)

            def ffn(i, n, tiles):
                pe.wait_ge(s_part, 2 * i + 2)
                for k in range(TOP * FC):
                    e, f = k // FC, k % FC
                    wait_from(pe, s_gelu, TOP * FC * i + k - 3)
                    step = 0
                    for c in range(DC):
                        for w, v in ((W1h, hTh), (W1h, hTl), (W1l, hTh)):
                            last = mm(bank[k % 4][:, 0:n], w[:, e, c, f * P:(f + 1) * P], v[:, c, 0:n],
                                      start=(step == 0), stop=(step == 3 * DC - 1))
                            step += 1
                    last.then_inc(s_ff1, 1)
                for k in range(TOP * FC):
                    pe.wait_ge(s_hidl, TOP * FC * i + k + 1)
                    for j in range(tiles):
                        if k == 0:
                            wait_from(pe, s_z, K * (i - 1) + j + 1)
                        js = slice(j * P, (j + 1) * P)
                        for step, (v, w) in enumerate(((hidh, W2h), (hidh, W2l), (hidl, W2h))):
                            last = mm(bank[4 + j][:, 0:D], v[:, k, js], w[:, k, :], start=(k == 0 and step == 0),
                                      stop=(k == TOP * FC - 1 and step == 2))
                        if k == TOP * FC - 1:
                            last.then_inc(s_ff2, 1)

            pe.wait_ge(s_W1l, TOP)
            pe.wait_ge(s_W2l, TOP)
            ffn(0, K * P, K)
            with pe.Fori(1, NFULL // K) as i:
                ffn(i, K * P, K)
            ffn(NFULL // K, P, 1)


_INS = ['x', 'src', 'dst', 'edge_weight', 'L0_gnn_W', 'L0_gnn_b', 'L0_ffn_Wr', 'L0_ffn_br', 'L0_ffn_W1', 'L0_ffn_b1',
        'L0_ffn_W2', 'L0_ffn_b2', 'L0_ffn_gamma', 'L0_ffn_beta']
_OUTS = [((6250, 256), 'float32')]


def kernel(**inputs):
    import numpy as _np
    import concourse.bacc as _bacc
    from concourse import mybir as _mybir
    from concourse.bass_utils import run_bass_kernel_spmd as _run

    nc = _bacc.Bacc("TRN2", target_bir_lowering=False, num_devices=1)
    arrays, args = {}, []
    for name in _INS:
        a = _np.ascontiguousarray(inputs[name])
        arrays[f"in_{name}_dram"] = a
        args.append(nc.dram_tensor(f"in_{name}_dram", a.shape, _mybir.dt.from_np(a.dtype), kind="ExternalInput").ap())
    for i, (shape, dtype) in enumerate(_OUTS):
        dt = _mybir.dt.from_np(_np.dtype(dtype))
        args.append(nc.dram_tensor(f"out_{i}_dram", shape, dt, kind="ExternalOutput").ap())
    gnn_ffn_kernel(nc, *args)
    r = _run(nc, [arrays], core_ids=[0])
    return r.results[0]["out_0_dram"]
```

```python
import concourse.bass as bass
from concourse import mybir
from contextlib import ExitStack



class Steps:

    def __init__(self, eng, sem):
        self.eng, self.sem, self.base, self.n = eng, sem, 0, 0

    def add(self, ins):
        ins.then_inc(self.sem, 1)
        self.n += 1
        return ins

    def wait(self, n=None):
        self.eng.wait_ge(self.sem, self.base + (self.n if n is None else n))

    def link(self, ins):
        self.add(ins)
        self.wait()

    def at(self, base):
        self.base, self.n = base, 0


def wait_from(eng, sem, value):
    if isinstance(value, int) and value <= 0:
        return
    eng.wait_ge(sem, value)


def gnn_ffn_kernel(nc, x_d, src_d, dst_d, ew_d, W_d, b_d, Wr_d, br_d, W1_d, b1_d, W2_d, b2_d, gamma_d, beta_d, out_d):
    fp32 = mybir.dt.float32
    bf16 = mybir.dt.bfloat16
    fp32r = mybir.dt.float32r
    i32 = mybir.dt.int32
    ALU = mybir.AluOpType
    ACT = mybir.ActivationFunctionType
    AX = mybir.AxisListType.X

    P = 128
    N, D = x_d.shape
    E = src_d.shape[0]
    NX, _, F = W1_d.shape
    TOP = 2
    EPS = 1e-5
    DC, FC = D // P, F // P
    NT = -(-N // P)
    NFULL = N // P
    TAIL = N - NFULL * P
    G = 8
    Q = -(-E // (G * P))
    QFULL = E // (G * P)
    EREST = E - QFULL * G * P
    EPAD = G * P - EREST
    K = 4
    NB = Q * G // K
    DUMMY = NT * P
    ROWS = DUMMY + P
    PADSRC = DUMMY - 1
    CAP = float(-(-N * 125 // (100 * NX)))
    S4 = 4
    XCH = 7
    CT = NT // XCH

    table_d = nc.dram_tensor("table_d", [N, D], fp32, kind="Internal").ap()
    sums_d = [nc.dram_tensor(f"sums{k}_d", [ROWS, D], fp32, kind="Internal").ap() for k in range(K)]
    starts_d = nc.dram_tensor("starts_d", [Q, G // K], i32, kind="Internal").ap()

    with ExitStack() as ctx:
        def sb(name, shape, dt=fp32):
            return ctx.enter_context(nc.sbuf_tensor(name, shape, dt))

        def sem(name):
            return ctx.enter_context(nc.semaphore(name))

        x = sb("x", [P, NT, D])
        hT = sb("hT", [P, DC, NT * P])
        edge = sb("edge", [P, 4, G, Q])
        src_hi = sb("src_hi", [P, G * P], bf16)
        src_lo = sb("src_lo", [P, G * P], bf16)
        ident = sb("ident", [P, P])
        identb = sb("identb", [P, P], bf16)
        ones = sb("ones", [P, P])
        iota = sb("iota", [P, P])
        before = sb("before", [P, P])
        dummyc = sb("dummyc", [P, 1])
        W = sb("W", [P, DC, D])
        b_row = sb("b_row", [1, D])
        gamma = sb("gamma", [P, D])
        beta = sb("beta", [P, D])
        b2c = sb("b2c", [P, D])
        Wr = sb("Wr", [P, DC, NX])
        dis = sb("dis", [P, NT])
        stats = sb("stats", [P, 8, 6])
        mv = sb("mv", [P, 8, 2])
        var = sb("var", [P, 8, 1])
        rstd = sb("rstd", [P, 8, 1])
        shiftm = sb("shiftm", [P, 8, 1])
        rowstat = sb("rowstat", [P, NT, 2])
        eps = sb("eps", [P, 1])
        half_power = sb("half_power", [P, NT])
        same_before = sb("same_before", [P, 2, K])
        shift = sb("shift", [P, 2, K])
        rows_to = sb("rows_to", [P, S4, K], i32)
        rows_of = sb("rows_of", [P, S4, K], i32)
        nat = sb("nat", [P, 4, G // K])
        starts_i = sb("starts_i", [P, G // K], i32)
        far = sb("far", [P, 2])
        flag_i = sb("flag_i", [P, 1], i32)
        colsum = sb("colsum", [P, DC, NT + 1])
        mean_col = sb("mean_col", [P, DC])
        rt = sb("rt", [1, 24, NX])
        rs = sb("rs", [1, 16])
        pick_i = sb("pick_i", [1, TOP], i32)
        wtop = sb("wtop", [P, TOP])
        b1s = sb("b1s", [P, TOP, FC])

        with ExitStack() as early:
            arena = early.enter_context(nc.sbuf_tensor("arena", [P, 8192], fp32))
            h = early.enter_context(nc.sbuf_tensor("h", [P, NT, D], fp32))
        W1h = sb("W1h", [P, TOP, DC, F], fp32r)
        W1l = sb("W1l", [P, TOP, DC, F], fp32r)
        W2h = sb("W2h", [P, TOP * FC, D], fp32r)
        W2l = sb("W2l", [P, TOP * FC, D], fp32r)
        hid = sb("hid", [P, 4, K * P])
        hidh = sb("hidh", [P, TOP * FC, K * P], fp32r)
        hidl = sb("hidl", [P, TOP * FC, K * P], fp32r)
        hTh = sb("hTh", [P, DC, K * P], fp32r)
        hTl = sb("hTl", [P, DC, K * P], fp32r)

        def part(t, at, shape, dt=fp32):
            n = 1
            for s in shape:
                n *= s
            if dt == bf16:
                n = (n + 1) // 2
            v = t[:, at:at + n]
            if dt != fp32:
                v = v.bitcast(dt)
            if len(shape) == 2:
                v = v.rearrange("p (a b) -> p a b", b=shape[1])
            if len(shape) == 3:
                v = v.rearrange("p (a b c) -> p a b c", b=shape[1], c=shape[2])
            return v

        scratch = hT[:, :, :].rearrange("p c n -> p (c n)")
        GP = G * P
        src_i = part(arena, 0, [GP], i32)
        dst_i = part(arena, GP, [GP], i32)
        w_n = part(arena, 2 * GP, [GP])
        src_n = part(arena, 3 * GP, [GP])
        dst_n = part(arena, 4 * GP, [GP])
        place_n = part(arena, 5 * GP, [GP])
        tmp_i = part(arena, 6 * GP, [GP], i32)
        tmp_n = part(arena, 7 * GP, [GP])
        dstT = part(scratch, 0, [G, Q])
        G2 = 2 * G
        assert Q == 2 * NT
        dst_hi = part(scratch, GP, [NT, G2], bf16)
        dst_lo = part(scratch, GP + GP // 2, [NT, G2], bf16)
        w3 = part(scratch, 2 * GP, [3, NT, G2], bf16)
        rest = part(scratch, 4 * GP, [G, Q])
        tmpT_i = part(scratch, 5 * GP, [G, Q], i32)
        tmpT2_i = part(scratch, 6 * GP, [G, Q], i32)
        ln = part(scratch, 8 * GP, [D])
        lnT = part(scratch, 8 * GP + D, [DC, P])
        unread = part(scratch, 8 * GP + 2 * D, [D])
        ZCH = 10
        zeros = part(scratch, 9 * GP, [ROWS * D // P // ZCH])
        starts = part(scratch, 9 * GP + ROWS * D // P // ZCH, [NB], i32)
        iota16 = part(arena, 0, [P, G2], bf16)
        oh_lo = [part(arena, GP * (1 + n), [P, G2], bf16) for n in range(2)]
        oh_hi = [part(arena, 3 * GP + 512 * n, [NT, G2], bf16) for n in range(2)]
        oh_w = [part(arena, 4 * GP + 1280 * n, [3, NT, G2], bf16) for n in range(2)]
        window = part(arena, 0, [S4 * K, D])
        sums = part(arena, S4 * K * D, [S4 * K, D])
        same = part(scratch, 5 * GP, [2, K, P])
        placed = part(scratch, 6 * GP, [2, K, P])
        mixT = part(scratch, 7 * GP, [2, K, P])
        junk = part(scratch, 8 * GP, [2 * K, P])
        SL = 4
        back = part(arena, 0, [SL * K, 2 * D])
        flat = edge[:, :, :, :].rearrange("p a g q -> p (a g q)")
        hs = part(flat, 0, [4, D])
        z = part(flat, 0, [K, D])
        zg = part(flat, K * D, [K, D])
        y = part(flat, 2 * K * D, [K, D])
        b2s = part(flat, 2 * K * D, [TOP, D])
        W1raw = hid[:, :, :]
        W2raw = part(flat, 0, [TOP * FC, D])

        srcT, placeT, wT, shiftT = (edge[:, n, :, :] for n in range(4))
        by_g = lambda v: v.rearrange("p t (u g) -> p g (t u)", g=G)
        as_tiles = lambda v: v.rearrange("p (g j) -> p g j", j=P)
        as_blocks = lambda v: v.rearrange("p (u j) -> p u j", j=K * P)

        bank = [ctx.enter_context(nc.psum_tensor(f"bank{n}", [P, 512], fp32)) for n in range(8)]

        s_pad = sem("s_pad")
        s_src, s_dst, s_ew = sem("s_src"), sem("s_dst"), sem("s_ew")
        s_x0, s_x, s_W, s_wr, s_gb = sem("s_x0"), sem("s_x"), sem("s_W"), sem("s_wr"), sem("s_gb")
        s_const = sem("s_const")
        s_zero = sem("s_zero")
        s_cleared = sem("s_cleared")
        s_dve = sem("s_dve")
        s_var, s_root = sem("s_var"), sem("s_root")
        s_dis = sem("s_dis")
        s_nat = sem("s_nat")
        s_starts, s_starts_d, s_starts_r = sem("s_starts"), sem("s_starts_d"), sem("s_starts_r")
        s_far, s_farall, s_flag = sem("s_far"), sem("s_farall"), sem("s_flag")
        s_turn = sem("s_turn")
        s_turned = sem("s_turned")
        s_split = sem("s_split")
        s_w3, s_rest = sem("s_w3"), sem("s_rest")
        s_ln, s_lnt, s_lnT = sem("s_ln"), sem("s_lnt"), sem("s_lnT")
        s_sup, s_supout = sem("s_sup"), sem("s_supout")
        s_mom = sem("s_mom")
        s_nb = sem("s_nb")
        s_hi, s_oh, s_ohp, s_deg = sem("s_hi"), sem("s_oh"), sem("s_ohp"), sem("s_deg")
        s_degall = sem("s_degall")
        s_scaled, s_table = sem("s_scaled"), sem("s_table")
        s_row = sem("s_row")
        s_same = sem("s_same")
        s_placed = sem("s_placed")
        s_dup, s_sh, s_to = sem("s_dup"), sem("s_sh"), sem("s_to")
        s_own = sem("s_own")
        s_of = sem("s_of")
        s_mix, s_mixT = sem("s_mix"), sem("s_mixT")
        s_window = [sem(f"s_window{n}") for n in range(S4)]
        s_msg = sem("s_msg")
        s_sums = sem("s_sums")
        s_go = sem("s_go")
        s_tick = sem("s_tick")
        s_tock = sem("s_tock")
        s_scat = [sem(f"s_scat{n}") for n in range(K)]
        s_back = [sem(f"s_back{n}") for n in range(SL)]
        s_pair = sem("s_pair")
        s_used = sem("s_used")
        s_h, s_ht, s_hT = sem("s_h"), sem("s_ht"), sem("s_hT")
        s_mcol, s_logit, s_e, s_pick, s_wt, s_wb, s_lg = (
            sem(n) for n in ("s_mcol", "s_logit", "s_e", "s_pick", "s_wt", "s_wb", "s_lg"))
        s_w1, s_w2 = ([sem(f"{n}_{e}") for e in range(TOP)] for n in ("s_w1", "s_w2"))
        s_b12, s_b2c, s_wtop = sem("s_b12"), sem("s_b2c"), sem("s_wtop")
        s_W1h, s_W1l, s_W2h, s_W2l = sem("s_W1h"), sem("s_W1l"), sem("s_W2h"), sem("s_W2l")
        s_part = sem("s_part")
        s_ff1, s_gelu, s_hidh, s_hidl, s_ff2 = (sem(n) for n in ("s_ff1", "s_gelu", "s_hidh", "s_hidl", "s_ff2"))
        s_res, s_hb = sem("s_res"), sem("s_hb")
        s_z, s_zn, s_zg, s_zx, s_y = sem("s_z"), sem("s_zn"), sem("s_zg"), sem("s_zx"), sem("s_y")
        s_last = sem("s_last")
        s_out = sem("s_out")
        s_cons = 9

        def tiles_of_x(eng, step, all_of_x=False):
            assert (NT - 5) % 4 == 0 and CT >= 5
            for t in range(3):
                step(t, t)
            if all_of_x:
                eng.wait_ge(s_x, 16 * XCH)
            with eng.Fori(0, (NT - 5) // 4) as i:
                for m in range(4):
                    step(4 * i + 3 + m, (3 + m) % 4)
            for t in range(NT - 2, NT):
                step(t, t % 4)

        block = ctx.enter_context(nc.Block())

        x_v = x_d[0:NFULL * P, :].rearrange("(t p) d -> p t d", p=P)
        table_v = table_d[0:NFULL * P, :].rearrange("(t p) d -> p t d", p=P)

        @block.sync
        def _(sp):
            for d, v, s in ((dst_d, dst_i, s_dst), (src_d, src_i, s_src), (ew_d, w_n, s_ew)):
                if s is s_src:
                    sp.wait_ge(s_pad, 2)
                sp.dma_start(v[0:QFULL, :], d[0:QFULL * GP].rearrange("(q c) -> q c", c=GP)).then_inc(s, 16)
                sp.dma_start(v[QFULL:Q, 0:EREST], d[QFULL * GP:E].rearrange("(q c) -> q c", q=1)).then_inc(s, 16)
                if s is s_dst:
                    sp.dma_start(dst_i[QFULL:Q, EREST:GP], dst_d[E - EPAD:E].rearrange("(q c) -> q c", q=1)).then_inc(s, 16)
            for c in range(1, XCH):
                last = min((c + 1) * CT, NFULL)
                sp.dma_start(x[:, c * CT:last, :], x_v[:, c * CT:last, :]).then_inc(s_x, 16)
            sp.wait_ge(s_const, 1)
            sp.dma_start(x[0:TAIL, NFULL, :], x_d[NFULL * P:N, :]).then_inc(s_x, 16)
            sp.wait_ge(s_x, 16 * XCH)
            sp.wait_ge(s_zero, 1)
            for k in range(K):
                v = sums_d[k].rearrange("(p r) d -> p (r d)", p=P)
                n = ROWS * D // P // ZCH
                for c in range(ZCH):
                    sp.dma_start(v[:, c * n:(c + 1) * n], zeros).then_inc(s_cleared, 16)
            sp.wait_ge(s_starts, 1)
            sp.dma_start(starts_d, starts_i[0:Q, :]).then_inc(s_starts_d, 16)
            sp.wait_ge(s_starts_d, 16)
            sp.dma_start(starts[0:1, :], starts_d.rearrange("(o q) g -> o (q g)", o=1)).then_inc(s_starts_r, 16)
            for c in range(XCH):
                sp.wait_ge(s_scaled, c + 1)
                last = min((c + 1) * CT, NFULL)
                sp.dma_start(table_v[:, c * CT:last, :], h[:, c * CT:last, :]).then_inc(s_table, 16)
            sp.dma_start(table_d[NFULL * P:N, :], h[0:TAIL, NFULL, :]).then_inc(s_table, 16)
            sp.wait_ge(s_table, 16 * (XCH + 1))
            sp.wait_ge(s_starts_r, 16)
            sp.wait_ge(s_flag, 1)
            sp.wait_ge(s_degall, 1)

            def windows(i):
                _, starts_of = nc.values_load_multi_w_load_instructions(starts[0:1, bass.ds(i * S4, S4)],
                                                                        engines=(mybir.EngineType.SP,), min_val=0, max_val=N - P)
                for n, at in enumerate(starts_of):
                    wait_from(sp, s_msg, S4 * (i - 1) + n + 1)
                    sp.dma_start(window[:, n * K, :], table_d[bass.ds(at, P), :]).then_inc(s_window[n], 16)

            gathers = sp.value_load(flag_i[0:1, 0:1], min_val=0, max_val=1)
            with sp.If(gathers < 1):
                windows(0)
                with sp.Fori(1, NB // S4) as i:
                    windows(i)

            for k in range(K):
                sp.wait_ge(s_scat[k], 16 * NB)

            def read_back(p, slot, n=2):
                for k in range(K):
                    v = sums_d[k][bass.ds(p * (2 * P), n * P), :] if not isinstance(p, int) else sums_d[k][p * 2 * P:(p * 2 + n) * P, :]
                    sp.dma_start(back[:, slot * K + k, 0:n * D].rearrange("p (j d) -> p j d", d=D),
                                 v.rearrange("(j p) d -> p j d", p=P)).then_inc(s_back[slot], 16)

            for slot in range(SL):
                read_back(slot, slot)
            with sp.Fori(1, NFULL // 2 // SL) as i:
                for slot in range(SL):
                    sp.wait_ge(s_used, SL * (i - 1) + slot + 1)
                    read_back(SL * i + slot, slot)
            sp.wait_ge(s_used, NFULL // 2 - SL + 1)
            read_back(NFULL // 2, 0, 1)

            sp.wait_ge(s_pick, 1)
            picks = [sp.value_load(pick_i[0:1, e:e + 1], min_val=0, max_val=NX - 1) for e in range(TOP)]
            for e, pick in enumerate(picks):
                sp.dma_start(W1raw[:, e * DC:(e + 1) * DC, :], W1_d[bass.ds(pick, 1), :, :].rearrange("o (c p) f -> p (o c) f", p=P)).then_inc(s_w1[e], 16)
            for e, pick in enumerate(picks):
                sp.dma_start(W2raw[:, e * FC:(e + 1) * FC, :], W2_d[bass.ds(pick, 1), :, :].rearrange("o (c p) n -> p (o c) n", p=P)).then_inc(s_w2[e], 16)
                with nc.allow_non_contiguous_dma(reason="a column of 512 biases"):
                    sp.dma_start(b1s[:, e, :], b1_d[bass.ds(pick, 1), :].rearrange("o (c p) -> p (o c)", p=P)).then_inc(s_b12, 16)
                sp.dma_start(b2s[:, e, :], b2_d[bass.ds(pick, 1), :].broadcast_to([P, D])).then_inc(s_b12, 16)

            with sp.Fori(0, NFULL // K) as i:
                sp.wait_ge(s_y, K * i + K)
                sp.dma_start(out_d[bass.ds(i * (K * P), K * P), :].rearrange("(t p) d -> p t d", p=P), y).then_inc(s_out, 16)
            sp.wait_ge(s_last, 4)
            sp.dma_start(out_d[NFULL * P:N, :], z[0:TAIL, 0, :]).then_inc(s_out, 16)
            sp.wait_ge(s_out, 16 * (NFULL // K + 1))

        @block.gpsimd
        def _(pool):
            nc.gpsimd.memset(src_i, PADSRC).then_inc(s_pad, 1)
            nc.gpsimd.memset(w_n, 0.0).then_inc(s_pad, 1)
            nc.gpsimd.memset(x[:, NFULL, :], 0.0).then_inc(s_const, 1)
            nc.gpsimd.iota(iota[:, :], [[1, P]], base=0, channel_multiplier=0,
                           allow_small_or_imprecise_dtypes=True).then_inc(s_const, 1)
            nc.gpsimd.memset(colsum[:, :, NT:NT + 1], 0.0)
            nc.gpsimd.iota(dummyc[:, :], [[0, 1]], base=DUMMY, channel_multiplier=1,
                           allow_small_or_imprecise_dtypes=True).then_inc(s_const, 1)
            nc.gpsimd.memset(eps[:, :], EPS)
            nc.gpsimd.memset(ones[:, :], 1.0).then_inc(s_const, 1)
            nc.gpsimd.memset(half_power[:, :], -0.5).then_inc(s_const, 1)
            nc.gpsimd.memset(ident[:, :], 0.0).then_inc(s_const, 1)
            pool.wait_ge(s_const, 6)
            nc.gpsimd.affine_select(out=ident[:, :], in_=ident[:, :], compare_op=ALU.not_equal, fill=1.0, base=0,
                                    pattern=[[-1, P]], channel_multiplier=1).then_inc(s_const, 1)
            nc.gpsimd.affine_select(out=before[:, :], in_=ones[:, :], compare_op=ALU.is_gt, fill=0.0, base=0,
                                    pattern=[[-1, P]], channel_multiplier=1).then_inc(s_const, 1)
            pool.wait_ge(s_const, 8)
            nc.gpsimd.tensor_copy(identb[:, :], ident[:, :]).then_inc(s_const, 1)
            nc.gpsimd.memset(zeros, 0.0).then_inc(s_zero, 1)
            pool.wait_ge(s_nat, 2)
            nc.gpsimd.iota(iota16, [[1, P], [0, G2]], base=0, channel_multiplier=0,
                           allow_small_or_imprecise_dtypes=True).then_inc(s_zero, 1)
            pool.wait_ge(s_w3, 1)
            nc.gpsimd.tensor_tensor(rest, wT, by_g(w3[:, 0, :, :]), ALU.subtract).then_inc(s_rest, 1)
            pool.wait_ge(s_split, 1)
            nc.gpsimd.tensor_tensor(src_lo[0:Q, :], src_n[0:Q, :], src_hi[0:Q, :], ALU.subtract).then_inc(s_split, 1)

            def root(n, m=1):
                nc.gpsimd.tensor_tensor(rstd[:, n:n + m, :], var[:, n:n + m, :],
                                        half_power[:, 0:m].unsqueeze(2), ALU.pow).then_inc(s_root, 1)

            def pool_root(t, m):
                pool.wait_ge(s_var, t + 1)
                wait_from(pool, s_ln, t - 3)
                root(m)

            def pool_rows(t, m):
                if not isinstance(t, int) or t + 1 < NT:
                    pool_root(t + 1, (m + 1) % 4)
                pool.wait_ge(s_hi, t + 1)
                wait_from(pool, s_deg, t - 1)
                tt = bass.ds(t, 1) if not isinstance(t, int) else slice(t, t + 1)
                nc.gpsimd.tensor_tensor(oh_w[m % 2][:, 2, :, :], oh_hi[m % 2], w3[:, 2, tt, :].broadcast_to([P, NT, G2]),
                                        ALU.mult).then_inc(s_ohp, 1)

            pool_root(0, 0)
            pool.wait_ge(s_w3, 3)
            tiles_of_x(pool, pool_rows)
            pool.wait_ge(s_dis, 1)
            for c in range(XCH):
                v = dis[:, c * CT:(c + 1) * CT]
                nc.gpsimd.tensor_tensor(v, v, half_power[:, 0:CT], ALU.pow).then_inc(s_dis, 1)

            pool.wait_ge(s_cleared, 16 * ZCH * K)
            pool.wait_ge(s_flag, 1)

            def scatter(b, n):
                pool.wait_ge(s_sums, b + 1)
                pool.wait_ge(s_to, b + 1)
                for j in range(K):
                    wait_from(pool, s_scat[j], 16 * b)
                    if not isinstance(b, int):
                        pool.sem_inc(s_go, 1)
                    pool.indirect_dma_start(
                        out=sums_d[j], out_offset=bass.IndirectOffsetOnAxis(ap=rows_to[:, n, j:j + 1], axis=0),
                        in_=sums[:, n * K + j, :], in_offset=None, compute_op=ALU.add).then_inc(s_scat[j], 16)

            def gather(b, n):
                pool.wait_ge(s_of, b + 1)
                wait_from(pool, s_msg, b - S4 + 1)
                if not isinstance(b, int):
                    pool.sem_inc(s_go, 1)
                for j in range(K):
                    pool.indirect_dma_start(
                        out=window[:, n * K + j, :], out_offset=None, in_=table_d,
                        in_offset=bass.IndirectOffsetOnAxis(ap=rows_of[:, n, j:j + 1], axis=0)).then_inc(s_window[n], 16)

            gathers = pool.value_load(flag_i[0:1, 0:1], min_val=0, max_val=1)
            with pool.If(gathers < 1):
                for n in range(S4):
                    scatter(n, n)
                with pool.Fori(1, NB // S4) as i:
                    for n in range(S4):
                        scatter(S4 * i + n, n)
            with pool.Else():
                pool.wait_ge(s_table, 16 * (XCH + 1))
                for n in range(S4):
                    gather(n, n)
                    scatter(n, n)
                with pool.Fori(1, NB // S4) as i:
                    for n in range(S4):
                        gather(S4 * i + n, n)
                        scatter(S4 * i + n, n)

            NP = NFULL // 2

            def pair(slot, turn, n=2):
                pool.wait_ge(s_back[slot], 16 * K * turn)
                a = back[:, slot * K:slot * K + 2, 0:n * D]
                nc.gpsimd.tensor_tensor(a, a, back[:, slot * K + 2:slot * K + 4, 0:n * D], ALU.add).then_inc(s_pair, 1)

            def root_rows(p, s, n=2):
                pool.wait_ge(s_var, NT + p + 1)
                wait_from(pool, s_h, p - 1)
                root(2 * s, n)

            assert NP % SL == 0
            for p in range(2):
                pair(p, 1)
            for p in range(SL):
                pair((p + 2) % SL, (p + 2) // SL + 1)
                root_rows(p, p % 2)
            with pool.Fori(1, NP // SL - 1) as i:
                for m in range(SL):
                    pair((m + 2) % SL, i + (m + 2) // SL + 1)
                    root_rows(SL * i + m, m % 2)
            for p in range(NP - SL, NP - 1):
                pair((p + 2) % SL, (p + 2) // SL + 1, 1 if p + 2 == NP else 2)
                root_rows(p, p % 2)
            root_rows(NP - 1, (NP - 1) % 2)
            root_rows(NP, NP % 2, 1)

            pool.wait_ge(s_b2c, 1)
            pool.wait_ge(s_gb, 32)

            def residual(t, j):
                pool.wait_ge(s_res, t + 1)
                nc.gpsimd.tensor_tensor(z[:, j, :], z[:, j, :], b2c[:, :], ALU.add).then_inc(s_hb, 1)

            def scaled(t, j, i):
                tt = slice(t, t + 1) if isinstance(t, int) else bass.ds(t, 1)
                pool.wait_ge(s_zn, t + 1)
                nc.gpsimd.tensor_tensor(zg[:, j, :], z[:, j, :], gamma[:, :], ALU.mult).then_inc(s_zg, 1)
                pool.wait_ge(s_zg, t + 1)
                pool.sem_inc(s_go, 1)
                nc.gpsimd.tensor_tensor(zg[:, j:j + 1, :], zg[:, j:j + 1, :], x[:, tt, :], ALU.add).then_inc(s_zx, 1)
                pool.wait_ge(s_zx, t + 1)
                wait_from(pool, s_out, 16 * i)
                nc.gpsimd.tensor_tensor(y[:, j, :], zg[:, j, :], beta[:, :], ALU.add).then_inc(s_y, 1)

            def pool_group(i, tiles):
                for j in range(tiles):
                    residual(K * i + j, j)
                pool.wait_ge(s_var, NT + NP + 1 + i + 1)
                root(4, tiles)
                for j in range(tiles):
                    scaled(K * i + j, j, i)

            pool_group(0, K)
            with pool.Fori(1, NFULL // K) as i:
                pool_group(i, K)
            pool.wait_ge(s_var, NT + NP + 1 + NFULL // K + 1)
            root(4)

        @block.scalar
        def _(act):
            act.wait_ge(s_pad, 2)
            act.dma_start(x[:, 0:CT, :], x_v[:, 0:CT, :]).then_inc(s_x0, 16)
            act.wait_ge(s_dst, 48)
            nc.scalar.copy(dst_n[0:Q, :], dst_i[0:Q, :]).then_inc(s_nat, 1)
            act.dma_start(W[:, :, :], W_d.rearrange("(c p) n -> p c n", p=P)).then_inc(s_W, 16)
            act.dma_start(b_row[0:1, :], b_d.rearrange("(o n) -> o n", o=1)).then_inc(s_W, 16)
            act.wait_ge(s_src, 32)
            nc.scalar.copy(src_n[0:Q, :], src_i[0:Q, :]).then_inc(s_nat, 1)

            for n, to in enumerate((dstT, wT, srcT, placeT)):
                for half in range(2):
                    act.wait_ge(s_turn, 2 * n + half + 1)
                    nc.scalar.copy(to[:, half * K:(half + 1) * K, :],
                                   bank[2 * (n % 2) + half][:, 0:K * Q].rearrange("p (g q) -> p g q", q=Q)).then_inc(s_turned, 1)
                if n == 1:
                    act.wait_ge(s_turned, 4)
                    nc.scalar.copy(by_g(w3[:, 0, :, :]), wT).then_inc(s_w3, 1)
                    act.wait_ge(s_nat, 2)
                    nc.scalar.copy(src_hi[0:Q, :], src_n[0:Q, :]).then_inc(s_split, 1)
                if n == 2:
                    act.wait_ge(s_rest, 1)
                    nc.scalar.copy(by_g(w3[:, 1, :, :]), rest).then_inc(s_w3, 1)
            act.dma_start(Wr[:, :, :], Wr_d.rearrange("(c p) n -> p c n", p=P)).then_inc(s_wr, 16)
            act.dma_start(rt[0:1, 0, :], br_d.rearrange("(o n) -> o n", o=1)).then_inc(s_wr, 16)
            act.dma_start(gamma[:, :], gamma_d.rearrange("(o n) -> o n", o=1).broadcast_to([P, D])).then_inc(s_gb, 16)
            act.dma_start(beta[:, :], beta_d.rearrange("(o n) -> o n", o=1).broadcast_to([P, D])).then_inc(s_gb, 16)

            def xs(t):
                return x[:, slice(t, t + 1) if isinstance(t, int) else bass.ds(t, 1), :]

            def row_sum(t, m):
                nc.scalar.activation(unread.unsqueeze(1), xs(t), ACT.Copy, accum_out=stats[:, m, 0:1]).then_inc(s_mom, 1)

            def row_mean(t, m):
                act.wait_ge(s_mom, 3 * t + 1)
                nc.scalar.activation(mv[:, m, 0:1], stats[:, m, 0:1], ACT.Copy, scale=-1.0 / D).then_inc(s_mom, 1)

            def row_squares(t, m):
                act.wait_ge(s_mom, 3 * t + 2)
                act.sem_inc(s_tock, 1)
                nc.scalar.activation(unread.unsqueeze(1), xs(t), ACT.Square, bias=mv[:, m, 0:1],
                                     accum_out=stats[:, m, 1:2]).then_inc(s_mom, 1)

            def row_var(t, m):
                act.wait_ge(s_mom, 3 * t + 3)
                nc.scalar.activation(var[:, m, :], stats[:, m, 1:2], ACT.Identity, scale=1.0 / D, bias=eps[:, :]).then_inc(s_var, 1)

            def row_shift(t, m):
                act.wait_ge(s_root, t + 1)
                nc.scalar.activation(shiftm[:, m, :], mv[:, m, 0:1], ACT.Copy, scale=rstd[:, m, :]).then_inc(s_nb, 1)

            def support_out(t):
                tt = slice(t, t + 1) if isinstance(t, int) else bass.ds(t, 1)
                act.wait_ge(s_sup, t + 1)
                nc.scalar.copy(h[:, tt, :], bank[2][:, None, 0:D]).then_inc(s_supout, 1)

            def act_rows(t, m):
                ahead = not isinstance(t, int) or t + 2 < NT
                m2 = (m + 2) % 4
                act.wait_ge(s_nb, t + 1)
                wait_from(act, s_lnt, t)
                act.sem_inc(s_tock, 1)
                nc.scalar.activation(ln.unsqueeze(1), xs(t), ACT.Identity, bias=shiftm[:, m, :], scale=rstd[:, m, :]).then_inc(s_ln, 1)
                if ahead:
                    row_sum(t + 2, m2)
                if not isinstance(t, int) or t >= 1:
                    support_out(t - 1)
                if ahead:
                    row_mean(t + 2, m2)
                act.wait_ge(s_lnt, t + 1)
                nc.scalar.copy(lnT, bank[1][:, 0:D].rearrange("p (c n) -> p c n", n=P)).then_inc(s_lnT, 1)
                if ahead:
                    row_squares(t + 2, m2)
                if not isinstance(t, int) or t + 1 < NT:
                    row_shift(t + 1, (m + 1) % 4)
                if ahead:
                    row_var(t + 2, m2)

            act.wait_ge(s_x0, 16)
            act.wait_ge(s_const, s_cons)
            for t in range(2):
                for f in (row_sum, row_mean, row_squares, row_var):
                    f(t, t)
            row_shift(0, 0)
            tiles_of_x(act, act_rows, all_of_x=True)
            support_out(NT - 1)

            def mix_out(i, n):
                b, q, half, m = S4 * i + n, 2 * i + n // 2, n % 2, n % 2
                ks = slice(half * K, (half + 1) * K)
                qq = slice(q, q + 1) if isinstance(q, int) else bass.ds(q, 1)
                wait_from(act, s_msg, S4 * (i - 1) + n + 1)
                nc.scalar.copy(rows_of[:, n, :].unsqueeze(2), dstT[:, ks, qq]).then_inc(s_of, 1)
                act.wait_ge(s_mix, b + 1)
                wait_from(act, s_msg, b - 1)
                nc.scalar.copy(mixT[:, m, :, :], bank[2 + m][:, :].rearrange("p (k n) -> p k n", n=P)).then_inc(s_mixT, 1)

            def sums_out(b, n):
                act.wait_ge(s_msg, b + 1)
                for k in range(K):
                    wait_from(act, s_scat[k], 16 * (b - S4 + 1))
                for c in range(2):
                    last = nc.scalar.copy(sums[:, n * K + 2 * c:n * K + 2 * c + 2, :],
                                          bank[4 + 2 * (n % 2) + c][:, :].rearrange("p (k n) -> p k n", n=D))
                last.then_inc(s_sums, 1)

            def act_blocks(i):
                for n in range(S4):
                    mix_out(i, n)
                    if not isinstance(i, int) or S4 * i + n >= 1:
                        sums_out(S4 * i + n - 1, (n - 1) % S4)

            act.wait_ge(s_degall, 1)
            act.wait_ge(s_table, 16 * (XCH + 1))
            act.wait_ge(s_cleared, 16 * ZCH * K)
            act_blocks(0)
            act_blocks(1)
            with act.Fori(2, NB // S4) as i:
                act_blocks(i)
            sums_out(NB - 1, S4 - 1)

            for k in range(K):
                act.wait_ge(s_scat[k], 16 * NB)

            def row_norm(p, s, n=2):
                for m in range(n):
                    t = 2 * p + m
                    tt = slice(t, t + 1) if isinstance(t, int) else bass.ds(t, 1)
                    if m == 0:
                        act.wait_ge(s_nb, NT + p + 1)
                        wait_from(act, s_ht, 2 * p - 2)
                    last = nc.scalar.activation(hs[:, 2 * s + m:2 * s + m + 1, :], x[:, tt, :], ACT.Identity,
                                                bias=shiftm[:, 2 * s + m, :], scale=rstd[:, 2 * s + m, :])
                last.then_inc(s_h, 1)

            def row_out(t, s, n=P):
                at = t * P
                act.wait_ge(s_ht, t + 1)
                for c in range(DC):
                    last = nc.scalar.activation(hT[:, c, at:at + n] if isinstance(t, int) else hT[:, c, bass.ds(at, n)],
                                                bank[s][:, c * P:c * P + n], ACT.Copy,
                                                accum_out=colsum[:, c, t:t + 1] if isinstance(t, int) else colsum[:, c, bass.ds(t, 1)])
                if n < P:
                    for c in range(DC):
                        last = nc.scalar.copy(hT[:, c, at + n:at + P], bank[s][:, c * P + n:(c + 1) * P])
                last.then_inc(s_hT, 1)

            def row_pairs(p, s):
                row_norm(p, s)
                if not isinstance(p, int) or p >= 1:
                    for m in range(2):
                        row_out(2 * (p - 1) + m, 2 * (1 - s) + m)

            NP = NFULL // 2
            for p in range(2):
                row_pairs(p, p % 2)
            with act.Fori(1, NP // 2) as i:
                for s in range(2):
                    row_pairs(2 * i + s, s)
            row_norm(NP, 0, 1)
            for m in range(2):
                row_out(NFULL - 2 + m, 2 + m)
            row_out(NFULL, 0, TAIL)

            for n in range(3):
                act.wait_ge(s_lg, n + 1)
                w = NX if n < 2 else TOP
                nc.scalar.activation(rt[0:1, 20 + n, 0:w], rt[0:1, 16 + n, 0:w], ACT.Exp).then_inc(s_e, 1)

            for e in range(TOP):
                act.wait_ge(s_w1[e], 16)
                for c in range(DC):
                    nc.scalar.copy(W1h[:, e, c, :], W1raw[:, e * DC + c, :]).then_inc(s_W1h, 1)
            act.wait_ge(s_wtop, 1)
            for e in range(TOP):
                act.wait_ge(s_w2[e], 16)
                nc.scalar.activation(W2h[:, e * FC:(e + 1) * FC, :], W2raw[:, e * FC:(e + 1) * FC, :], ACT.Copy,
                                     scale=wtop[:, e:e + 1]).then_inc(s_W2h, 1)

            act.wait_ge(s_b12, 64)
            act.wait_ge(s_W1l, TOP)

            def gelu(i, n):
                for k in range(TOP * FC):
                    c = TOP * FC * i + k
                    act.wait_ge(s_ff1, c + 1)
                    wait_from(act, s_hidl, c - 3)
                    nc.scalar.activation(hid[:, k % 4, 0:n], bank[k % 4][:, 0:n], ACT.Gelu,
                                         bias=b1s[:, k // FC, k % FC:k % FC + 1]).then_inc(s_gelu, 1)
                    act.wait_ge(s_gelu, c + 1)
                    if k == 0:
                        wait_from(act, s_ff2, K * i)
                    nc.scalar.copy(hidh[:, k, 0:n], hid[:, k % 4, 0:n]).then_inc(s_hidh, 1)

            gelu(0, K * P)
            with act.Fori(1, NFULL // K) as i:
                gelu(i, K * P)
            gelu(NFULL // K, P)

        @block.vector
        def _(dve):
            me = Steps(dve, s_dve)

            dve.wait_ge(s_nat, 1)
            least, most, start, toofar = (nat[0:Q, n, :] for n in range(4))
            nc.vector.tensor_reduce(least, as_blocks(dst_n[0:Q, :]), AX, ALU.min)
            me.link(nc.vector.tensor_reduce(most, as_blocks(dst_n[0:Q, :]), AX, ALU.max))
            me.link(nc.vector.tensor_scalar(start, least, float(N - P), None, ALU.min))
            nc.vector.tensor_copy(starts_i[0:Q, :], start).then_inc(s_starts, 1)
            me.link(nc.vector.tensor_tensor(toofar, most, start, ALU.subtract))
            me.link(nc.vector.tensor_scalar(toofar, toofar, P - 0.5, None, ALU.is_gt))
            nc.vector.tensor_reduce(far[0:Q, 0:1], toofar, AX, ALU.add).then_inc(s_far, 1)
            me.link(nc.vector.tensor_tensor(as_blocks(place_n[0:Q, :]), as_blocks(dst_n[0:Q, :]),
                                            start.unsqueeze(2).broadcast_to([Q, G // K, K * P]), ALU.subtract))
            dve.wait_ge(s_farall, 1)
            me.link(nc.vector.tensor_scalar(far[:, 1:2], bank[7][:, 0:1], 0.5, None, ALU.is_gt))
            nc.vector.tensor_copy(flag_i[:, :], far[:, 1:2]).then_inc(s_flag, 1)
            dve.wait_ge(s_const, s_cons)
            me.link(nc.vector.tensor_tensor(as_tiles(tmp_n[0:Q, :]), iota[0:Q, None, :].broadcast_to([Q, G, P]),
                                            as_tiles(place_n[0:Q, :]), ALU.subtract))
            nc.vector.scalar_tensor_tensor(out=place_n[0:Q, :], in0=tmp_n[0:Q, :], scalar=far[0:Q, 1:2],
                                           in1=place_n[0:Q, :], op0=ALU.mult, op1=ALU.add).then_inc(s_nat, 1)
            dve.wait_ge(s_turned, 2)
            me.link(nc.vector.tensor_copy(tmpT_i, dstT))
            me.link(nc.vector.tensor_scalar(tmpT2_i, tmpT_i, 7, None, ALU.arith_shift_right))
            me.link(nc.vector.tensor_copy(by_g(dst_hi), tmpT2_i))
            me.link(nc.vector.tensor_scalar(tmpT2_i, tmpT_i, 127, None, ALU.bitwise_and))
            me.link(nc.vector.tensor_copy(by_g(dst_lo), tmpT2_i))
            dve.wait_ge(s_w3, 2)
            dve.wait_ge(s_rest, 1)
            nc.vector.tensor_tensor(by_g(w3[:, 2, :, :]), rest, by_g(w3[:, 1, :, :]), ALU.subtract).then_inc(s_w3, 1)

            def statistics(of, n):
                dve.sem_inc(s_tick, 1)
                me.link(nc.vector.bn_stats(stats[:, n, :], of))
                dve.sem_inc(s_tick, 1)
                me.link(nc.vector.bn_aggr(mv[:, n, :], stats[:, n, :]))
                nc.vector.tensor_scalar(var[:, n, :], mv[:, n, 1:2], EPS, None, ALU.add).then_inc(s_var, 1)

            def normalize(to, of, n):
                return nc.vector.tensor_scalar(to, of, mv[:, n, 0:1], rstd[:, n, :], ALU.subtract, ALU.mult)

            def minus_mean(n, m=1):
                nc.vector.scalar_tensor_tensor(out=shiftm[:, n:n + m, :], in0=mv[:, n:n + m, 0:1], scalar=-1.0,
                                               in1=rstd[:, n:n + m, :], op0=ALU.mult, op1=ALU.mult).then_inc(s_nb, 1)

            def degrees(t, m):
                m = m % 2
                tt = slice(t, t + 1) if isinstance(t, int) else bass.ds(t, 1)
                wait_from(dve, s_deg, t - 1)
                wait_from(dve, s_ohp, t - 1)
                nc.vector.tensor_tensor(oh_hi[m], iota16[:, 0:NT, :], dst_hi[:, tt, :].broadcast_to([P, NT, G2]),
                                        ALU.is_equal).then_inc(s_hi, 1)
                nc.vector.tensor_tensor(oh_lo[m], iota16, dst_lo[:, tt, :].broadcast_to([P, P, G2]), ALU.is_equal)
                dve.wait_ge(s_hi, t + 1)
                for n in range(2):
                    last = nc.vector.tensor_tensor(oh_w[m][:, n, :, :], oh_hi[m], w3[:, n, tt, :].broadcast_to([P, NT, G2]),
                                                   ALU.mult)
                last.then_inc(s_oh, 1)

            dve.wait_ge(s_zero, 2)
            dve.wait_ge(s_turn, 8)
            dve.wait_ge(s_split, 2)
            tiles_of_x(dve, degrees)

            dve.wait_ge(s_degall, 1)
            me.link(nc.vector.tensor_scalar(dis[:, :], bank[0][:, 0:NT], 1.0, None, ALU.add))
            me.link(nc.vector.tensor_tensor(dis[:, :], dis[:, :], bank[0][:, NT:2 * NT], ALU.add))
            nc.vector.tensor_tensor(dis[:, :], dis[:, :], bank[0][:, 2 * NT:3 * NT], ALU.add).then_inc(s_dis, 1)
            dve.wait_ge(s_supout, NT)
            for c in range(XCH):
                dve.wait_ge(s_dis, c + 2)
                v = h[:, c * CT:(c + 1) * CT, :]
                nc.vector.tensor_tensor(v, v, dis[:, c * CT:(c + 1) * CT].unsqueeze(2).broadcast_to([P, CT, D]),
                                        ALU.mult).then_inc(s_scaled, 1)

            def messages(i, n):
                b, q, half, m = S4 * i + n, 2 * i + n // 2, n % 2, n % 2
                qq = slice(q, q + 1) if isinstance(q, int) else bass.ds(q, 1)
                ks = slice(half * K, (half + 1) * K)
                wait_from(dve, s_mix, b - 1)
                dve.wait_ge(s_row, b + 1)
                nc.vector.tensor_tensor(same[:, m, :, :], bank[m][:, :].rearrange("p (k n) -> p k n", n=P),
                                        srcT[:, ks, qq].broadcast_to([P, K, P]), ALU.is_equal).then_inc(s_same, 1)
                for j in range(K):
                    last = nc.vector.tensor_scalar(placed[:, m, j, :], iota[:, :], placeT[:, half * K + j, qq],
                                                   wT[:, half * K + j, qq], ALU.is_equal, ALU.mult)
                last.then_inc(s_placed, 1)
                dve.wait_ge(s_same, b + 1)
                for j in range(K):
                    last = nc.vector.tensor_tensor_reduce(out=junk[:, m * K + j, :], in0=same[:, m, j, :], in1=before[:, :],
                                                          scale=1.0, scalar=0.0, op0=ALU.mult, op1=ALU.add,
                                                          accum_out=same_before[:, m, j:j + 1])
                last.then_inc(s_dup, 1)
                dve.wait_ge(s_dup, b + 1)
                nc.vector.scalar_tensor_tensor(out=shift[:, m, :].unsqueeze(2), in0=same_before[:, m, :].unsqueeze(2),
                                               scalar=0.5, in1=shiftT[:, ks, qq], op0=ALU.is_gt, op1=ALU.mult).then_inc(s_sh, 1)
                dve.wait_ge(s_sh, b + 1)
                for k in range(K):
                    wait_from(dve, s_scat[k], 16 * (b - S4 + 1))
                nc.vector.tensor_tensor(rows_to[:, n, :].unsqueeze(2), shift[:, m, :].unsqueeze(2),
                                        srcT[:, ks, qq], ALU.add).then_inc(s_to, 1)

            dve.wait_ge(s_turned, 8)
            me.link(nc.vector.tensor_scalar(shiftT, srcT, -1.0, dummyc[:, 0:1], ALU.mult, ALU.add))
            dve.wait_ge(s_cleared, 16 * ZCH * K)
            def own_rows(t):
                t1 = bass.ds(t, 1) if not isinstance(t, int) else slice(t, t + 1)
                xt = x[:, t1, :].rearrange("p o d -> p (o d)")
                nc.vector.scalar_tensor_tensor(out=xt, in0=h[:, t1, :].rearrange("p o d -> p (o d)"), scalar=dis[:, t1], in1=xt,
                                               op0=ALU.mult, op1=ALU.add).then_inc(s_own, 1)

            assert NB // S4 == NT
            for n in range(S4):
                messages(0, n)
            own_rows(0)
            with dve.Fori(1, NB // S4) as i:
                for n in range(S4):
                    messages(i, n)
                own_rows(i)

            dve.wait_ge(s_own, NT)
            done = me.base + me.n
            NP = NFULL // 2

            def squares(p, s, n=2):
                dve.wait_ge(s_used, p + 1)
                dve.sem_inc(s_tick, 1)
                for m in range(n):
                    t = 2 * p + m
                    xt = x[:, bass.ds(t, 1) if not isinstance(t, int) else slice(t, t + 1), :].rearrange("p o d -> p (o d)")
                    last = nc.vector.bn_stats(stats[:, 2 * s + m, :], xt)
                me.add(last)

            def moments(s, n=2):
                dve.sem_inc(s_tick, 1)
                for m in range(n):
                    last = nc.vector.bn_aggr(mv[:, 2 * s + m, :], stats[:, 2 * s + m, :])
                me.add(last)

            def variances(s, n=2):
                nc.vector.tensor_scalar(var[:, 2 * s:2 * s + n, :], mv[:, 2 * s:2 * s + n, 1:2], EPS, None, ALU.add).then_inc(s_var, 1)

            def new_stats(p, s, n=2):
                tt = bass.ds(2 * p, n) if not isinstance(p, int) else slice(2 * p, 2 * p + n)
                dve.wait_ge(s_root, NT + p + 1)
                wait_from(dve, s_h, p - 1)
                minus_mean(2 * s, n)
                nc.vector.tensor_copy(rowstat[:, tt, 0:1], rstd[:, 2 * s:2 * s + n, :])
                dve.wait_ge(s_nb, NT + p + 1)
                me.add(nc.vector.tensor_copy(rowstat[:, tt, 1:2], shiftm[:, 2 * s:2 * s + n, :]))

            def new_rows(p, slot, n=2, before_it=True, two_before=True):
                s = slot % 2
                a, c = (back[:, slot * K + k, 0:n * D] for k in range(2))
                dve.wait_ge(s_pair, p + 1)
                me.add(nc.vector.tensor_tensor(a, a, c, ALU.add))
                one = me.n
                if before_it:
                    squares(p - 1, 1 - s)
                a2 = a.rearrange("p (j d) -> p j d", d=D)
                me.wait(one)
                for m in range(n):
                    t = 2 * p + m
                    t1 = bass.ds(t, 1) if not isinstance(t, int) else slice(t, t + 1)
                    xt = x[:, t1, :].rearrange("p o d -> p (o d)")
                    last = nc.vector.scalar_tensor_tensor(out=xt, in0=a2[:, m, :], scalar=dis[:, t1], in1=xt, op0=ALU.mult, op1=ALU.add)
                last.then_inc(s_used, 1)
                if before_it:
                    me.wait()
                    moments(1 - s)
                    me.wait()
                    variances(1 - s)
                if two_before:
                    new_stats(p - 2, s)

            dve.wait_ge(s_to, NB)
            dve.wait_ge(s_mix, NB)
            me.at(done)
            new_rows(0, 0, before_it=False, two_before=False)
            new_rows(1, 1, two_before=False)
            done += me.n
            one = 4
            for p in range(2, SL):
                me.at(done + (p - 2) * one)
                new_rows(p, p % SL)
            assert me.n == one
            with dve.Fori(1, NP // SL) as i:
                for m in range(SL):
                    p = SL * i + m
                    me.at(done + (p - 2) * one)
                    new_rows(p, m)
                    assert me.n == one
            me.at(done + (NP - 2) * one)
            new_rows(NP, 0, n=1)
            new_stats(NP - 1, 1)
            squares(NP, 0, 1)
            me.wait()
            moments(0, 1)
            me.wait()
            variances(0, 1)
            new_stats(NP, 0, 1)

            R = lambda n: rt[0:1, n, :]
            S = lambda n: rs[0:1, n:n + 1]
            def split_rows(i, n):
                cols = slice(i * K * P, i * K * P + n) if isinstance(i, int) else bass.ds(i * (K * P), n)
                wait_from(dve, s_ff1, TOP * FC * i)
                nc.vector.tensor_copy(hTh[:, :, 0:n], hT[:, :, cols]).then_inc(s_part, 1)
                dve.wait_ge(s_part, 2 * i + 1)
                nc.vector.tensor_tensor(hTl[:, :, 0:n], hT[:, :, cols], hTh[:, :, 0:n].bitcast(fp32), ALU.subtract).then_inc(s_part, 1)

            dve.wait_ge(s_hT, K)
            split_rows(0, K * P)
            dve.wait_ge(s_hT, NT)
            me.link(nc.vector.tensor_reduce(mean_col[:, :], colsum[:, :, 0:NT], AX, ALU.add))
            nc.vector.tensor_scalar(mean_col[:, :], mean_col[:, :], 1.0 / N, None, ALU.mult).then_inc(s_mcol, 1)
            dve.wait_ge(s_logit, 1)
            dve.wait_ge(s_wr, 32)
            me.link(nc.vector.tensor_tensor(R(1), bank[5][0:1, 0:NX], R(0), ALU.add))

            def softmax(of, n, w, to):
                me.link(nc.vector.tensor_reduce(S(0), of, AX, ALU.max))
                nc.vector.tensor_scalar(rt[0:1, 16 + n, 0:w], of, S(0), None, ALU.subtract).then_inc(s_lg, 1)
                dve.wait_ge(s_e, n + 1)
                me.link(nc.vector.tensor_reduce(S(1), rt[0:1, 20 + n, 0:w], AX, ALU.add))
                me.link(nc.vector.reciprocal(S(2), S(1)))
                me.link(nc.vector.tensor_scalar(to, rt[0:1, 20 + n, 0:w], S(2), None, ALU.mult))

            softmax(R(1), 0, NX, R(2))
            me.link(nc.vector.tensor_scalar(R(3), R(2), float(N), None, ALU.mult))
            me.link(nc.vector.reciprocal(R(4), R(3)))
            me.link(nc.vector.tensor_scalar(R(4), R(4), CAP, None, ALU.mult))
            me.link(nc.vector.tensor_scalar(R(5), R(3), CAP, None, ALU.is_gt))
            me.link(nc.vector.tensor_scalar(R(6), R(3), CAP, None, ALU.is_le))
            me.link(nc.vector.tensor_tensor(R(4), R(4), R(5), ALU.mult))
            me.link(nc.vector.tensor_tensor(R(4), R(4), R(6), ALU.add))
            me.link(nc.vector.tensor_tensor(R(7), R(2), R(4), ALU.mult))
            softmax(R(7), 1, NX, R(8))
            for e in range(TOP):
                me.link(nc.vector.tensor_reduce(rs[0:1, 4 + e:5 + e], R(8), AX, ALU.max))
                me.link(nc.vector.tensor_scalar(R(9), R(8), S(4 + e), float(NX), ALU.is_lt, ALU.mult))
                me.link(nc.vector.tensor_tensor(R(9), R(9), iota[0:1, 0:NX], ALU.add))
                me.link(nc.vector.tensor_reduce(rs[0:1, 6 + e:7 + e], R(9), AX, ALU.min))
                me.link(nc.vector.tensor_scalar(R(10), iota[0:1, 0:NX], S(6 + e), -2.0, ALU.is_equal, ALU.mult))
                me.link(nc.vector.tensor_tensor(R(8), R(8), R(10), ALU.add))
            nc.vector.tensor_copy(pick_i[0:1, :], rs[0:1, 6:6 + TOP]).then_inc(s_pick, 1)
            softmax(rs[0:1, 4:4 + TOP], 2, TOP, rs[0:1, 8:8 + TOP])
            dve.wait_ge(s_dve, me.base + me.n)
            nc.vector.tensor_copy(rs[0:1, 10:10 + TOP], rs[0:1, 8:8 + TOP]).then_inc(s_wt, 1)

            for e in range(TOP):
                dve.wait_ge(s_W1h, (e + 1) * DC)
                nc.vector.tensor_tensor(W1l[:, e, :, :], W1raw[:, e * DC:(e + 1) * DC, :], W1h[:, e, :, :].bitcast(fp32),
                                        ALU.subtract).then_inc(s_W1l, 1)
            dve.wait_ge(s_wb, 1)
            nc.vector.tensor_copy(wtop[:, :], bank[4][:, 0:TOP]).then_inc(s_wtop, 1)

            dve.wait_ge(s_wtop, 1)
            dve.wait_ge(s_b12, 64)
            me.link(nc.vector.tensor_scalar(b2c[:, :], b2s[:, 0, :], wtop[:, 0:1], None, ALU.mult))
            nc.vector.scalar_tensor_tensor(out=b2c[:, :], in0=b2s[:, 1, :], scalar=wtop[:, 1:2], in1=b2c[:, :],
                                           op0=ALU.mult, op1=ALU.add).then_inc(s_b2c, 1)
            for e in range(TOP):
                dve.wait_ge(s_W2h, e + 1)
                v = slice(e * FC, (e + 1) * FC)
                nc.vector.scalar_tensor_tensor(out=W2l[:, v, :], in0=W2raw[:, v, :], scalar=wtop[:, e:e + 1],
                                               in1=W2h[:, v, :].bitcast(fp32), op0=ALU.mult, op1=ALU.subtract).then_inc(s_W2l, 1)
            dve.wait_ge(s_W2l, TOP)

            def residual(t, j):
                t1 = bass.ds(t, 1) if not isinstance(t, int) else slice(t, t + 1)
                wait_from(dve, s_zg, t - K + 1)
                nc.vector.tensor_scalar(z[:, j:j + 1, :], x[:, t1, :], rowstat[:, t1, 0:1].rearrange("p o d -> p (o d)"),
                                        rowstat[:, t1, 1:2].rearrange("p o d -> p (o d)"), ALU.mult, ALU.add).then_inc(s_res, 1)

            def low_part(i, k, n):
                dve.wait_ge(s_hidh, TOP * FC * i + k + 1)
                if k == 0:
                    wait_from(dve, s_ff2, K * i)
                nc.vector.tensor_tensor(hidl[:, k, 0:n], hid[:, k % 4, 0:n], hidh[:, k, 0:n].bitcast(fp32),
                                        ALU.subtract).then_inc(s_hidl, 1)

            def last_sum(t, j):
                dve.wait_ge(s_ff2, t + 1)
                if not isinstance(t, int) or t < NFULL:
                    dve.wait_ge(s_hb, t + 1)
                nc.vector.tensor_tensor(z[:, j, :], bank[4 + j][:, 0:D], z[:, j, :], ALU.add).then_inc(s_z, 1)

            def last_squares(t, j):
                dve.wait_ge(s_z, t + 1)
                dve.sem_inc(s_tick, 1)
                me.add(nc.vector.bn_stats(stats[:, 4 + j, :], z[:, j, :]))

            def last_variances(tiles):
                me.wait()
                dve.sem_inc(s_tick, 1)
                for j in range(tiles):
                    me.add(nc.vector.bn_aggr(mv[:, 4 + j, :], stats[:, 4 + j, :]))
                me.wait()
                nc.vector.tensor_scalar(var[:, 4:4 + tiles, :], mv[:, 4:4 + tiles, 1:2], EPS, None, ALU.add).then_inc(s_var, 1)

            def last_normal(i, j):
                dve.wait_ge(s_root, NT + NP + 1 + i + 1)
                normalize(z[:, j, :], z[:, j, :], 4 + j).then_inc(s_zn, 1)

            done = me.base + me.n
            GR = NFULL // K

            def group(i, n, tiles, after):
                me.at(done + (i - 1) * (2 * K))
                t = K * (i - 1)
                for j in range(2):
                    last_sum(t + j, j)
                for j in range(2):
                    last_squares(t + j, j)
                last_sum(t + 2, 2)
                low_part(i, 0, n)
                last_sum(t + 3, 3)
                for j in range(2, K):
                    last_squares(t + j, j)
                low_part(i, 1, n)
                last_variances(K)
                assert me.n == 2 * K
                low_part(i, 2, n)
                for j in range(K):
                    last_normal(i - 1, j)
                    low_part(i, 3 + j, n)
                low_part(i, TOP * FC - 1, n)
                if after:
                    split_rows(i + 1, after)
                for j in range(tiles):
                    residual(K * i + j, j)

            for k in range(TOP * FC):
                low_part(0, k, K * P)
            split_rows(1, K * P)
            for j in range(K):
                residual(j, j)
            with dve.Fori(1, GR - 1) as i:
                group(i, K * P, K, K * P)
            group(GR - 1, K * P, K, P)
            group(GR, P, 1, 0)
            me.at(done + GR * 2 * K)
            z0 = z[:, 0, :]
            dve.wait_ge(s_res, NT)
            nc.vector.tensor_tensor(z0, z0, b2c[:, :], ALU.add).then_inc(s_last, 1)
            dve.wait_ge(s_last, 1)
            last_sum(NFULL, 0)
            last_squares(NFULL, 0)
            last_variances(1)
            last_normal(GR, 0)
            dve.wait_ge(s_zn, NT)
            dve.wait_ge(s_gb, 32)
            nc.vector.tensor_tensor(z0, z0, gamma[:, :], ALU.mult).then_inc(s_last, 1)
            dve.wait_ge(s_last, 2)
            nc.vector.tensor_tensor(z0, z0, x[:, NFULL, :], ALU.add).then_inc(s_last, 1)
            dve.wait_ge(s_last, 3)
            nc.vector.tensor_tensor(z0, z0, beta[:, :], ALU.add).then_inc(s_last, 1)

        @block.tensor
        def _(pe):
            mm = nc.tensor.matmul
            pe.wait_ge(s_const, s_cons)
            for n, of in enumerate((dst_n, w_n, src_n, place_n)):
                if n == 0:
                    pe.wait_ge(s_nat, 1)
                if n == 1:
                    pe.wait_ge(s_ew, 32)
                if n == 2:
                    pe.wait_ge(s_nat, 2)
                if n == 3:
                    pe.wait_ge(s_far, 1)
                    mm(bank[7][:, 0:1], ones[0:Q, :], far[0:Q, 0:1], start=True, stop=True).then_inc(s_farall, 1)
                    pe.wait_ge(s_nat, 3)
                for half in range(2):
                    to = bank[2 * (n % 2) + half]
                    if n >= 2:
                        pe.wait_ge(s_turned, 2 * (n - 2) + half + 1)
                    for j in range(K):
                        last = nc.tensor.transpose(to[:, j * Q:(j + 1) * Q], of[0:Q, (half * K + j) * P:(half * K + j + 1) * P],
                                                   ident[0:Q, 0:Q])
                    last.then_inc(s_turn, 1)

            pe.wait_ge(s_turned, 8)
            pe.wait_ge(s_zero, 1)
            pe.wait_ge(s_W, 32)
            mm(bank[0][:, 0:3 * NT], zeros[:, 0:P], zeros[:, 0:3 * NT], start=True, stop=False, skip_group_check=True)

            def one_hots(t, m):
                pe.wait_ge(s_oh, t + 1)
                pe.wait_ge(s_ohp, t + 1)
                for g in range(G2):
                    last = mm(bank[0][:, 0:3 * NT], oh_lo[m][:, :, g], oh_w[m][:, :, :, g], start=False,
                              stop=False, skip_group_check=True)
                last.then_inc(s_deg, 1)

            def pe_rows(t, m):
                pe.wait_ge(s_ln, t + 1)
                for c in range(DC):
                    last = nc.tensor.transpose(bank[1][:, c * P:(c + 1) * P], ln[:, c * P:(c + 1) * P], ident[:, :])
                last.then_inc(s_lnt, 1)
                if not isinstance(t, int) or t >= 1:
                    one_hots(t - 1, (m - 1) % 2)
                pe.wait_ge(s_lnT, t + 1)
                wait_from(pe, s_supout, t)
                mm(bank[2][:, 0:D], ones[0:1, :], b_row[0:1, :], start=True, stop=False)
                for c in range(DC):
                    last = mm(bank[2][:, 0:D], lnT[:, c, :], W[:, c, :], start=False, stop=(c == DC - 1))
                last.then_inc(s_sup, 1)

            tiles_of_x(pe, pe_rows)
            one_hots(NT - 1, (NT - 1) % 2)
            mm(bank[0][:, 0:3 * NT], zeros[:, 0:P], zeros[:, 0:3 * NT], start=False, stop=True,
               skip_group_check=True).then_inc(s_degall, 1)

            def src_rows(i, half):
                to = bank[half][:, :]
                pick = identb[0:Q, bass.ds(i, 1)] if not isinstance(i, int) else identb[0:Q, i:i + 1]
                pick = pick.broadcast_to([Q, P])
                mm(to, pick, src_hi[0:Q, half * K * P:(half + 1) * K * P], start=True, stop=False)
                mm(to, pick, src_lo[0:Q, half * K * P:(half + 1) * K * P], start=False, stop=True).then_inc(s_row, 1)

            def mix(b, half):
                pe.wait_ge(s_same, b + 1)
                pe.wait_ge(s_placed, b + 1)
                wait_from(pe, s_mixT, b - 1)
                for j in range(K):
                    last = mm(bank[2 + half][:, j * P:(j + 1) * P], placed[:, half, j, :], same[:, half, j, :],
                              start=True, stop=True)
                last.then_inc(s_mix, 1)

            def msgs(b, n, turn, gathered):
                pe.wait_ge(s_mixT, b + 1)
                pe.wait_ge(s_window[n], 16 * (K if gathered else 1) * turn)
                wait_from(pe, s_sums, b - 1)
                for j in range(K):
                    c = j % 2
                    last = mm(bank[4 + 2 * (n % 2) + j // 2][:, c * D:(c + 1) * D], mixT[:, n % 2, j, :],
                              window[:, n * K + (j if gathered else 0), :], start=True, stop=True)
                last.then_inc(s_msg, 1)

            pe.wait_ge(s_split, 2)
            pe.wait_ge(s_scaled, 1)
            pe.wait_ge(s_supout, NT)
            def pe_blocks(i, gathered):
                for n in range(S4):
                    b, q = S4 * i + n, 2 * i + n // 2
                    wait_from(pe, s_same, b - 1)
                    src_rows(q, n % 2)
                    if not isinstance(i, int) or b >= 1:
                        mix(b - 1, (n - 1) % 2)
                    if not isinstance(i, int) or b >= 2:
                        msgs(b - 2, (n - 2) % S4, i + n // 2, gathered)

            def pe_messages(gathered):
                pe_blocks(0, gathered)
                with pe.Fori(1, NB // S4) as i:
                    pe_blocks(i, gathered)
                mix(NB - 1, 1)
                msgs(NB - 2, S4 - 2, NB // S4, gathered)
                msgs(NB - 1, S4 - 1, NB // S4, gathered)

            pe.wait_ge(s_flag, 1)
            gathers = pe.value_load(flag_i[0:1, 0:1], min_val=0, max_val=1)
            with pe.If(gathers < 1):
                pe_messages(False)
            with pe.Else():
                pe_messages(True)

            pe.wait_ge(s_sums, NB)
            NP = NFULL // 2

            def turn_rows(p, s, n=2):
                pe.wait_ge(s_h, p + 1)
                for m in range(n):
                    t = 2 * p + m
                    wait_from(pe, s_hT, t - 3)
                    for c in range(DC):
                        last = nc.tensor.transpose(bank[2 * s + m][:, c * P:(c + 1) * P], hs[:, 2 * s + m, c * P:(c + 1) * P], ident[:, :])
                    last.then_inc(s_ht, 1)

            for p in range(2):
                turn_rows(p, p)
            with pe.Fori(1, NP // 2) as i:
                for s in range(2):
                    turn_rows(2 * i + s, s)
            turn_rows(NP, 0, 1)

            pe.wait_ge(s_mcol, 1)
            pe.wait_ge(s_wr, 32)
            for c in range(DC):
                last = mm(bank[5][0:1, 0:NX], mean_col[:, c:c + 1], Wr[:, c, :], start=(c == 0), stop=(c == DC - 1))
            last.then_inc(s_logit, 1)
            pe.wait_ge(s_wt, 1)
            mm(bank[4][:, 0:TOP], ones[0:1, :], rs[0:1, 10:10 + TOP], start=True, stop=True).then_inc(s_wb, 1)

            def ffn(i, n, tiles):
                pe.wait_ge(s_part, 2 * i + 2)
                first = isinstance(i, int) and i == 0
                for k in range(TOP * FC):
                    e, f = k // FC, k % FC
                    if first and f == 0:
                        pe.wait_ge(s_W1l, e + 1)
                    wait_from(pe, s_gelu, TOP * FC * i + k - 3)
                    step = 0
                    for c in range(DC):
                        for w, v in ((W1h, hTh), (W1h, hTl), (W1l, hTh)):
                            last = mm(bank[k % 4][:, 0:n], w[:, e, c, f * P:(f + 1) * P], v[:, c, 0:n],
                                      start=(step == 0), stop=(step == 3 * DC - 1))
                            step += 1
                    last.then_inc(s_ff1, 1)
                for k in range(TOP * FC):
                    if first and k % FC == 0:
                        pe.wait_ge(s_W2l, k // FC + 1)
                    pe.wait_ge(s_hidl, TOP * FC * i + k + 1)
                    for j in range(tiles):
                        if k == 0:
                            wait_from(pe, s_z, K * (i - 1) + j + 1)
                        js = slice(j * P, (j + 1) * P)
                        for step, (v, w) in enumerate(((hidh, W2h), (hidh, W2l), (hidl, W2h))):
                            last = mm(bank[4 + j][:, 0:D], v[:, k, js], w[:, k, :], start=(k == 0 and step == 0),
                                      stop=(k == TOP * FC - 1 and step == 2))
                        if k == TOP * FC - 1:
                            last.then_inc(s_ff2, 1)

            ffn(0, K * P, K)
            with pe.Fori(1, NFULL // K) as i:
                ffn(i, K * P, K)
            ffn(NFULL // K, P, 1)


_INS = ['x', 'src', 'dst', 'edge_weight', 'L0_gnn_W', 'L0_gnn_b', 'L0_ffn_Wr', 'L0_ffn_br', 'L0_ffn_W1', 'L0_ffn_b1',
        'L0_ffn_W2', 'L0_ffn_b2', 'L0_ffn_gamma', 'L0_ffn_beta']
_OUTS = [((6250, 256), 'float32')]


def kernel(**inputs):
    import numpy as _np
    import concourse.bacc as _bacc
    from concourse import mybir as _mybir
    from concourse.bass_utils import run_bass_kernel_spmd as _run

    nc = _bacc.Bacc("TRN2", target_bir_lowering=False, num_devices=1)
    arrays, args = {}, []
    for name in _INS:
        a = _np.ascontiguousarray(inputs[name])
        arrays[f"in_{name}_dram"] = a
        args.append(nc.dram_tensor(f"in_{name}_dram", a.shape, _mybir.dt.from_np(a.dtype), kind="ExternalInput").ap())
    for i, (shape, dtype) in enumerate(_OUTS):
        dt = _mybir.dt.from_np(_np.dtype(dtype))
        args.append(nc.dram_tensor(f"out_{i}_dram", shape, dt, kind="ExternalOutput").ap())
    gnn_ffn_kernel(nc, *args)
    r = _run(nc, [arrays], core_ids=[0])
    return r.results[0]["out_0_dram"]
```
